# Optimizing a Trainium2 kernel written in Bass

```python
import numpy as np
import jax
import jax.numpy as jnp

def _softmax(x, axis=-1):
    return jax.nn.softmax(x, axis=axis)

def _gelu(x):
    return jax.nn.gelu(x, approximate=True)

def _silu(x):
    return jax.nn.silu(x)

def _sigmoid(x):
    return jax.nn.sigmoid(x)

def _layernorm(x, axis=-1, eps=1e-05):
    m = jnp.mean(x, axis=axis, keepdims=True)
    v = jnp.var(x, axis=axis, keepdims=True)
    return (x - m) / jnp.sqrt(v + eps)

def _scatter_add(tgt, idx, src, axis=0):
    return tgt.at[idx].add(src)

def _segment_sum(src, seg, n):
    return jax.ops.segment_sum(src, seg, n)
kernel_name = 'mk_seq_preln_d1_jaxref_r4_d73c2d'

def setup_inputs(seed: int=0):
    np.random.seed(seed)
    _w = jnp.asarray

    def _L0_attn_setup():
        import jax, jax.numpy as jnp
        import numpy as np
        D_MODEL = 256
        NUM_HEADS = 16
        B, S = (1, 1024)
        key = jax.random.key(seed)
        kx, kq, kk, kv, ko = jax.random.split(key, 5)
        std = (1.0 / D_MODEL) ** 0.5

        def trunc(k):
            return std * jax.random.truncated_normal(k, -3.0, 3.0, (D_MODEL, D_MODEL), dtype=jnp.float32)
        return {'x': jax.random.normal(kx, (B, S, D_MODEL), dtype=jnp.float32), 'W_Q': trunc(kq), 'W_K': trunc(kk), 'W_V': trunc(kv), 'W_O': trunc(ko)}
    _L0_attn_in = _L0_attn_setup()

    def _L0_ffn_setup():
        import jax, jax.numpy as jnp
        import numpy as np
        HIDDEN = 256
        MOE_FF = 128
        SHARED_FF = 704
        NUM_EXPERTS = 16
        TOP_K = 2
        NORM_TOPK = True
        key = jax.random.key(seed)
        ks = jax.random.split(key, 8)
        s = 0.02
        return {'layer_input': jax.random.normal(ks[0], (1, 512, HIDDEN), dtype=jnp.float32), 'gate_w': jax.random.normal(ks[1], (NUM_EXPERTS, HIDDEN), dtype=jnp.float32) * s, 'w_gate_up': jax.random.normal(ks[2], (NUM_EXPERTS, HIDDEN, 2 * MOE_FF), dtype=jnp.float32) * s, 'w_down': jax.random.normal(ks[3], (NUM_EXPERTS, MOE_FF, HIDDEN), dtype=jnp.float32) * s, 'shared_w_gate': jax.random.normal(ks[4], (SHARED_FF, HIDDEN), dtype=jnp.float32) * s, 'shared_w_up': jax.random.normal(ks[5], (SHARED_FF, HIDDEN), dtype=jnp.float32) * s, 'shared_w_down': jax.random.normal(ks[6], (HIDDEN, SHARED_FF), dtype=jnp.float32) * s, 'shared_gate_w': jax.random.normal(ks[7], (1, HIDDEN), dtype=jnp.float32) * s}
    _L0_ffn_in = _L0_ffn_setup()
    _d = {'L0_attn_x': _L0_attn_in['x'], 'L0_attn_W_Q': _L0_attn_in['W_Q'], 'L0_attn_W_K': _L0_attn_in['W_K'], 'L0_attn_W_V': _L0_attn_in['W_V'], 'L0_attn_W_O': _L0_attn_in['W_O'], 'L0_ffn_gate_w': _L0_ffn_in['gate_w'], 'L0_ffn_w_gate_up': _L0_ffn_in['w_gate_up'], 'L0_ffn_w_down': _L0_ffn_in['w_down'], 'L0_ffn_shared_w_gate': _L0_ffn_in['shared_w_gate'], 'L0_ffn_shared_w_up': _L0_ffn_in['shared_w_up'], 'L0_ffn_shared_w_down': _L0_ffn_in['shared_w_down'], 'L0_ffn_shared_gate_w': _L0_ffn_in['shared_gate_w']}
    _x0 = _d['L0_attn_x']
    _d['L0_attn_x'] = jax.random.normal(jax.random.fold_in(jax.random.key(seed), 1), (8, 512, 256), dtype=_x0.dtype)
    del _x0
    return _d

def reference(L0_attn_x, L0_attn_W_Q, L0_attn_W_K, L0_attn_W_V, L0_attn_W_O, L0_ffn_gate_w, L0_ffn_w_gate_up, L0_ffn_w_down, L0_ffn_shared_w_gate, L0_ffn_shared_w_up, L0_ffn_shared_w_down, L0_ffn_shared_gate_w):

    def _L0_attn_ref(x, W_Q, W_K, W_V, W_O):
        import jax, jax.numpy as jnp
        import numpy as np
        D_MODEL = 256
        NUM_HEADS = 16
        B, S = (1, 1024)
        Bx, Sx, Dm = x.shape
        H = NUM_HEADS
        d_attn = Dm // H
        Q = x @ W_Q.T
        K = x @ W_K.T
        V = x @ W_V.T
        Q = Q.reshape(Bx, Sx, H, d_attn).transpose(0, 2, 1, 3)
        K = K.reshape(Bx, Sx, H, d_attn).transpose(0, 2, 1, 3)
        V = V.reshape(Bx, Sx, H, d_attn).transpose(0, 2, 1, 3)
        scale = 1.0 / jnp.sqrt(jnp.asarray(d_attn, dtype=x.dtype))
        attn = jnp.einsum('bhqd,bhkd->bhqk', Q, K) * scale
        causal = jnp.tril(jnp.ones((Sx, Sx), dtype=bool))
        attn = jnp.where(causal, attn, jnp.asarray(-jnp.inf, dtype=attn.dtype))
        probs = jax.nn.softmax(attn, axis=-1)
        y = jnp.einsum('bhqk,bhkd->bhqd', probs, V)
        y = y.transpose(0, 2, 1, 3).reshape(Bx, Sx, Dm)
        return y @ W_O.T

    def _L0_ffn_ref(layer_input, gate_w, w_gate_up, w_down, shared_w_gate, shared_w_up, shared_w_down, shared_gate_w):
        import jax, jax.numpy as jnp
        import numpy as np
        HIDDEN = 256
        MOE_FF = 128
        SHARED_FF = 704
        NUM_EXPERTS = 16
        TOP_K = 2
        NORM_TOPK = True
        B, S, D = layer_input.shape
        x = layer_input.reshape(-1, D)
        N = x.shape[0]
        shared = jax.nn.silu(x @ shared_w_gate.T) * (x @ shared_w_up.T) @ shared_w_down.T
        shared = shared * jax.nn.sigmoid(x @ shared_gate_w.T)
        logits = x @ gate_w.T
        probs = jax.nn.softmax(logits.astype(jnp.float32), axis=-1)
        rw, sel = jax.lax.top_k(probs, TOP_K)
        if NORM_TOPK:
            rw = rw / rw.sum(axis=-1, keepdims=True)
        rw = rw.astype(x.dtype)
        combine = jnp.zeros((N, NUM_EXPERTS), x.dtype).at[jnp.arange(N)[:, None], sel].set(rw)
        gu = jnp.einsum('nd,edf->nef', x, w_gate_up)
        g, h = jnp.split(gu, 2, axis=-1)
        h = jax.nn.silu(g) * h
        expert_out = jnp.einsum('nef,efd,ne->nd', h, w_down, combine)
        out = expert_out + shared
        return out.reshape(B, S, D)
    x = L0_attn_x
    x = x + _L0_attn_ref(_layernorm(x, axis=-1), L0_attn_W_Q, L0_attn_W_K, L0_attn_W_V, L0_attn_W_O)
    x = x + _L0_ffn_ref(_layernorm(x, axis=-1), L0_ffn_gate_w, L0_ffn_w_gate_up, L0_ffn_w_down, L0_ffn_shared_w_gate, L0_ffn_shared_w_up, L0_ffn_shared_w_down, L0_ffn_shared_gate_w)
    return x

_drawn_inputs = setup_inputs


def setup_inputs(seed=0):
    import zlib

    import numpy as np

    out = dict(_drawn_inputs(seed))
    spreads = {}
    factors = {'L0_ffn_gate_w': 7.261,
     'L0_ffn_w_gate_up': 6.734,
     'L0_ffn_w_down': 6.73,
     'L0_ffn_shared_w_gate': 4.117,
     'L0_ffn_shared_w_up': 4.06,
     'L0_ffn_shared_w_down': 4.078,
     'L0_ffn_shared_gate_w': 8.0}
    for name, (base, spread) in spreads.items():
        noise = np.random.default_rng([zlib.crc32(name.encode()), seed]).standard_normal(out[name].shape)
        drawn = base * np.exp(spread * noise) if base else spread * noise
        out[name] = jnp.asarray(drawn.astype(out[name].dtype))
    for name, factor in factors.items():
        out[name] = (out[name] * factor).astype(out[name].dtype)
    return out
```

```python
import concourse.bass as bass
from concourse import mybir
from contextlib import ExitStack

P = 128
B, S, D = 8, 512, 256
H, DH = 16, 16
DK = D // P
TB = S // P
NT = B * TB
HU = 8
GH = 4
UNITS = H // HU
GROUPS = HU // GH
STRIP = P // GH
E = 16
LOGITS = E + 1
EPS = 1e-5
NEG = -1.0e30
SCALE = float(DH) ** -0.5

ROW_HH, ROW_HL, ROW_LH = 0, DH, 2 * DH
ROWS_QK = 96
ROW_M = 96
ROWS_ALL = ROW_M + 1

BANK = 512
PAIRS = 5
PAIR = 2 * BANK


def block_of(head, kt):
    width = (TB - kt) * P
    if kt == 0:
        return head // 2, (head % 2) * BANK, width
    if kt == 1:
        return 2 + head // 2, (head % 2) * BANK, width
    if kt == 3:
        return 2 + head // 2, (head % 2) * BANK + 3 * P, width
    return 4, head * 2 * P, width


def max_jobs_of_group():
    return [(3, (h,)) for h in range(GH)] + [(2, (h,)) for h in range(GH)] + [(1, (0, 1)), (1, (2, 3)), (0, (0, 1, 2, 3))]


MAX_JOBS = max_jobs_of_group()
MAX_SPLIT = [0, 2, 4, 6, 8, 11]

WORK_BANKS = 3


def work_jobs(it):
    jobs = []
    if it < B:
        jobs += [("xT", 0, "dve"), ("xT", 1, "dve"), ("Q", 0, "dve"), ("K", 0, "dve")]
        jobs += [("max", (0, g, n), "dve") for g in range(GROUPS) for n in range(len(MAX_JOBS))]
        jobs += [("mT", 0, "act"), ("Q", 1, "dve"), ("K", 1, "dve"), ("V", 0, "act"), ("V", 1, "act")]
    if it > 0:
        jobs += [("O", 0, "dve"), ("O", 1, "dve")]
    if it < B:
        jobs += [("max", (1, g, n), "dve") for g in range(GROUPS) for n in range(len(MAX_JOBS))]
        jobs += [("mT", 1, "act")]
    if it > 0:
        jobs += [("x2T", 0, "act"), ("x2T", 1, "act"), ("L", 0, "dve"), ("L", 1, "dve")]
    return jobs


class Work:

    def __init__(self, it, kind):
        first, full = work_jobs(0), work_jobs(1)
        self.jobs = {"first": first, "full": full, "last": work_jobs(B)}[kind]
        self.at = {(k, w): n for n, (k, w, _) in enumerate(self.jobs)}
        self.kind = kind
        self.base = {}
        for e in (None, "act", "dve"):
            in_first, in_full = (sum(e in (None, j[2]) for j in x) for x in (first, full))
            self.base[e] = 0 if kind == "first" else (it - 1) * in_full + in_first
        assert len(first) % WORK_BANKS == 0 and len(full) % WORK_BANKS == 0

    def ready(self, kind, which):
        return self.base[None] + (self.at[kind, which] + 1)

    def bank(self, kind, which):
        return self.at[kind, which] % WORK_BANKS

    def freed(self, kind, which):
        n = self.at[kind, which]
        e = self.jobs[n][2]
        return e, self.base[e] + sum(j[2] == e for j in self.jobs[:n + 1])

    def needed(self, kind, which):
        n = self.at[kind, which] - WORK_BANKS
        if n >= 0:
            return [self.freed(*self.jobs[n][:2])]
        return [] if self.kind == "first" else [(e, self.base[e]) for e in ("act", "dve")]


def is_number(value, *which):
    return isinstance(value, int) and value in which


class Chain:

    def __init__(self, engine, sem, base=0):
        self.engine, self.sem, self.base, self.n = engine, sem, base, 0

    def step(self, instruction):
        instruction.then_inc(self.sem, 1)
        self.n += 1

    def wait(self):
        self.engine.wait_ge(self.sem, self.base + self.n)


class Ticks(Chain):

    def __init__(self, engine, sem, tiny):
        super().__init__(engine, sem)
        self.tiny = tiny

    def start(self, base):
        self.base, self.n = base, 0

    def tick(self):
        self.wait()
        self.step(self.tiny())


def exact_product(pe, out, stationary, moving, start, stop):
    (s_hi, s_lo), (m_hi, m_lo) = stationary, moving
    pe.matmul(out, s_hi, m_hi, start=start, stop=False)
    pe.matmul(out, s_hi, m_lo, start=False, stop=False)
    return pe.matmul(out, s_lo, m_hi, start=False, stop=stop)


def build_attention(nc, ctx, x, wq, wk, wv, wo, gates, logits_all, qk_dram, x1_dram, xn2_dram, xg_dram):
    f32, f32r, bf16 = mybir.dt.float32, mybir.dt.float32r, mybir.dt.bfloat16
    ALU, ACT, AX = mybir.AluOpType, mybir.ActivationFunctionType, mybir.AxisListType

    def sb(name, shape, dt):
        return ctx.enter_context(nc.sbuf_tensor(name, shape, dt))

    def ps(name, shape):
        return ctx.enter_context(nc.psum_tensor(name, shape, f32))

    def sem(name):
        return ctx.enter_context(nc.semaphore(name))

    wstage = sb("wstage", [P, 3, DK, D], f32)
    w_hi = sb("w_hi", [P, 3, DK, D], f32r)
    w_lo = sb("w_lo", [P, 3, DK, D], f32r)
    wo_sb = sb("wo_sb", [P, UNITS * GROUPS, D], f32)
    gates_sb = sb("gates_sb", [P, DK, LOGITS], f32)
    ident = sb("ident", [P, P], f32)
    ident16 = sb("ident16", [P, P], bf16)
    mask16 = sb("mask16", [P, P], bf16)
    minus_half = sb("minus_half", [P, TB], f32)
    zeros = sb("zeros", [P, 4, D], f32)
    xb = sb("xb", [P, TB, D], f32)
    xn = sb("xn", [P, TB, D], f32)
    xT_hi = sb("xT_hi", [P, DK, S], f32r)
    xT_lo = sb("xT_lo", [P, DK, S], f32r)
    qk_sb = sb("qk_sb", [P, 2, 2, S], f32r)
    q_st = [sb(f"q_st{u}", [P, HU, S], f32r) for u in range(UNITS)]
    k_st = [sb(f"k_st{u}", [P, HU, S], f32r) for u in range(UNITS)]
    v_aug = sb("v_aug", [P, TB, H, STRIP], f32)
    probs = sb("probs", [P, GROUPS, PAIRS * PAIR], f32)
    neg_max = [sb(f"neg_max{u}", [P, TB, HU], f32) for u in range(UNITS)]
    max_row = [sb(f"max_row{u}", [HU, S], f32r) for u in range(UNITS)]
    sums = sb("sums", [P, S], f32)
    o_norm = sb("o_norm", [P, UNITS * GROUPS, S], f32)
    xres = sb("xres", [P, TB, D], f32)
    x1 = sb("x1", [P, TB, D], f32)
    xn2 = sb("xn2", [P, TB, D], f32)
    x2T = sb("x2T", [P, DK, S], f32)
    stats = [sb(f"stats{n}", [P, TB, 6], f32) for n in range(2)]
    mean_var = [sb(f"mean_var{n}", [P, TB, 2], f32) for n in range(2)]
    rstd = [sb(f"rstd{n}", [P, TB], f32) for n in range(2)]
    pool_scratch, dve_scratch = sb("pool_scratch", [1, 3], f32), sb("dve_scratch", [1, 1], f32)

    ps_s = ps("ps_s", [P, 2, PAIR])
    ps_o = ps("ps_o", [P, S])
    ps_w = ps("ps_w", [P, WORK_BANKS, BANK])

    weights_in, wo_in = sem("weights_in"), sem("wo_in")
    stack_zeroed, zeros_made, weights_split = sem("stack_zeroed"), sem("zeros_made"), sem("weights_split")
    zero_rows_out = sem("zero_rows_out")
    x_in, xres_in = sem("x_in"), sem("xres_in")
    moments_done = [sem(f"moments_done{n}") for n in range(2)]
    xn_done, xn2_done = sem("xn_done"), sem("xn2_done")
    work_ready = sem("work_ready")
    freed = {"act": sem("freed_by_act"), "dve": sem("freed_by_dve")}
    hi_done = sem("hi_done")
    stack_out = sem("stack_out")
    stack_in = [sem(f"stack_in{u}") for u in range(UNITS)]
    max_row_in = [sem(f"max_row_in{u}") for u in range(UNITS)]
    scores_ready, exp_done, mask_done = sem("scores_ready"), sem("exp_done"), sem("mask_done")
    pv_done, o_done = sem("pv_done"), sem("o_done")
    x1_out, xn2_out = sem("x1_out"), sem("xn2_out")
    dve_chain, pool_chain, dve_ticks, pool_ticks = (sem(n) for n in ("dve_chain", "pool_chain", "dve_ticks", "pool_ticks"))

    x_v = x.rearrange("b (t p) d -> b p t d", p=P)
    x1_v = x1_dram.rearrange("(b t p) d -> b p t d", b=B, p=P)
    xn2_v = xn2_dram.rearrange("(b t p) d -> b p t d", b=B, p=P)
    STACK_READS = 6

    def batch(view, b):
        if isinstance(b, int):
            return view[b]
        return view[bass.ds(b, 1)].rearrange("o p t d -> (o p) t d")

    def iterations(engine, body):
        body(0, "first")
        with engine.Fori(1, B - 1) as it:
            body(it, "full")
        body(B - 1, "full")
        body(B, "last")

    POOL_CONSTS = 8

    block = ctx.enter_context(nc.Block())

    @block.sync
    def _(sp):
        for n, w in enumerate((wq, wk, wv)):
            sp.dma_start(wstage[:, n], w).then_inc(weights_in, 16)
        sp.dma_start(xb[:, :, :], batch(x_v, 0)).then_inc(x_in, 16)
        sp.dma_start(wo_sb[:, :, :], wo).then_inc(wo_in, 16)
        sp.dma_start(gates_sb[:, :, :], gates).then_inc(wo_in, 16)

        def stack(w, it, u):
            q = it * UNITS + u
            if u == 1:
                sp.wait_ge(freed["dve"], w.freed("K", u)[1])
            if w.kind != "first":
                sp.wait_ge(stack_in[u], STACK_READS * 16 * it)
            if u == 0:
                sp.wait_ge(freed["dve"], w.freed("K", u)[1])
            for op in range(2):
                sp.dma_start(qk_dram[u, op], qk_sb[:, op].bitcast(f32)).then_inc(stack_out, 16)
            if w.kind != "first":
                sp.wait_ge(scores_ready, GROUPS * PAIRS * (q - 1))
            else:
                sp.wait_ge(stack_zeroed, 2 * UNITS)
            sp.wait_ge(stack_out, 32 * (q + 1))
            for op, (dst, parts) in enumerate(((q_st[u], (0, 0, 1)), (k_st[u], (0, 1, 0)))):
                for n, part in enumerate(parts):
                    src = qk_dram[u, op].rearrange("(j d) r t -> r d j t", d=DH)[part]
                    sp.dma_start(dst[n * DH:(n + 1) * DH].bitcast(f32), src).then_inc(stack_in[u], 16)

        def max_rows(w, it, u):
            sp.wait_ge(freed["act"], w.freed("mT", u)[1])
            sp.dma_start(q_st[u][ROW_M:ROW_M + 1].bitcast(f32).rearrange("o j t -> o (j t)"), max_row[u][:, :].bitcast(f32)).then_inc(max_row_in[u], 16)

        def body(it, kind):
            w = Work(it, kind)
            if kind != "first":
                sp.wait_ge(x1_out, 16 * it)
                sp.dma_start(xres[:, :, :], batch(x_v, it - 1)).then_inc(xres_in, 16)
            if kind != "last":
                stack(w, it, 0)
                if not is_number(it, B - 1):
                    sp.wait_ge(xn_done, it + 1)
                    sp.dma_start(xb[:, :, :], batch(x_v, it + 1)).then_inc(x_in, 16)
                if kind == "first":
                    sp.wait_ge(zeros_made, 1)
                    for n in range(MOE_TILES // 4):
                        sp.dma_start(xg_dram[n * 4:(n + 1) * 4].rearrange("t p d -> p t d"), zeros[:, :, :]).then_inc(zero_rows_out, 16)
                max_rows(w, it, 0)
                stack(w, it, 1)
            if kind != "first":
                sp.wait_ge(freed["dve"], w.freed("O", 1)[1])
                sp.dma_start(batch(x1_v, it - 1), x1[:, :, :]).then_inc(x1_out, 16)
                sp.wait_ge(xn2_done, it)
                sp.dma_start(batch(xn2_v, it - 1), xn2[:, :, :]).then_inc(xn2_out, 16)
            if kind != "last":
                max_rows(w, it, 1)

        iterations(sp, body)
        sp.wait_ge(x1_out, 16 * (B + 1))
        sp.wait_ge(xn2_out, 16 * (B + 1))
        sp.wait_ge(zero_rows_out, 16 * (MOE_TILES // 4))

    @block.gpsimd
    def _(pool):
        first = Chain(pool, pool_chain)
        first.step(pool.memset(ident[:, :], 0.0))
        first.step(pool.memset(ident16[:, :], 0.0))
        first.step(pool.memset(mask16[:, :], 0.0))
        first.step(pool.memset(minus_half[:, :], -0.5))
        first.step(pool.memset(v_aug[:, :, :, DH:STRIP], 1.0))
        pool.memset(zeros[:, :, :], 0.0).then_inc(zeros_made, 1)
        pool.memset(pool_scratch[:, 0:1], 0.0).then_inc(x1_out, 16)
        pool.memset(pool_scratch[:, 1:2], 0.0).then_inc(xn2_out, 16)
        first.wait()
        for m in (ident, ident16):
            first.step(pool.affine_select(out=m[:, :], in_=m[:, :], compare_op=ALU.not_equal, fill=1.0, base=0,
                                          pattern=[[-1, P]], channel_multiplier=1))
        first.step(pool.affine_select(out=mask16[:, :], in_=mask16[:, :], compare_op=ALU.is_ge, fill=NEG, base=0,
                                      pattern=[[-1, P]], channel_multiplier=1))
        tiny = first.n
        assert tiny == POOL_CONSTS

        ticks = Ticks(pool, pool_ticks, lambda: pool.tensor_tensor(out=pool_scratch[:, 2:3], in0=minus_half[0:1, 0:1],
                                                                   in1=minus_half[0:1, 0:1], op=ALU.add))

        def layer_norm(n, source, target, base):
            chain = Chain(pool, pool_chain, base)
            mv = mean_var[n]
            chain.step(pool.tensor_scalar(out=rstd[n][:, :], in0=mv[:, :, 1], scalar1=EPS, scalar2=None, op0=ALU.add))
            chain.wait()
            chain.step(pool.tensor_tensor(out=rstd[n][:, :], in0=rstd[n][:, :], in1=minus_half[:, :], op=ALU.pow))
            chain.wait()
            ticks.tick()
            for t in range(TB):
                last = pool.tensor_scalar(out=target[:, t, :], in0=source[:, t, :], scalar1=mv[:, t, 0:1],
                                          scalar2=rstd[n][:, t:t + 1], op0=ALU.subtract, op1=ALU.mult)
            return chain, last

        def masks(q, g):
            for p in range(PAIRS):
                pool.wait_ge(exp_done, PAIRS * (GROUPS * q + g) + p + 1)
                ticks.tick()
                v = probs[:, g, p * PAIR:(p + 1) * PAIR]
                for first_col, step, number in [[(0, BANK, 2)], [(0, BANK, 2), (3 * P, BANK, 2)], [(0, 2 * P, 4)]][(p >= 2) + (p >= 4)]:
                    diagonal = v.rearrange("p (k n) -> p k n", n=step)[:, :, first_col:first_col + P]
                    last = pool.affine_select(out=diagonal, in_=diagonal, compare_op=ALU.is_ge, fill=0.0, base=0,
                                              pattern=[[0, number], [1, P]], channel_multiplier=-1)
                last.then_inc(mask_done, 1)

        LN_STEPS = 2

        def norm_x(it, steps):
            pool.wait_ge(moments_done[0], it + 1)
            ticks.tick()
            _, last = layer_norm(0, xb, xn, steps)
            last.then_inc(xn_done, 1)

        norm_x(0, tiny)

        def body(it, kind):
            w = Work(it, kind)
            base = tiny + LN_STEPS if kind == "first" else tiny + 2 * LN_STEPS + (it - 1) * 2 * LN_STEPS
            LN_TICKS, MASK_TICKS = 2, GROUPS * PAIRS
            in_full = 2 * LN_TICKS + UNITS * MASK_TICKS
            ticks.start(LN_TICKS if kind == "first" else (it - 1) * in_full + (2 * LN_TICKS + MASK_TICKS))
            if kind == "last":
                base = base - LN_STEPS
                ticks.base -= LN_TICKS
            if kind != "first":
                for g in range(GROUPS):
                    masks(2 * it - 1, g)
                pool.wait_ge(moments_done[1], it)
                pool.wait_ge(xn2_out, 16 * it)
                pool.wait_ge(work_ready, w.base[None])
                ticks.tick()
                _, last = layer_norm(1, x1, xn2, base)
                last.then_inc(xn2_done, 1)
                base = base + LN_STEPS
            if kind != "last" and not is_number(it, B - 1):
                pool.wait_ge(work_ready, w.ready("xT", 1))
                norm_x(it + 1, base)
            if kind != "last":
                for g in range(GROUPS):
                    masks(2 * it, g)

        iterations(pool, body)

    @block.scalar
    def _(act):
        def hi(w, kind, which, out, scale=1.0):
            act.wait_ge(work_ready, w.ready(kind, which))
            act.activation(out, ps_w[:, w.bank(kind, which), :], ACT.Copy, scale=scale).then_inc(hi_done, 1)

        def exps(q, g):
            G = GROUPS * q + g
            if not is_number(G, 0, 1):
                act.wait_ge(pv_done, G - 1)
            for p in range(PAIRS):
                act.wait_ge(scores_ready, PAIRS * G + p + 1)
                act.activation(probs[:, g, p * PAIR:(p + 1) * PAIR], ps_s[:, (PAIRS * g + p) % 2, :], ACT.Exp)\
                   .then_inc(exp_done, 1)

        def max_rows(w, it, u):
            act.wait_ge(work_ready, w.ready("mT", u))
            if w.kind != "first":
                act.wait_ge(max_row_in[u], 16 * it)
            act.activation(max_row[u][:, :], ps_w[0:HU, w.bank("mT", u), :], ACT.Copy).then_inc(freed["act"], 1)

        def qk_hi(w, it, u):
            q = it * UNITS + u
            if not (w.kind == "first" and u == 0):
                act.wait_ge(stack_out, 32 * q)
            hi(w, "Q", u, qk_sb[:, 0, 0, :], SCALE)
            hi(w, "K", u, qk_sb[:, 1, 0, :])

        def body(it, kind):
            w = Work(it, kind)
            if kind != "last":
                for k in range(DK):
                    hi(w, "xT", k, xT_hi[:, k, :])
                qk_hi(w, it, 0)
            if kind != "first":
                for g in range(GROUPS):
                    exps(2 * it - 1, g)
            if kind != "last":
                max_rows(w, it, 0)
                qk_hi(w, it, 1)
                for n in range(2):
                    act.wait_ge(work_ready, w.ready("V", n))
                    act.activation(v_aug[:, 2 * n:2 * n + 2, :, 0:DH],
                                   ps_w[:, w.bank("V", n), :].rearrange("p (t h d) -> p t h d", t=2, h=H), ACT.Copy)\
                       .then_inc(freed["act"], 1)
                for g in range(GROUPS):
                    exps(2 * it, g)
                max_rows(w, it, 1)
            if kind != "first":
                for k in range(DK):
                    act.wait_ge(work_ready, w.ready("x2T", k))
                    act.activation(x2T[:, k, :], ps_w[:, w.bank("x2T", k), :], ACT.Copy).then_inc(freed["act"], 1)

        iterations(act, body)

    @block.vector
    def _(dve):
        zeroed = Chain(dve, dve_chain)
        for u in range(UNITS):
            zeroed.step(dve.memset(q_st[u][:, :, :].bitcast(f32), 0.0))
            zeroed.step(dve.memset(k_st[u][:, :, :].bitcast(f32), 0.0))
        zeroed.wait()
        for u in range(UNITS):
            dve.memset(k_st[u][ROW_M:ROW_M + 1, :, :].bitcast(f32), 1.0).then_inc(stack_zeroed, 2)
        dve.wait_ge(weights_in, 48)
        zeroed.step(dve.tensor_copy(w_hi[:, :, :, :], wstage[:, :, :, :]))
        zeroed.wait()
        dve.tensor_tensor(out=w_lo[:, :, :, :], in0=wstage[:, :, :, :], in1=w_hi[:, :, :, :].bitcast(f32), op=ALU.subtract)\
           .then_inc(weights_split, 1)
        at_start = zeroed.n

        ticks = Ticks(dve, dve_ticks, lambda: dve.memset(dve_scratch[:, :], 0.0))

        def moments(n, source, base):
            chain = Chain(dve, dve_chain, base)
            for t in range(TB):
                chain.step(dve.bn_stats(out=stats[n][:, t, :], in_=source[:, t, :]))
            chain.wait()
            ticks.tick()
            for t in range(TB):
                last = dve.bn_aggr(out=mean_var[n][:, t, :], in_=stats[n][:, t, :])
            last.then_inc(moments_done[n], 1)
            return chain.n

        def lo(w, it, kind, which, n, hi_part, lo_part, scale=1.0):
            dve.wait_ge(hi_done, 6 * it + n + 1)
            dve.scalar_tensor_tensor(out=lo_part, in0=ps_w[:, w.bank(kind, which), :], scalar=scale,
                                     in1=hi_part.bitcast(f32), op0=ALU.mult, op1=ALU.subtract).then_inc(freed["dve"], 1)

        def qk_lo(w, it, u):
            lo(w, it, "Q", u, 2 + 2 * u, qk_sb[:, 0, 0, :], qk_sb[:, 0, 1, :], SCALE)
            lo(w, it, "K", u, 3 + 2 * u, qk_sb[:, 1, 0, :], qk_sb[:, 1, 1, :])

        def maxima(w, u, g):
            for n, (qt, heads) in enumerate(MAX_JOBS):
                dve.wait_ge(work_ready, w.ready("max", (u, g, n)))
                width = (qt + 1) * P
                h = g * GH + heads[0]
                dve.tensor_reduce(out=neg_max[u][:, qt, h:h + len(heads)],
                                  in_=ps_w[:, w.bank("max", (u, g, n)), 0:len(heads) * width].rearrange("p (h n) -> p h n", h=len(heads)),
                                  axis=AX.X, op=ALU.max, negate=True).then_inc(freed["dve"], 1)

        NORM_STEPS = 2

        def normalise(q, g, slot, base):
            chain = Chain(dve, dve_chain, base)
            dve.wait_ge(pv_done, GROUPS * q + g + 1)
            ticks.tick()
            chain.step(dve.stream_shuffle(sums[:, :], ps_o[:, :], [DH + n % DH for n in range(STRIP)]))
            chain.wait()
            chain.step(dve.reciprocal(sums[:, :], sums[:, :]))
            chain.wait()
            dve.tensor_tensor(out=o_norm[:, slot, :], in0=ps_o[:, :], in1=sums[:, :], op=ALU.mult).then_inc(o_done, 1)

        MOMENT_STEPS = TB
        dve.wait_ge(x_in, 16)
        moments(0, xb, at_start)
        IN_FIRST = MOMENT_STEPS + NORM_STEPS
        IN_FULL = 4 * NORM_STEPS + 2 * MOMENT_STEPS

        def body(it, kind):
            w = Work(it, kind)
            base = at_start + MOMENT_STEPS
            if kind != "first":
                base = base + IN_FIRST + (it - 1) * IN_FULL
            ticks.start(1 if kind == "first" else (it - 1) * 6 + 3)
            if kind == "last":
                ticks.base -= 1
                base = base - MOMENT_STEPS
            if kind != "last":
                for k in range(DK):
                    lo(w, it, "xT", k, k, xT_hi[:, k, :], xT_lo[:, k, :])
                qk_lo(w, it, 0)
            if kind != "first":
                normalise(2 * it - 2, 1, 1, base)
                base = base + NORM_STEPS
            for g in range(GROUPS):
                if kind != "last":
                    maxima(w, 0, g)
            if kind != "first":
                normalise(2 * it - 1, 0, 2, base)
                base = base + NORM_STEPS
            if kind != "last":
                qk_lo(w, it, 1)
            if kind != "first":
                normalise(2 * it - 1, 1, 3, base)
                base = base + NORM_STEPS
                dve.wait_ge(xres_in, 16 * it)
                dve.wait_ge(x1_out, 16 * it)
                dve.wait_ge(xn2_out, 16 * it)
                for n in range(2):
                    dve.wait_ge(work_ready, w.ready("O", n))
                    dve.tensor_tensor(out=x1[:, 2 * n:2 * n + 2, :], in0=ps_w[:, w.bank("O", n), :].rearrange("p (t d) -> p t d", t=2),
                                      in1=xres[:, 2 * n:2 * n + 2, :], op=ALU.add).then_inc(freed["dve"], 1)
                dve.wait_ge(freed["dve"], w.freed("O", 1)[1])
                moments(1, x1, base)
                base = base + MOMENT_STEPS
            if kind != "last":
                if not is_number(it, B - 1):
                    dve.wait_ge(x_in, 16 * (it + 2))
                    moments(0, xb, base)
                    base = base + MOMENT_STEPS
                for g in range(GROUPS):
                    maxima(w, 1, g)
                normalise(2 * it, 0, 0, base)
            if kind != "first":
                for n in range(2):
                    dve.wait_ge(work_ready, w.ready("L", n))
                    first_tile = (it - 1) * TB + 2 * n
                    dve.tensor_copy(logits_all[:, bass.ds(first_tile, 2), :],
                                    ps_w[:, w.bank("L", n), 0:2 * LOGITS].rearrange("p (t e) -> p t e", t=2)).then_inc(freed["dve"], 1)

        iterations(dve, body)

    @block.tensor
    def _(pe):
        def bank_for(w, kind, which):
            for e, count in w.needed(kind, which):
                pe.wait_ge(freed[e], count)
            return ps_w[:, w.bank(kind, which), :]

        def transposed(w, kind, source):
            for k in range(DK):
                out = bank_for(w, kind, k)
                for t in range(TB):
                    last = pe.transpose(out[:, t * P:(t + 1) * P], source[:, t, k * P:(k + 1) * P], ident[:, :])
                last.then_inc(work_ready, 1)

        def project_qk(w, u):
            pe.wait_ge(freed["dve"], w.freed("xT", 1)[1])
            for n, kind in enumerate(("Q", "K")):
                out = bank_for(w, kind, u)
                for k in range(DK):
                    cols = slice(u * P, (u + 1) * P)
                    last = exact_product(pe, out, (w_hi[:, n, k, cols], w_lo[:, n, k, cols]), (xT_hi[:, k, :], xT_lo[:, k, :]),
                                         start=k == 0, stop=k == DK - 1)
                last.then_inc(work_ready, 1)

        def project_v(w):
            for n in range(2):
                out = bank_for(w, "V", n)
                for t in (2 * n, 2 * n + 1):
                    for k in range(DK):
                        cols = slice(t * P, (t + 1) * P)
                        last = exact_product(pe, out[:, (t % 2) * D:(t % 2 + 1) * D], (xT_hi[:, k, cols], xT_lo[:, k, cols]),
                                             (w_hi[:, 2, k, :], w_lo[:, 2, k, :]), start=k == 0, stop=k == DK - 1)
                last.then_inc(work_ready, 1)

        def max_job(w, u, g, n):
            qt, heads = MAX_JOBS[n]
            width = (qt + 1) * P
            out = bank_for(w, "max", (u, g, n))
            for i, hh in enumerate(heads):
                h = g * GH + hh
                pe.matmul(out[:, i * width:(i + 1) * width], q_st[u][0:ROWS_QK, h, qt * P:(qt + 1) * P], k_st[u][0:ROWS_QK, h, 0:width],
                          start=True, stop=False)
                last = pe.matmul(out[:, (i + 1) * width - P:(i + 1) * width], ident16[:, :], mask16[:, :], start=False, stop=True)
            last.then_inc(work_ready, 1)

        def score_pair(q, u, g, p):
            n = PAIRS * (GROUPS * q + g) + p
            if not is_number(n, 0, 1):
                pe.wait_ge(exp_done, n - 1)
            for hh in range(GH):
                for kt in range(TB):
                    pair, col, width = block_of(hh, kt)
                    if pair == p:
                        h = g * GH + hh
                        last = pe.matmul(ps_s[:, (PAIRS * g + p) % 2, col:col + width], k_st[u][0:ROWS_ALL, h, kt * P:(kt + 1) * P],
                                         q_st[u][0:ROWS_ALL, h, kt * P:S], start=True, stop=True)
            last.then_inc(scores_ready, 1)

        def p_v(q, u, g):
            G = GROUPS * q + g
            pe.wait_ge(mask_done, PAIRS * (G + 1))
            if not is_number(G, 0):
                pe.wait_ge(o_done, G)
            for kt in range(TB):
                for hh in range(GH):
                    pair, col, width = block_of(hh, kt)
                    last = pe.matmul(ps_o[hh * STRIP:(hh + 1) * STRIP, kt * P:S], v_aug[:, kt, u * HU + g * GH + hh, :],
                                     probs[:, g, pair * PAIR + col:pair * PAIR + col + width], start=kt == 0, stop=kt == TB - 1)
            last.then_inc(pv_done, 1)

        def phase(w, it, u_max, q, u_scores):
            if u_max is not None:
                pe.wait_ge(stack_in[u_max], STACK_READS * 16 * (it + 1))
            if q is not None:
                pe.wait_ge(max_row_in[u_scores], 16 * ((it if u_scores == 0 else it - 1) + 1))
            for g in range(GROUPS):
                for p in range(PAIRS):
                    if q is not None:
                        score_pair(q, u_scores, g, p)
                    if u_max is not None:
                        for n in range(MAX_SPLIT[p], MAX_SPLIT[p + 1]):
                            max_job(w, u_max, g, n)
            if q is not None:
                p_v(q, u_scores, 0)

        def max_rows(w, u):
            out = bank_for(w, "mT", u)
            pe.wait_ge(freed["dve"], w.freed("max", (u, GROUPS - 1, len(MAX_JOBS) - 1))[1])
            for t in range(TB):
                last = pe.transpose(out[0:HU, t * P:(t + 1) * P], neg_max[u][:, t, :], ident[:, :])
            last.then_inc(work_ready, 1)

        def body(it, kind):
            w = Work(it, kind)
            if kind != "last":
                pe.wait_ge(xn_done, it + 1)
                transposed(w, "xT", xn)
                project_qk(w, 0)
            if kind != "first":
                p_v(2 * it - 2, 0, 1)
            phase(w, it, 0 if kind != "last" else None, 2 * it - 1 if kind != "first" else None, 1)
            if kind != "last":
                max_rows(w, 0)
                project_qk(w, 1)
            if kind != "first":
                p_v(2 * it - 1, 1, 1)
            if kind != "last":
                project_v(w)
            if kind != "first":
                pe.wait_ge(o_done, 4 * it)
                for n in range(2):
                    out = bank_for(w, "O", n)
                    for t in (2 * n, 2 * n + 1):
                        for s in range(UNITS * GROUPS):
                            last = pe.matmul(out[:, (t % 2) * D:(t % 2 + 1) * D], o_norm[:, s, t * P:(t + 1) * P], wo_sb[:, s, :],
                                             start=s == 0, stop=s == UNITS * GROUPS - 1)
                    last.then_inc(work_ready, 1)
            if kind != "last":
                pe.wait_ge(freed["act"], w.freed("V", 1)[1])
                phase(w, it, 1, 2 * it, 0)
                max_rows(w, 1)
            if kind != "first":
                pe.wait_ge(xn2_done, it)
                transposed(w, "x2T", xn2)
                pe.wait_ge(freed["act"], w.freed("x2T", 1)[1])
                for n in range(2):
                    out = bank_for(w, "L", n)
                    for t in (2 * n, 2 * n + 1):
                        for k in range(DK):
                            last = pe.matmul(out[:, (t % 2) * LOGITS:(t % 2 + 1) * LOGITS], x2T[:, k, t * P:(t + 1) * P], gates_sb[:, k, :],
                                             start=k == 0, stop=k == DK - 1)
                    last.then_inc(work_ready, 1)

        pe.wait_ge(pool_chain, POOL_CONSTS)
        pe.wait_ge(stack_zeroed, 2 * UNITS)
        pe.wait_ge(weights_split, 1)
        pe.wait_ge(wo_in, 32)
        iterations(pe, body)


FF = 704
FT = (FF + P - 1) // P
FF_LAST = FF - (FT - 1) * P
F = 128
EW = DK * 2 * F + D
MOE_TILES = (2 * B * S + E * (P - 1)) // P
MOE_TILES += MOE_TILES % 2
SLOTS = MOE_TILES * P
HALF = B // 2


def build_routing(nc, ctx, logits_all, slots, tile_expert, weight, gate):
    f32, bf16, i32, u32 = mybir.dt.float32, mybir.dt.bfloat16, mybir.dt.int32, mybir.dt.uint32
    ALU, ACT, AX = mybir.AluOpType, mybir.ActivationFunctionType, mybir.AxisListType

    def sb(name, shape, dt=f32):
        return ctx.enter_context(nc.sbuf_tensor(name, shape, dt))

    def sem(name):
        return ctx.enter_context(nc.semaphore(name))

    iota_e, iota_t = sb("iota_e", [P, E]), sb("iota_t", [P, MOE_TILES])
    before, ones = sb("before", [P, P], bf16), sb("ones", [P, P], bf16)
    top, index = sb("top", [P, NT, 8]), sb("index", [P, NT, 8], u32)
    index_f = sb("index_f", [P, NT, 2])
    args, exps = sb("args", [P, 2, NT]), sb("exps", [P, 2, NT])
    hot = sb("hot", [P, 2, NT, E])
    both = sb("both", [P, NT, E], bf16)
    counts, incl, excl = sb("counts", [P, E, NT]), sb("incl", [P, E, NT]), sb("excl", [P, E, NT])
    one_col = sb("one_col", [P, E * NT])
    total, tiles_i, tiles = sb("total", [P, E]), sb("tiles_i", [P, E], i32), sb("tiles", [P, E])
    tiles_to, tiles_before, base = sb("tiles_to", [P, E]), sb("tiles_before", [P, E]), sb("base", [P, E])
    slot_of, slot_f = sb("slot_of", [P, NT, E]), sb("slot_f", [P, 2, NT])
    passed, expert_f = sb("passed", [P, MOE_TILES, E]), sb("expert_f", [P, MOE_TILES])
    ps_rank = ctx.enter_context(nc.psum_tensor("ps_rank", [P, NT, E], f32))
    ps_count = ctx.enter_context(nc.psum_tensor("ps_count", [P, NT, E], f32))

    consts_done, consts_raw = sem("consts_done"), sem("consts_raw")
    args_ready, exps_ready = sem("args_ready"), sem("exps_ready")
    choices_ready, counts_ready = sem("choices_ready"), sem("counts_ready")
    dve_steps = sem("dve_steps")

    block = ctx.enter_context(nc.Block())

    @block.gpsimd
    def _(pool):
        pool.iota(iota_e[:, :], pattern=[[1, E]], base=0, channel_multiplier=0, allow_small_or_imprecise_dtypes=True).then_inc(consts_done, 1)
        pool.iota(iota_t[:, :], pattern=[[1, MOE_TILES]], base=0, channel_multiplier=0, allow_small_or_imprecise_dtypes=True).then_inc(consts_done, 1)
        pool.memset(one_col[:, :], 1.0).then_inc(consts_done, 1)
        pool.memset(ones[:, :], 1.0).then_inc(consts_done, 1)
        pool.memset(before[:, :], 1.0).then_inc(consts_raw, 1)
        pool.wait_ge(consts_raw, 1)
        pool.affine_select(out=before[:, :], in_=before[:, :], compare_op=ALU.is_gt, fill=0.0, base=0,
                           pattern=[[1, P]], channel_multiplier=-1).then_inc(consts_done, 1)

    @block.scalar
    def _(act):
        act.wait_ge(args_ready, 2)
        act.activation(exps[:, :, :], args[:, :, :], ACT.Exp).then_inc(exps_ready, 1)

    @block.tensor
    def _(pe):
        pe.wait_ge(consts_done, 5)
        pe.wait_ge(choices_ready, 1)
        flat = both[:, :, :].rearrange("p t e -> p (t e)")
        pe.matmul(ps_rank[:, :, :].rearrange("p t e -> p (t e)"), before[:, :], flat, start=True, stop=True)
        pe.matmul(ps_count[:, :, :].rearrange("p t e -> p (t e)"), ones[:, :], flat, start=True, stop=True).then_inc(counts_ready, 1)

    @block.vector
    def _(dve):
        chain = Chain(dve, dve_steps)

        def do(instruction):
            chain.step(instruction)
            chain.wait()

        for t in range(NT):
            chain.step(dve.max(out=top[:, t, :], in_=logits_all[:, t, 0:E]))
        chain.wait()
        dve.tensor_tensor(out=args[:, 0, :], in0=top[:, :, 1], in1=top[:, :, 0], op=ALU.subtract).then_inc(args_ready, 1)
        dve.tensor_scalar(out=args[:, 1, :], in0=logits_all[:, :, E], scalar1=-1.0, scalar2=None, op0=ALU.mult).then_inc(args_ready, 1)
        for t in range(NT):
            chain.step(dve.max_index(out=index[:, t, :], in_max=top[:, t, :], in_values=logits_all[:, t, 0:E]))
        chain.wait()
        do(dve.tensor_copy(index_f[:, :, :], index[:, :, 0:2]))
        dve.wait_ge(consts_done, 5)
        for c in range(2):
            chain.step(dve.tensor_tensor(out=hot[:, c], in0=iota_e[:, :].unsqueeze(1).to_broadcast([P, NT, E]),
                                         in1=index_f[:, :, c].unsqueeze(2).to_broadcast([P, NT, E]), op=ALU.is_equal))
        chain.wait()
        dve.tensor_tensor(out=both[:, :, :], in0=hot[:, 0], in1=hot[:, 1], op=ALU.add).then_inc(choices_ready, 1)
        dve.wait_ge(exps_ready, 1)
        do(dve.tensor_scalar(out=args[:, :, :], in0=exps[:, :, :], scalar1=1.0, scalar2=None, op0=ALU.add))
        do(dve.reciprocal(args[:, :, :], args[:, :, :]))
        dve.tensor_copy(weight[:, 0, :], args[:, 0, :])
        dve.tensor_tensor(out=weight[:, 1, :], in0=exps[:, 0, :], in1=args[:, 0, :], op=ALU.mult)
        dve.tensor_copy(gate[:, :], args[:, 1, :])
        dve.wait_ge(counts_ready, 1)
        do(dve.tensor_copy(counts[:, :, :], ps_count[:, :, :].rearrange("p t e -> p e t")))
        flat = lambda v: v[:, :, :].rearrange("p e t -> p (e t)")
        do(dve.tensor_tensor_scan(flat(incl), one_col[:, :], flat(counts), 0.0, ALU.mult, ALU.add))
        do(dve.tensor_tensor(out=excl[:, :, :], in0=incl[:, :, :], in1=counts[:, :, :], op=ALU.subtract))
        do(dve.tensor_reduce(out=total[:, :], in_=counts[:, :, :], axis=AX.X, op=ALU.add))
        do(dve.tensor_scalar(out=tiles_i[:, :], in0=total[:, :], scalar1=float(P - 1), scalar2=None, op0=ALU.add))
        do(dve.tensor_scalar(out=tiles_i[:, :], in0=tiles_i[:, :], scalar1=P.bit_length() - 1, scalar2=None, op0=ALU.arith_shift_right))
        do(dve.tensor_copy(tiles[:, :], tiles_i[:, :]))
        do(dve.tensor_tensor_scan(tiles_to[:, :], one_col[:, 0:E], tiles[:, :], 0.0, ALU.mult, ALU.add))
        do(dve.tensor_tensor(out=tiles_before[:, :], in0=tiles_to[:, :], in1=tiles[:, :], op=ALU.subtract))
        do(dve.scalar_tensor_tensor(out=base[:, :], in0=tiles_before[:, :], scalar=float(P), in1=excl[:, :, 0], op0=ALU.mult, op1=ALU.subtract))
        do(dve.tensor_tensor(out=excl[:, :, :], in0=excl[:, :, :], in1=base[:, :].unsqueeze(2).to_broadcast([P, E, NT]), op=ALU.add))
        do(dve.tensor_tensor(out=slot_of[:, :, :], in0=ps_rank[:, :, :], in1=excl[:, :, :].rearrange("p e t -> p t e"), op=ALU.add))
        for c in range(2):
            do(dve.tensor_tensor(out=hot[:, c], in0=hot[:, c], in1=slot_of[:, :, :], op=ALU.mult))
            do(dve.tensor_reduce(out=slot_f[:, c, :], in_=hot[:, c], axis=AX.X, op=ALU.add))
        dve.tensor_copy(slots[:, :, :], slot_f[:, :, :])
        do(dve.tensor_tensor(out=passed[:, :, :], in0=iota_t[:, :].unsqueeze(2).to_broadcast([P, MOE_TILES, E]),
                             in1=tiles_to[:, :].unsqueeze(1).to_broadcast([P, MOE_TILES, E]), op=ALU.is_ge))
        do(dve.tensor_reduce(out=expert_f[:, :], in_=passed[:, :, :], axis=AX.X, op=ALU.add))
        dve.tensor_scalar(out=tile_expert[:, :], in0=expert_f[:, :], scalar1=float(E - 1), scalar2=None, op0=ALU.min)


def build_ffn(nc, ctx, slots, tile_expert, weight, gate, x1_dram, xn2_dram, xg_dram, yg_dram, y1_dram,
              shared_up, shared_down, experts, out):
    f32, f32r = mybir.dt.float32, mybir.dt.float32r
    ALU, ACT = mybir.AluOpType, mybir.ActivationFunctionType

    def sb(name, shape, dt=f32):
        return ctx.enter_context(nc.sbuf_tensor(name, shape, dt))

    def sem(name):
        return ctx.enter_context(nc.semaphore(name))

    up_hi, up_lo = sb("up_hi", [P, DK * 2 * FF], f32r), sb("up_lo", [P, DK * 2 * FF], f32r)
    down_hi, down_lo = sb("down_hi", [P, FT * D], f32r), sb("down_lo", [P, FT * D], f32r)
    ex_hi, ex_lo = sb("ex_hi", [P, E * EW], f32r), sb("ex_lo", [P, E * EW], f32r)
    stage = sb("stage", [P, 2, EW])
    ident = sb("ident_f", [P, P])
    xn = sb("xn_f", [P, TB, D])
    x1 = sb("x1_f", [P, TB, D])
    xT_hi, xT_lo = sb("xT_hi_f", [P, DK, S], f32r), sb("xT_lo_f", [P, DK, S], f32r)
    silu, h = sb("silu", [P, 2, S]), sb("h", [P, 2, S])
    h_hi, h_lo = sb("h_hi", [P, FT, S], f32r), sb("h_lo", [P, FT, S], f32r)
    xg, y_e = xn[:, 0:2, :], xn[:, 2:4, :]
    xgT_hi, xgT_lo = (v[:, 0, :].rearrange("p (two n) -> p two n", two=2) for v in (xT_hi, xT_lo))
    hT_hi, hT_lo = (v[:, 1, 0:2 * P].rearrange("p (two n) -> p two n", two=2) for v in (xT_hi, xT_lo))
    silu_e, h_e = silu[:, :, 0:F], h[:, :, 0:F]
    srow = sb("srow", [P, 2, TB, D])
    back = srow[:, :, :, :].rearrange("p a (t c) d -> p (a t) c d", c=2)
    y1 = sb("y1", [P, TB, D])
    ps = ctx.enter_context(nc.psum_tensor("ps_f", [P, 8, BANK], f32))

    ident_made = sem("ident_made")
    stage_in, w_hi_done, w_split = [sem("stage_in0"), sem("stage_in1")], sem("w_hi_done"), sem("w_split")
    xn_in, x1_in, y1_out = sem("xn_in"), sem("x1_in_f"), sem("y1_out")
    xT_ready, xT_hi_done, xT_split = sem("xT_ready"), sem("xT_hi_done"), sem("xT_split")
    up_ready, silu_done, h_done, h_hi_done, h_split = (sem(n) for n in ("up_ready", "silu_done", "h_done", "h_hi_done", "h_split"))
    down_ready, y_done = sem("down_ready"), sem("y_done")
    rows_in, scattered = [sem("rows_in0"), sem("rows_in1")], [sem("scattered0"), sem("scattered1")]
    moe_in, moe_out = [sem("moe_in0"), sem("moe_in1")], [sem("moe_out0"), sem("moe_out1")]
    m_xT, m_xT_hi, m_xT_split = sem("m_xT"), sem("m_xT_hi"), sem("m_xT_split")
    m_up, m_silu, m_h = sem("m_up"), sem("m_silu"), sem("m_h")
    m_hT, m_hT_hi, m_hT_split = sem("m_hT"), sem("m_hT_hi"), sem("m_hT_split")
    m_down, m_y = sem("m_down"), sem("m_y")
    gathered = [sem(f"gathered{n}") for n in range(4)]
    y1_in, first_added, both_added, result_out = sem("y1_in"), sem("first_added"), sem("both_added"), sem("result_out")

    rows = lambda d: d.rearrange("(b t p) d -> b p t d", p=P, t=TB)
    x1_v, xn2_v, y1_v = rows(x1_dram), rows(xn2_dram), rows(y1_dram)
    out_v = out.rearrange("b (t p) d -> b p t d", p=P)
    SCATTERS = 2 * TB * 16

    def item(view, n):
        return view[n] if isinstance(n, int) else view[bass.ds(n, 1)].squeeze(0)

    halves = lambda n, width: slice(n * width, (n + 1) * width)
    chunks = [(shared_up[:, halves(n, FF)], up_hi[:, halves(n, FF)], up_lo[:, halves(n, FF)]) for n in range(4)]
    chunks += [(shared_down[:, halves(n, EW)], down_hi[:, halves(n, EW)], down_lo[:, halves(n, EW)]) for n in range(FT * D // EW)]
    NC = len(chunks)
    PER = E // HALF
    assert NC % 2 == 0 and PER % 2 == 0

    def two_halves(engine, first_half, between, second_half):
        first_half(0)
        with engine.Fori(1, HALF) as b:
            first_half(b)
        between()
        with engine.Fori(HALF, B) as b:
            second_half(b)

    def tiles_loop(engine, step, lag):
        for n in range(6):
            step(n, n % 2)
        with engine.Fori(6, MOE_TILES - 1, 2) as n:
            step(n, 0)
            step(n + 1, 1)
        for n in range(MOE_TILES, MOE_TILES + lag):
            step(n, n % 2)

    def width(j):
        return P if j < FT - 1 else FF_LAST

    def has(n):
        return not isinstance(n, int) or 0 <= n < MOE_TILES

    block = ctx.enter_context(nc.Block())

    @block.sync
    def _(sp):
        for n, (src, _, _) in enumerate(chunks):
            if n >= 2:
                sp.wait_ge(w_split, n - 1)
            sp.dma_start(stage[:, n % 2, 0:src.shape[1]], src).then_inc(stage_in[n % 2], 16)

        def load_xn(b):
            sp.dma_start(xn[:, :, :], item(xn2_v, b)).then_inc(xn_in, 16)

        def load_x1(b):
            sp.wait_ge(y1_out, 16 * b)
            sp.dma_start(x1[:, :, :], item(x1_v, b)).then_inc(x1_in, 16)

        def store_y1(b):
            sp.wait_ge(y_done, TB * (b + 1))
            sp.dma_start(item(y1_v, b), x1[:, :, :]).then_inc(y1_out, 16)

        def first_half(b):
            load_x1(b)
            sp.wait_ge(xT_ready, DK * (b + 1))
            load_xn(b + 1)
            for par in range(2):
                sp.wait_ge(scattered[par], SCATTERS * b)
                sp.dma_start(srow[:, par], item(xn2_v, b * 2 + par)).then_inc(rows_in[par], 16)
            for i in range(PER):
                e = b * PER + i
                sp.wait_ge(w_split, e + (NC - 1))
                sp.dma_start(stage[:, i % 2, :], item(experts, e)).then_inc(stage_in[i % 2], 16)
            store_y1(b)

        def tiles_step(n, par):
            if has(n):
                if not is_number(n, 0, 1):
                    sp.wait_ge(m_xT, n - 1)
                sp.dma_start(xg[:, par, :], item(xg_dram, n)).then_inc(moe_in[par], 16)
            if has(n - 4):
                sp.wait_ge(m_y, n - 3)
                sp.dma_start(item(yg_dram, n - 4), y_e[:, par, :]).then_inc(moe_out[par], 16)

        def tiles():
            for par in range(2):
                sp.wait_ge(scattered[par], SCATTERS * HALF)
            tiles_loop(sp, tiles_step, 4)
            for par in range(2):
                sp.wait_ge(moe_out[par], 16 * (MOE_TILES // 2))
            load_xn(HALF)

        def load_y1(b):
            sp.wait_ge(result_out, 16 * b)
            sp.dma_start(y1[:, :, :], item(y1_v, b)).then_inc(y1_in, 16)

        def store_result(b):
            sp.wait_ge(both_added, TB * (b + 1))
            sp.dma_start(item(out_v, b), y1[:, :, :]).then_inc(result_out, 16)

        def second_half(b, last):
            load_x1(b)
            load_y1(b - HALF)
            if not last:
                sp.wait_ge(xT_ready, DK * (b + 1))
                load_xn(b + 1)
            store_y1(b)
            store_result(b - HALF)

        load_xn(0)
        first_half(0)
        with sp.Fori(1, HALF - 1) as b:
            first_half(b)
        load_x1(HALF - 1)
        b = HALF - 1
        for par in range(2):
            sp.wait_ge(scattered[par], SCATTERS * b)
            sp.dma_start(srow[:, par], item(xn2_v, b * 2 + par)).then_inc(rows_in[par], 16)
        for i in range(PER):
            e = b * PER + i
            sp.wait_ge(w_split, e + (NC - 1))
            sp.dma_start(stage[:, i % 2, :], item(experts, e)).then_inc(stage_in[i % 2], 16)
        store_y1(b)
        tiles()
        second_half(HALF, False)
        with sp.Fori(HALF + 1, B - 1) as b:
            second_half(b, False)
        second_half(B - 1, True)
        sp.wait_ge(y1_out, 16 * B)
        with sp.Fori(HALF, B) as b:
            load_y1(b)
            store_result(b)
        sp.wait_ge(result_out, 16 * B)

    @block.gpsimd
    def _(pool):
        pool.memset(ident[:, :], 0.0).then_inc(ident_made, 1)
        pool.wait_ge(ident_made, 1)
        pool.affine_select(out=ident[:, :], in_=ident[:, :], compare_op=ALU.not_equal, fill=1.0, base=0,
                           pattern=[[-1, P]], channel_multiplier=1).then_inc(ident_made, 1)
        xg_rows, yg_rows = (v.rearrange("n p d -> (n p) d") for v in (xg_dram, yg_dram))
        for n in range(NT):
            b, t = divmod(n, TB)
            if t == 0:
                pool.wait_ge(rows_in[b % 2], 16 * (b // 2 + 1))
            for c in range(2):
                pool.indirect_dma_start(out=xg_rows, out_offset=bass.IndirectOffsetOnAxis(ap=slots[:, c, n:n + 1], axis=0),
                                        in_=srow[:, b % 2, t, :], in_offset=None).then_inc(scattered[b % 2], 16)
        for par in range(2):
            pool.wait_ge(scattered[par], SCATTERS * HALF)
            pool.wait_ge(moe_out[par], 16 * (MOE_TILES // 2))
        for n in range(NT):
            if n >= 4:
                pool.wait_ge(both_added, n - 3)
            for c in range(2):
                pool.indirect_dma_start(out=back[:, n % 4, c, :], out_offset=None, in_=yg_rows,
                                        in_offset=bass.IndirectOffsetOnAxis(ap=slots[:, c, n:n + 1], axis=0)).then_inc(gathered[n % 4], 16)

    @block.scalar
    def _(act):
        for n, (_, hi, _) in enumerate(chunks):
            act.wait_ge(stage_in[n % 2], 16 * (n // 2 + 1))
            act.activation(hi, stage[:, n % 2, 0:hi.shape[1]], ACT.Copy).then_inc(w_hi_done, 1)

        def shared(b):
            for k in range(DK):
                act.wait_ge(xT_ready, b * DK + (k + 1))
                act.activation(xT_hi[:, k, :], ps[:, k, :], ACT.Copy).then_inc(xT_hi_done, 1)
            for j in range(FT + 1):
                n = b * FT + j
                if j < FT:
                    act.wait_ge(up_ready, n + 1)
                    act.wait_ge(h_done, n - 1 if j else n)
                    act.activation(silu[0:width(j), j % 2, :], ps[0:width(j), 2 + 2 * (j % 2), :], ACT.Silu).then_inc(silu_done, 1)
                if j > 0:
                    act.wait_ge(h_done, n)
                    if j == 1:
                        act.wait_ge(down_ready, b * 2)
                    act.activation(h_hi[0:width(j - 1), j - 1, :], h[0:width(j - 1), (j - 1) % 2, :], ACT.Copy).then_inc(h_hi_done, 1)

        def first_half(b):
            shared(b)
            for i in range(PER):
                e = b * PER + i
                act.wait_ge(stage_in[i % 2], 8 * (e - i % 2) + 16 * (NC // 2 + 1))
                act.activation(ex_hi[:, bass.ds(e * EW, EW)], stage[:, i % 2, :], ACT.Copy).then_inc(w_hi_done, 1)

        def tiles_step(n, par):
            if has(n):
                act.wait_ge(m_xT, n + 1)
                act.activation(xgT_hi[:, par, :], ps[:, par, 0:D], ACT.Copy).then_inc(m_xT_hi, 1)
            if has(n - 1):
                act.wait_ge(m_up, n)
                if has(n - 3):
                    act.wait_ge(m_h, n - 2)
                act.activation(silu_e[:, 1 - par, :], ps[:, 3 - par, 0:F], ACT.Silu).then_inc(m_silu, 1)
            if has(n - 2):
                act.wait_ge(m_hT, n - 1)
                act.activation(hT_hi[:, par, :], ps[:, 4 + par, 0:P], ACT.Copy).then_inc(m_hT_hi, 1)

        two_halves(act, first_half, lambda: tiles_loop(act, tiles_step, 2), shared)

    @block.vector
    def _(dve):
        for n, (_, hi, lo) in enumerate(chunks):
            dve.wait_ge(w_hi_done, n + 1)
            dve.tensor_tensor(out=lo, in0=stage[:, n % 2, 0:hi.shape[1]], in1=hi.bitcast(f32), op=ALU.subtract).then_inc(w_split, 1)

        def shared(b):
            for k in range(DK):
                dve.wait_ge(xT_hi_done, b * DK + (k + 1))
                dve.tensor_tensor(out=xT_lo[:, k, :], in0=ps[:, k, :], in1=xT_hi[:, k, :].bitcast(f32), op=ALU.subtract).then_inc(xT_split, 1)
            for j in range(FT + 1):
                n = b * FT + j
                if j < FT:
                    dve.wait_ge(silu_done, n + 1)
                    for done in (h_hi_done, h_split):
                        dve.wait_ge(done, n - 1 if j else n)
                    up = ps[:, 3 + 2 * (j % 2), :] if j < FT - 1 else ps[FF_LAST:P, 2 + 2 * (j % 2), :]
                    dve.tensor_tensor(out=h[0:width(j), j % 2, :], in0=up, in1=silu[0:width(j), j % 2, :], op=ALU.mult).then_inc(h_done, 1)
                if j > 0:
                    dve.wait_ge(h_hi_done, n)
                    dve.tensor_tensor(out=h_lo[0:width(j - 1), j - 1, :], in0=h[0:width(j - 1), (j - 1) % 2, :],
                                      in1=h_hi[0:width(j - 1), j - 1, :].bitcast(f32), op=ALU.subtract).then_inc(h_split, 1)
            dve.wait_ge(x1_in, 16 * (b + 1))
            for t in range(TB):
                dve.wait_ge(down_ready, b * 2 + (t // 2 + 1))
                dve.scalar_tensor_tensor(out=x1[:, t, :], in0=ps[:, 6 + t // 2, (t % 2) * D:(t % 2 + 1) * D],
                                         scalar=gate[:, bass.ds(b * TB + t, 1)], in1=x1[:, t, :], op0=ALU.mult, op1=ALU.add).then_inc(y_done, 1)

        def first_half(b):
            shared(b)
            for i in range(PER):
                e = b * PER + i
                dve.wait_ge(w_hi_done, e + (NC + 1))
                dve.tensor_tensor(out=ex_lo[:, bass.ds(e * EW, EW)], in0=stage[:, i % 2, :],
                                  in1=ex_hi[:, bass.ds(e * EW, EW)].bitcast(f32), op=ALU.subtract).then_inc(w_split, 1)

        def tiles_step(n, par):
            if has(n):
                dve.wait_ge(m_xT_hi, n + 1)
                dve.tensor_tensor(out=xgT_lo[:, par, :], in0=ps[:, par, 0:D], in1=xgT_hi[:, par, :].bitcast(f32), op=ALU.subtract)\
                   .then_inc(m_xT_split, 1)
            if has(n - 1):
                dve.wait_ge(m_silu, n)
                if has(n - 3):
                    dve.wait_ge(m_hT, n - 2)
                dve.tensor_tensor(out=h_e[:, 1 - par, :], in0=ps[:, 3 - par, F:2 * F], in1=silu_e[:, 1 - par, :], op=ALU.mult).then_inc(m_h, 1)
            if has(n - 2):
                dve.wait_ge(m_hT_hi, n - 1)
                dve.tensor_tensor(out=hT_lo[:, par, :], in0=ps[:, 4 + par, 0:P], in1=hT_hi[:, par, :].bitcast(f32), op=ALU.subtract)\
                   .then_inc(m_hT_split, 1)
            if has(n - 3):
                dve.wait_ge(m_down, n - 2)
                if has(n - 5):
                    dve.wait_ge(moe_out[1 - par], 8 * (n - 3 - (1 - par)))
                dve.tensor_copy(y_e[:, 1 - par, :], ps[:, 7 - par, 0:D]).then_inc(m_y, 1)

        def combine(b):
            dve.wait_ge(y1_in, 16 * (b + 1))
            for c, done in enumerate((first_added, both_added)):
                for t in range(TB):
                    if c == 0:
                        dve.wait_ge(gathered[t], 32 * (b + 1))
                    elif t == 0:
                        dve.wait_ge(first_added, TB * (b + 1))
                    dve.scalar_tensor_tensor(out=y1[:, t, :], in0=back[:, t, c, :], scalar=weight[:, c, bass.ds(b * TB + t, 1)],
                                             in1=y1[:, t, :], op0=ALU.mult, op1=ALU.add).then_inc(done, 1)

        def second_half(b):
            shared(b)
            combine(b - HALF)

        two_halves(dve, first_half, lambda: tiles_loop(dve, tiles_step, 3), second_half)
        with dve.Fori(HALF, B) as b:
            combine(b)

    @block.tensor
    def _(pe):
        def shared(b):
            pe.wait_ge(xn_in, 16 * (b + 1))
            pe.wait_ge(xT_split, b * DK)
            for k in range(DK):
                for t in range(TB):
                    last = pe.transpose(ps[:, k, t * P:(t + 1) * P], xn[:, t, k * P:(k + 1) * P], ident[:, :])
                last.then_inc(xT_ready, 1)
            pe.wait_ge(xT_split, (b + 1) * DK)
            for j in range(FT):
                pe.wait_ge(h_done, b * FT + max(j - 1, 0))
                tiles_ = 2 if j < FT - 1 else 1
                for i in range(tiles_):
                    col = (2 * j + i) * P
                    for k in range(DK):
                        at = slice(k * 2 * FF + col, k * 2 * FF + col + P)
                        last = exact_product(pe, ps[:, 2 + 2 * (j % 2) + i, :], (up_hi[:, at], up_lo[:, at]), (xT_hi[:, k, :], xT_lo[:, k, :]),
                                             start=k == 0, stop=k == DK - 1)
                last.then_inc(up_ready, 1)
            pe.wait_ge(h_split, (b + 1) * FT)
            pe.wait_ge(y_done, b * TB)
            for t in range(TB):
                for j in range(FT):
                    height = P if j < FT - 1 else FF_LAST
                    last = exact_product(pe, ps[:, 6 + t // 2, (t % 2) * D:(t % 2 + 1) * D],
                                         tuple(v[0:height, j, t * P:(t + 1) * P] for v in (h_hi, h_lo)),
                                         tuple(v[0:height, j * D:(j + 1) * D] for v in (down_hi, down_lo)), start=j == 0, stop=j == FT - 1)
                if t % 2:
                    last.then_inc(down_ready, 1)

        def expert_of(n):
            return pe.value_load(tile_expert[0:1, bass.ds(n, 1)], min_val=0, max_val=E - 1)

        def tiles_step(n, par):
            if has(n):
                pe.wait_ge(moe_in[par], 8 * (n - par) + 16)
                if has(n - 2):
                    pe.wait_ge(m_xT_split, n - 1)
                for k in range(DK):
                    last = pe.transpose(ps[:, par, k * P:(k + 1) * P], xg[:, par, k * P:(k + 1) * P], ident[:, :])
                last.then_inc(m_xT, 1)
            if has(n - 1):
                q = 1 - par
                pe.wait_ge(m_xT_split, n)
                if has(n - 3):
                    pe.wait_ge(m_h, n - 2)
                e = expert_of(n - 1)
                for k in range(DK):
                    cols = bass.ds(e * EW + k * 2 * F, 2 * F)
                    last = exact_product(pe, ps[:, 2 + q, 0:2 * F], tuple(v[:, q, k * P:(k + 1) * P] for v in (xgT_hi, xgT_lo)),
                                         (ex_hi[:, cols], ex_lo[:, cols]), start=k == 0, stop=k == DK - 1)
                last.then_inc(m_up, 1)
            if has(n - 2):
                pe.wait_ge(m_h, n - 1)
                if has(n - 4):
                    pe.wait_ge(m_hT_split, n - 3)
                pe.transpose(ps[:, 4 + par, 0:P], h_e[:, par, :], ident[:, :]).then_inc(m_hT, 1)
            if has(n - 3):
                q = 1 - par
                pe.wait_ge(m_hT_split, n - 2)
                if has(n - 5):
                    pe.wait_ge(m_y, n - 4)
                e = expert_of(n - 3)
                cols = bass.ds(e * EW + DK * 2 * F, D)
                exact_product(pe, ps[:, 6 + q, 0:D], tuple(v[:, q, :] for v in (hT_hi, hT_lo)), (ex_hi[:, cols], ex_lo[:, cols]),
                              start=True, stop=True).then_inc(m_down, 1)

        def tiles():
            pe.wait_ge(w_split, NC + E)
            pe.wait_ge(xT_split, HALF * DK)
            pe.wait_ge(h_done, HALF * FT)
            pe.wait_ge(y_done, HALF * TB)
            tiles_loop(pe, tiles_step, 3)
            pe.wait_ge(m_xT_split, MOE_TILES)
            pe.wait_ge(m_h, MOE_TILES)
            pe.wait_ge(m_hT_split, MOE_TILES)
            pe.wait_ge(m_y, MOE_TILES)

        pe.wait_ge(ident_made, 2)
        pe.wait_ge(w_split, NC)
        two_halves(pe, shared, tiles, shared)


def block_program(nc, x, wq, wk, wv, wo, gates, shared_up, shared_down, experts, out):
    f32, i32 = mybir.dt.float32, mybir.dt.int32
    dram = lambda name, shape: nc.dram_tensor(name, shape, f32).ap()
    x1_dram, xn2_dram, y1_dram = (dram(n, [B * S, D]) for n in ("x1_dram", "xn2_dram", "y1_dram"))
    qk_dram = dram("qk_dram", [UNITS, 2, P, 2, S])
    xg_dram, yg_dram = (dram(n, [MOE_TILES, P, D]) for n in ("xg_dram", "yg_dram"))
    with ExitStack() as whole:
        sb = lambda name, shape, dt: whole.enter_context(nc.sbuf_tensor(name, shape, dt))
        logits_all = sb("logits_all", [P, NT, LOGITS], f32)
        slots, tile_expert = sb("slots", [P, 2, NT], i32), sb("tile_expert", [P, MOE_TILES], i32)
        weight, gate = sb("weight", [P, 2, NT], f32), sb("gate", [P, NT], f32)
        with ExitStack() as ctx:
            build_attention(nc, ctx, x, wq, wk, wv, wo, gates, logits_all, qk_dram, x1_dram, xn2_dram, xg_dram)
        with ExitStack() as ctx:
            build_routing(nc, ctx, logits_all, slots, tile_expert, weight, gate)
        with ExitStack() as ctx:
            build_ffn(nc, ctx, slots, tile_expert, weight, gate, x1_dram, xn2_dram, xg_dram, yg_dram, y1_dram,
                      shared_up, shared_down, experts, out)


def kernel(L0_attn_x, L0_attn_W_Q, L0_attn_W_K, L0_attn_W_V, L0_attn_W_O, L0_ffn_gate_w, L0_ffn_w_gate_up, L0_ffn_w_down,
           L0_ffn_shared_w_gate, L0_ffn_shared_w_up, L0_ffn_shared_w_down, L0_ffn_shared_gate_w):
    import numpy as np
    import concourse.bacc as bacc
    from concourse.bass_utils import run_bass_kernel_spmd

    def by_input(w):
        w = np.asarray(w)
        return np.ascontiguousarray(w.T.reshape(-1, P, w.shape[0]).transpose(1, 0, 2))

    wo = np.zeros((UNITS * GROUPS, GH, STRIP, D), np.float32)
    wo[:, :, :DH] = np.asarray(L0_attn_W_O).T.reshape(UNITS * GROUPS, GH, DH, D)
    wo = np.ascontiguousarray(wo.reshape(UNITS * GROUPS, P, D).transpose(1, 0, 2))
    gates = by_input(np.concatenate([np.asarray(L0_ffn_gate_w), np.asarray(L0_ffn_shared_gate_w)]))
    tiles = []
    for lo in range(0, FF, P):
        tiles += [np.asarray(L0_ffn_shared_w_gate)[lo:lo + P], np.asarray(L0_ffn_shared_w_up)[lo:lo + P]]
    shared_up = by_input(np.concatenate(tiles)).reshape(P, -1)
    down = np.zeros((FT * P, D), np.float32)
    down[:FF] = np.asarray(L0_ffn_shared_w_down).T
    shared_down = np.ascontiguousarray(down.reshape(FT, P, D).transpose(1, 0, 2)).reshape(P, -1)
    gate_up = np.asarray(L0_ffn_w_gate_up).reshape(E, DK, P, 2 * F).transpose(0, 2, 1, 3).reshape(E, P, -1)
    experts = np.ascontiguousarray(np.concatenate([gate_up, np.asarray(L0_ffn_w_down)], axis=2))

    arrays = {"x": np.asarray(L0_attn_x), "wq": by_input(L0_attn_W_Q), "wk": by_input(L0_attn_W_K), "wv": by_input(L0_attn_W_V),
              "wo": wo, "gates": gates, "shared_up": shared_up, "shared_down": shared_down, "experts": experts}
    nc = bacc.Bacc("TRN2", target_bir_lowering=False, num_devices=1)
    args = [nc.dram_tensor(n, a.shape, mybir.dt.from_np(a.dtype), kind="ExternalInput").ap() for n, a in arrays.items()]
    out = nc.dram_tensor("out", (B, S, D), mybir.dt.float32, kind="ExternalOutput").ap()
    block_program(nc, *args, out)
    result = run_bass_kernel_spmd(nc, [arrays], core_ids=[0])
    return result.results[0]["out"]
```

```python
import concourse.bass as bass
from concourse import mybir
from contextlib import ExitStack

P = 128
B, S, D = 8, 512, 256
H, DH = 16, 16
DK = D // P
TB = S // P
NT = B * TB
HU = 8
GH = 4
UNITS = H // HU
GROUPS = HU // GH
STRIP = P // GH
E = 16
LOGITS = E + 1
EPS = 1e-5
NEG = -1.0e30
SCALE = float(DH) ** -0.5

ROW_HH, ROW_HL, ROW_LH = 0, DH, 2 * DH
ROWS_QK = 96
ROW_M = 96
ROWS_ALL = ROW_M + 1

BANK = 512
PAIRS = 5
PAIR = 2 * BANK


def block_of(head, kt):
    width = (TB - kt) * P
    if kt == 0:
        return head // 2, (head % 2) * BANK, width
    if kt == 1:
        return 2 + head // 2, (head % 2) * BANK, width
    if kt == 3:
        return 2 + head // 2, (head % 2) * BANK + 3 * P, width
    return 4, head * 2 * P, width


def max_jobs_of_group():
    return [(3, (h,)) for h in range(GH)] + [(2, (h,)) for h in range(GH)] + [(1, (0, 1)), (1, (2, 3)), (0, (0, 1, 2, 3))]


MAX_JOBS = max_jobs_of_group()
MAX_SPLIT = [0, 2, 4, 6, 8, 11]

WORK_BANKS = 3


def phase_steps(u, with_max, with_scores, between):
    steps = []
    for g in range(GROUPS):
        for p in range(PAIRS):
            if with_scores:
                steps.append(("S", (1 - u, g, p)))
            if with_max:
                steps += [("max", (u, g, n)) for n in range(MAX_SPLIT[p], MAX_SPLIT[p + 1])]
            steps += between.get((g, p), [])
    return steps


def steps_of(kind):
    before = kind in ("full", "eighth", "last")
    this = kind in ("first", "full", "eighth")
    after = kind in ("first", "full")
    project = [("xT", 0), ("xT", 1), ("Q", 0), ("K", 0)]
    if kind == "start":
        return [("moments_x", 0)] + project

    def only(condition, *steps):
        return list(steps) if condition else []

    steps = only(before, ("PV", 1))
    steps += phase_steps(0, this, before, {(0, 1): only(before, ("oT", 1)), (1, 3): only(before, ("PV", 2))})
    steps += only(this, ("mT", 0), ("Q", 1), ("K", 1)) + only(before, ("oT", 2), ("PV", 3))
    steps += only(this, ("V", 0), ("V", 1)) + only(before, ("oT", 3)) + only(after, ("moments_x", 0))
    steps += phase_steps(1, this, this, {(0, 1): only(before, ("oTT", 0), ("oTT", 1)),
                                         (0, 4): only(before, ("O", 0), ("O", 1), ("moments_x1", 0)),
                                         (1, 3): only(this, ("PV", 0))})
    if after:
        steps += project
    steps += only(this, ("mT", 1), ("oT", 0))
    steps += only(before, ("x2T", 0), ("x2T", 1), ("L", 0), ("L", 1))
    return steps


EMPTIED_BY = {"xT": "dve", "Q": "dve", "K": "dve", "max": "dve", "mT": "act", "V": "act", "oT": "dve", "oTT": "dve",
              "O": "dve", "x2T": "act", "L": "dve"}
SPLIT_STEPS = ("xT", "Q", "K", "oTT")


class Work:

    def __init__(self, it, kind):
        self.steps, self.kind = steps_of(kind), kind
        self.banked = [x for x in self.steps if x[0] in EMPTIED_BY]
        self.it = it

    @staticmethod
    def amount(steps, what):
        if what == "ready":
            return sum(k in EMPTIED_BY for k, _ in steps)
        if what == "hi":
            return sum(k in SPLIT_STEPS for k, _ in steps)
        if what == "chain":
            return sum({"moments_x": TB, "moments_x1": TB, "oT": 1}.get(k, 0) for k, _ in steps)
        if what == "ticks":
            return sum(k in ("moments_x", "moments_x1") for k, _ in steps)
        return sum(EMPTIED_BY.get(k) == what for k, _ in steps)

    def base(self, what):
        if self.kind == "start":
            return 0
        base = self.amount(steps_of("start"), what)
        if self.kind == "first":
            return base
        full, eighth = (self.amount(steps_of(k), what) for k in ("full", "eighth"))
        base += self.amount(steps_of("first"), what)
        if self.kind == "last":
            return base + (B - 2) * full + eighth
        return (self.it - 1) * full + base

    def before(self, what, kind, which):
        return self.base(what) + self.amount(self.steps[:self.steps.index((kind, which))], what)

    def upto(self, what, kind, which):
        return self.base(what) + self.amount(self.steps[:self.steps.index((kind, which)) + 1], what)

    def bank(self, kind, which):
        first = {"start": (), "first": ("start",)}.get(self.kind, ("start", "first"))
        return (sum(self.amount(steps_of(k), "ready") for k in first) + self.banked.index((kind, which))) % WORK_BANKS

    def freed(self, kind, which):
        return EMPTIED_BY[kind], self.upto(EMPTIED_BY[kind], kind, which)

    def needed(self, kind, which):
        n = self.banked.index((kind, which)) - WORK_BANKS
        if n >= 0:
            return [self.freed(*self.banked[n])]
        return [] if self.kind == "start" else [(e, self.base(e)) for e in ("act", "dve")]


assert Work.amount(steps_of("full"), "ready") % WORK_BANKS == 0


def is_number(value, *which):
    return isinstance(value, int) and value in which


class Chain:

    def __init__(self, engine, sem, base=0):
        self.engine, self.sem, self.base, self.n = engine, sem, base, 0

    def step(self, instruction):
        instruction.then_inc(self.sem, 1)
        self.n += 1

    def wait(self):
        self.engine.wait_ge(self.sem, self.base + self.n)


class Ticks(Chain):

    def __init__(self, engine, sem, tiny):
        super().__init__(engine, sem)
        self.tiny = tiny

    def start(self, base):
        self.base, self.n = base, 0

    def tick(self):
        self.wait()
        self.step(self.tiny())


def exact_product(pe, out, stationary, moving, start, stop):
    (s_hi, s_lo), (m_hi, m_lo) = stationary, moving
    pe.matmul(out, s_hi, m_hi, start=start, stop=False)
    pe.matmul(out, s_hi, m_lo, start=False, stop=False)
    return pe.matmul(out, s_lo, m_hi, start=False, stop=stop)


def build_attention(nc, ctx, x, wq, wk, wv, wo, gates, logits_all, qk_dram, x1_dram, xn2_dram, xg_dram):
    f32, f32r, bf16 = mybir.dt.float32, mybir.dt.float32r, mybir.dt.bfloat16
    ALU, ACT, AX = mybir.AluOpType, mybir.ActivationFunctionType, mybir.AxisListType

    def sb(name, shape, dt):
        return ctx.enter_context(nc.sbuf_tensor(name, shape, dt))

    def ps(name, shape):
        return ctx.enter_context(nc.psum_tensor(name, shape, f32))

    def sem(name):
        return ctx.enter_context(nc.semaphore(name))

    wstage = sb("wstage", [P, 4, DK, D], f32)
    w_hi = sb("w_hi", [P, 4, DK, D], f32r)
    w_lo = sb("w_lo", [P, 4, DK, D], f32r)
    gates_sb = sb("gates_sb", [P, DK, LOGITS], f32)
    ident = sb("ident", [P, P], f32)
    ident16 = sb("ident16", [P, P], bf16)
    mask16 = sb("mask16", [P, P], bf16)
    minus_half = sb("minus_half", [P, TB], f32)
    zeros = sb("zeros", [P, 4, D], f32)
    xb = sb("xb", [P, TB, D], f32)
    xn = sb("xn", [P, TB, D], f32)
    xT_hi = sb("xT_hi", [P, DK, S], f32r)
    xT_lo = sb("xT_lo", [P, DK, S], f32r)
    qk_sb = sb("qk_sb", [P, 2, 2, S], f32r)
    q_st = [sb(f"q_st{u}", [P, HU, S], f32r) for u in range(UNITS)]
    k_st = [sb(f"k_st{u}", [P, HU, S], f32r) for u in range(UNITS)]
    v_aug = sb("v_aug", [P, TB, H, STRIP], f32)
    probs = sb("probs", [P, GROUPS, PAIRS * PAIR], f32)
    neg_max = [sb(f"neg_max{u}", [P, TB, HU], f32) for u in range(UNITS)]
    max_row = [sb(f"max_row{u}", [HU, S], f32r) for u in range(UNITS)]
    o_raw = sb("o_raw", [P, 2, S], f32)
    inverse = sb("inverse", [P, TB, GH], f32)
    o_tok = sb("o_tok", [P, TB, D], f32)
    oT_hi, oT_lo = sb("oT_hi", [P, DK, S], f32r), sb("oT_lo", [P, DK, S], f32r)
    xres = sb("xres", [P, TB, D], f32)
    x1 = sb("x1", [P, TB, D], f32)
    xn2 = sb("xn2", [P, TB, D], f32)
    x2T = sb("x2T", [P, DK, S], f32)
    stats = [sb(f"stats{n}", [P, TB, 6], f32) for n in range(2)]
    mean_var = [sb(f"mean_var{n}", [P, TB, 2], f32) for n in range(2)]
    rstd = [sb(f"rstd{n}", [P, TB], f32) for n in range(2)]
    pool_scratch, dve_scratch = sb("pool_scratch", [1, 3], f32), sb("dve_scratch", [1, 1], f32)

    ps_s = ps("ps_s", [P, 2, PAIR])
    ps_o = ps("ps_o", [P, S])
    ps_w = ps("ps_w", [P, WORK_BANKS, BANK])

    weights_in, gates_in = sem("weights_in"), sem("gates_in")
    stack_made = [sem(f"stack_made{u}") for u in range(UNITS)]
    zeros_made, weights_split = sem("zeros_made"), sem("weights_split")
    zero_rows_out = sem("zero_rows_out")
    x_in, xres_in = sem("x_in"), sem("xres_in")
    moments_done = [sem(f"moments_done{n}") for n in range(2)]
    xn_done, xn2_done = sem("xn_done"), sem("xn2_done")
    work_ready = sem("work_ready")
    freed = {"act": sem("freed_by_act"), "dve": sem("freed_by_dve")}
    hi_done = sem("hi_done")
    stack_out = sem("stack_out")
    stack_in = [sem(f"stack_in{u}") for u in range(UNITS)]
    max_row_in = [sem(f"max_row_in{u}") for u in range(UNITS)]
    scores_ready, exp_done, mask_done = sem("scores_ready"), sem("exp_done"), sem("mask_done")
    pv_done, o_copied = sem("pv_done"), sem("o_copied")
    x1_out, xn2_out = sem("x1_out"), sem("xn2_out")
    dve_chain, pool_chain, dve_ticks, pool_ticks = (sem(n) for n in ("dve_chain", "pool_chain", "dve_ticks", "pool_ticks"))

    x_v = x.rearrange("b (t p) d -> b p t d", p=P)
    x1_v = x1_dram.rearrange("(b t p) d -> b p t d", b=B, p=P)
    xn2_v = xn2_dram.rearrange("(b t p) d -> b p t d", b=B, p=P)
    STACK_READS = 6

    def batch(view, b):
        if isinstance(b, int):
            return view[b]
        return view[bass.ds(b, 1)].rearrange("o p t d -> (o p) t d")

    def iterations(engine, body):
        body(0, "first")
        with engine.Fori(1, B - 1) as it:
            body(it, "full")
        body(B - 1, "eighth")
        body(B, "last")

    def has(kind):
        return kind in ("full", "eighth", "last"), kind != "last", kind in ("first", "full")

    def group_of(it, slot):
        return 4 * it + (slot - 4 if slot else 0)

    POOL_CONSTS = 8

    block = ctx.enter_context(nc.Block())

    @block.sync
    def _(sp):
        sp.dma_start(xb[:, :, :], batch(x_v, 0)).then_inc(x_in, 16)
        for n, w in enumerate((wq, wk, wv, wo)):
            sp.dma_start(wstage[:, n], w).then_inc(weights_in, 16)
        sp.dma_start(gates_sb[:, :, :], gates).then_inc(gates_in, 16)

        def stack(w, it, u):
            q = it * UNITS + u
            start = is_number(it, 0)
            sp.wait_ge(freed["dve"], w.freed("K", u)[1])
            for op in range(2):
                sp.dma_start(qk_dram[u, op], qk_sb[:, op].bitcast(f32)).then_inc(stack_out, 16)
            if not start:
                sp.wait_ge(scores_ready, GROUPS * PAIRS * (q - 1))
            else:
                sp.wait_ge(stack_made[u], 3)
            sp.wait_ge(stack_out, 32 * (q + 1))
            for op, (dst, parts) in enumerate(((q_st[u], (0, 0, 1)), (k_st[u], (0, 1, 0)))):
                for n, part in enumerate(parts):
                    src = qk_dram[u, op].rearrange("(j d) r t -> r d j t", d=DH)[part]
                    sp.dma_start(dst[n * DH:(n + 1) * DH].bitcast(f32), src).then_inc(stack_in[u], 16)

        def max_rows(w, it, u):
            sp.wait_ge(freed["act"], w.freed("mT", u)[1])
            sp.dma_start(q_st[u][ROW_M:ROW_M + 1].bitcast(f32).rearrange("o j t -> o (j t)"), max_row[u][:, :].bitcast(f32)).then_inc(max_row_in[u], 16)

        def body(it, kind):
            w = Work(it, kind)
            before, this, after = has(kind)
            if after:
                sp.wait_ge(xn_done, it + 1)
                sp.dma_start(xb[:, :, :], batch(x_v, it + 1)).then_inc(x_in, 16)
            if before:
                sp.wait_ge(x1_out, 16 * it)
                sp.dma_start(xres[:, :, :], batch(x_v, it - 1)).then_inc(xres_in, 16)
            if this:
                max_rows(w, it, 0)
                stack(w, it, 1)
            if kind == "first":
                sp.wait_ge(zeros_made, 1)
                for n in range(MOE_TILES // 4):
                    sp.dma_start(xg_dram[n * 4:(n + 1) * 4].rearrange("t p d -> p t d"), zeros[:, :, :]).then_inc(zero_rows_out, 16)
            if before:
                sp.wait_ge(freed["dve"], w.freed("O", 1)[1])
                sp.dma_start(batch(x1_v, it - 1), x1[:, :, :]).then_inc(x1_out, 16)
                sp.wait_ge(xn2_done, it)
                sp.dma_start(batch(xn2_v, it - 1), xn2[:, :, :]).then_inc(xn2_out, 16)
            if after:
                stack(w, it + 1, 0)
            if this:
                max_rows(w, it, 1)

        stack(Work(0, "start"), 0, 0)
        iterations(sp, body)
        sp.wait_ge(x1_out, 16 * (B + 1))
        sp.wait_ge(xn2_out, 16 * (B + 1))
        sp.wait_ge(zero_rows_out, 16 * (MOE_TILES // 4))

    @block.gpsimd
    def _(pool):
        first = Chain(pool, pool_chain)
        first.step(pool.memset(ident[:, :], 0.0))
        first.step(pool.memset(ident16[:, :], 0.0))
        first.step(pool.memset(mask16[:, :], 0.0))
        first.step(pool.memset(minus_half[:, :], -0.5))
        first.step(pool.memset(v_aug[:, :, :, DH:STRIP], 1.0))
        pool.memset(zeros[:, :, :], 0.0).then_inc(zeros_made, 1)
        pool.memset(pool_scratch[:, 0:1], 0.0).then_inc(x1_out, 16)
        pool.memset(pool_scratch[:, 1:2], 0.0).then_inc(xn2_out, 16)
        first.wait()
        for m in (ident, ident16):
            first.step(pool.affine_select(out=m[:, :], in_=m[:, :], compare_op=ALU.not_equal, fill=1.0, base=0,
                                          pattern=[[-1, P]], channel_multiplier=1))
        first.step(pool.affine_select(out=mask16[:, :], in_=mask16[:, :], compare_op=ALU.is_ge, fill=NEG, base=0,
                                      pattern=[[-1, P]], channel_multiplier=1))
        pool.memset(q_st[0][:, :, :].bitcast(f32), 0.0).then_inc(stack_made[0], 1)
        tiny = first.n
        assert tiny == POOL_CONSTS

        ticks = Ticks(pool, pool_ticks, lambda: pool.tensor_tensor(out=pool_scratch[:, 2:3], in0=minus_half[0:1, 0:1],
                                                                   in1=minus_half[0:1, 0:1], op=ALU.add))

        def layer_norm(n, source, target, base):
            chain = Chain(pool, pool_chain, base)
            mv = mean_var[n]
            chain.step(pool.tensor_scalar(out=rstd[n][:, :], in0=mv[:, :, 1], scalar1=EPS, scalar2=None, op0=ALU.add))
            chain.wait()
            chain.step(pool.tensor_tensor(out=rstd[n][:, :], in0=rstd[n][:, :], in1=minus_half[:, :], op=ALU.pow))
            chain.wait()
            ticks.tick()
            for t in range(TB):
                last = pool.tensor_scalar(out=target[:, t, :], in0=source[:, t, :], scalar1=mv[:, t, 0:1],
                                          scalar2=rstd[n][:, t:t + 1], op0=ALU.subtract, op1=ALU.mult)
            return chain, last

        def masks(q, g):
            for p in range(PAIRS):
                pool.wait_ge(exp_done, PAIRS * (GROUPS * q + g) + p + 1)
                ticks.tick()
                v = probs[:, g, p * PAIR:(p + 1) * PAIR]
                for first_col, step, number in [[(0, BANK, 2)], [(0, BANK, 2), (3 * P, BANK, 2)], [(0, 2 * P, 4)]][(p >= 2) + (p >= 4)]:
                    diagonal = v.rearrange("p (k n) -> p k n", n=step)[:, :, first_col:first_col + P]
                    last = pool.affine_select(out=diagonal, in_=diagonal, compare_op=ALU.is_ge, fill=0.0, base=0,
                                              pattern=[[0, number], [1, P]], channel_multiplier=-1)
                last.then_inc(mask_done, 1)

        LN_STEPS = 2

        def norm_x(it, steps):
            pool.wait_ge(moments_done[0], it + 1)
            ticks.tick()
            _, last = layer_norm(0, xb, xn, steps)
            last.then_inc(xn_done, 1)

        norm_x(0, tiny)
        pool.memset(q_st[1][:, :, :].bitcast(f32), 0.0).then_inc(stack_made[1], 1)
        pool.memset(k_st[1][0:ROW_M].bitcast(f32), 0.0).then_inc(stack_made[1], 1)

        def body(it, kind):
            w = Work(it, kind)
            base = tiny + LN_STEPS if kind == "first" else tiny + 2 * LN_STEPS + (it - 1) * 2 * LN_STEPS
            LN_TICKS, MASK_TICKS = 2, GROUPS * PAIRS
            in_full = 2 * LN_TICKS + UNITS * MASK_TICKS
            ticks.start(LN_TICKS if kind == "first" else (it - 1) * in_full + (2 * LN_TICKS + MASK_TICKS))
            if kind == "last":
                base = base - LN_STEPS
                ticks.base -= LN_TICKS
            before, this, after = has(kind)
            if before:
                for g in range(GROUPS):
                    masks(2 * it - 1, g)
            if after:
                pool.wait_ge(work_ready, w.base("ready"))
                norm_x(it + 1, base)
                base = base + LN_STEPS
            if this:
                masks(2 * it, 0)
            if before:
                pool.wait_ge(moments_done[1], it)
                pool.wait_ge(xn2_out, 16 * it)
                pool.wait_ge(work_ready, w.base("ready"))
                ticks.tick()
                _, last = layer_norm(1, x1, xn2, base)
                last.then_inc(xn2_done, 1)
            if this:
                masks(2 * it, 1)

        iterations(pool, body)

    @block.scalar
    def _(act):
        def step(w, it, kind, which):
            if kind in EMPTIED_BY and kind not in ("max", "oT", "O", "L"):
                act.wait_ge(work_ready, w.upto("ready", kind, which))
                bank = ps_w[:, w.bank(kind, which), :]
            if kind == "xT":
                act.activation(xT_hi[:, which, :], bank, ACT.Copy).then_inc(hi_done, 1)
            elif kind == "Q":
                q = (it + 1) * UNITS if which == 0 and w.kind != "start" else it * UNITS + which
                if not is_number(q, 0):
                    act.wait_ge(stack_out, 32 * q)
                act.activation(qk_sb[:, 0, 0, :], bank, ACT.Copy, scale=SCALE).then_inc(hi_done, 1)
            elif kind == "K":
                act.activation(qk_sb[:, 1, 0, :], bank, ACT.Copy).then_inc(hi_done, 1)
            elif kind == "oTT":
                act.activation(oT_hi[:, which, :], bank, ACT.Copy).then_inc(hi_done, 1)
            elif kind == "mT":
                if w.kind != "first":
                    act.wait_ge(max_row_in[which], 16 * it)
                act.activation(max_row[which][:, :], bank[0:HU, :], ACT.Copy).then_inc(freed["act"], 1)
            elif kind == "V":
                act.activation(v_aug[:, 2 * which:2 * which + 2, :, 0:DH], bank.rearrange("p (t h d) -> p t h d", t=2, h=H), ACT.Copy)\
                   .then_inc(freed["act"], 1)
            elif kind == "x2T":
                act.activation(x2T[:, which, :], bank, ACT.Copy).then_inc(freed["act"], 1)
            elif kind == "S":
                u, g, p = which
                G = GROUPS * (2 * it - u) + g
                if p == 0 and not is_number(G, 0, 1):
                    act.wait_ge(pv_done, G - 1)
                act.wait_ge(scores_ready, PAIRS * G + p + 1)
                act.activation(probs[:, g, p * PAIR:(p + 1) * PAIR], ps_s[:, (PAIRS * g + p) % 2, :], ACT.Exp).then_inc(exp_done, 1)
            elif kind == "PV":
                G = group_of(it, which)
                act.wait_ge(pv_done, G + 1)
                if w.kind != "first":
                    act.wait_ge(work_ready, w.base("ready") if which in (1, 2) else w.upto("ready", "oT", {3: 1, 0: 2}[which]))
                act.activation(o_raw[:, which % 2, :], ps_o[:, :], ACT.Copy).then_inc(o_copied, 1)

        def body(it, kind):
            w = Work(it, kind)
            for name, which in w.steps:
                step(w, it, name, which)

        body(0, "start")
        iterations(act, body)

    @block.vector
    def _(dve):
        at_start = Chain(dve, dve_chain)
        dve.wait_ge(weights_in, 64)
        at_start.step(dve.tensor_copy(w_hi[:, :, :, :], wstage[:, :, :, :]))
        at_start.wait()
        dve.tensor_tensor(out=w_lo[:, :, :, :], in0=wstage[:, :, :, :], in1=w_hi[:, :, :, :].bitcast(f32), op=ALU.subtract)\
           .then_inc(weights_split, 1)
        at_start = at_start.n

        ticks = Ticks(dve, dve_ticks, lambda: dve.memset(dve_scratch[:, :], 0.0))

        def moments(n, source, base):
            chain = Chain(dve, dve_chain, base)
            for t in range(TB):
                chain.step(dve.bn_stats(out=stats[n][:, t, :], in_=source[:, t, :]))
            chain.wait()
            ticks.tick()
            for t in range(TB):
                last = dve.bn_aggr(out=mean_var[n][:, t, :], in_=stats[n][:, t, :])
            last.then_inc(moments_done[n], 1)
            return chain.n

        def lower(w, kind, which, hi_part, lo_part, scale=1.0):
            dve.wait_ge(hi_done, w.upto("hi", kind, which))
            dve.scalar_tensor_tensor(out=lo_part, in0=ps_w[:, w.bank(kind, which), :], scalar=scale,
                                     in1=hi_part.bitcast(f32), op0=ALU.mult, op1=ALU.subtract).then_inc(freed["dve"], 1)

        def step(w, it, kind, which):
            if kind in ("max", "oT", "O", "L"):
                dve.wait_ge(work_ready, w.upto("ready", kind, which))
                bank = ps_w[:, w.bank(kind, which), :]
            if kind == "xT":
                lower(w, kind, which, xT_hi[:, which, :], xT_lo[:, which, :])
            elif kind == "Q":
                lower(w, kind, which, qk_sb[:, 0, 0, :], qk_sb[:, 0, 1, :], SCALE)
            elif kind == "K":
                lower(w, kind, which, qk_sb[:, 1, 0, :], qk_sb[:, 1, 1, :])
            elif kind == "oTT":
                lower(w, kind, which, oT_hi[:, which, :], oT_lo[:, which, :])
            elif kind == "max":
                u, g, n = which
                qt, heads = MAX_JOBS[n]
                width, h = (qt + 1) * P, g * GH + heads[0]
                dve.tensor_reduce(out=neg_max[u][:, qt, h:h + len(heads)],
                                  in_=bank[:, 0:len(heads) * width].rearrange("p (h n) -> p h n", h=len(heads)),
                                  axis=AX.X, op=ALU.max, negate=True).then_inc(freed["dve"], 1)
            elif kind == "oT":
                dve.wait_ge(freed["dve"], w.before("dve", kind, which))
                v = bank.rearrange("p (t h c) -> p t h c", t=TB, h=GH)
                chain = Chain(dve, dve_chain, w.before("chain", kind, which) + at_start)
                chain.step(dve.reciprocal(inverse[:, :, :], v[:, :, :, DH]))
                chain.wait()
                head = {0: 0, 1: GH, 2: HU, 3: HU + GH}[which]
                dve.tensor_tensor(out=o_tok[:, :, head * DH:(head + GH) * DH].rearrange("p t (h d) -> p t h d", h=GH), in0=v[:, :, :, 0:DH],
                                  in1=inverse[:, :, :].unsqueeze(3).to_broadcast([P, TB, GH, DH]), op=ALU.mult).then_inc(freed["dve"], 1)
            elif kind == "O":
                if which == 0:
                    dve.wait_ge(xres_in, 16 * it)
                    dve.wait_ge(x1_out, 16 * it)
                    dve.wait_ge(xn2_out, 16 * it)
                dve.tensor_tensor(out=x1[:, 2 * which:2 * which + 2, :], in0=bank.rearrange("p (t d) -> p t d", t=2),
                                  in1=xres[:, 2 * which:2 * which + 2, :], op=ALU.add).then_inc(freed["dve"], 1)
            elif kind in ("moments_x", "moments_x1"):
                ticks.start(w.before("ticks", kind, which))
                base = w.before("chain", kind, which) + at_start
                if kind == "moments_x1":
                    dve.wait_ge(freed["dve"], w.freed("O", 1)[1])
                    moments(1, x1, base)
                else:
                    dve.wait_ge(x_in, 16 if w.kind == "start" else 16 * (it + 2))
                    moments(0, xb, base)
            elif kind == "L":
                dve.tensor_copy(logits_all[:, bass.ds((it - 1) * TB + 2 * which, 2), :],
                                bank[:, 0:2 * LOGITS].rearrange("p (t e) -> p t e", t=2)).then_inc(freed["dve"], 1)

        def body(it, kind):
            w = Work(it, kind)
            for name, which in w.steps:
                step(w, it, name, which)

        start = Work(0, "start")
        step(start, 0, "moments_x", 0)
        dve.memset(k_st[0][0:ROW_M].bitcast(f32), 0.0).then_inc(stack_made[0], 1)
        dve.memset(k_st[0][ROW_M:P].bitcast(f32), 1.0).then_inc(stack_made[0], 1)
        for name, which in start.steps[1:]:
            step(start, 0, name, which)
        dve.memset(k_st[1][ROW_M:P].bitcast(f32), 1.0).then_inc(stack_made[1], 1)
        iterations(dve, body)

    @block.tensor
    def _(pe):
        def bank_for(w, kind, which):
            for e, count in w.needed(kind, which):
                pe.wait_ge(freed[e], count)
            return ps_w[:, w.bank(kind, which), :]

        def transposed(w, kind, k, source):
            out = bank_for(w, kind, k)
            for t in range(TB):
                last = pe.transpose(out[:, t * P:(t + 1) * P], source[:, t, k * P:(k + 1) * P], ident[:, :])
            last.then_inc(work_ready, 1)

        def project_qk(w, kind, u):
            out, n, cols = bank_for(w, kind, u), ("Q", "K").index(kind), slice(u * P, (u + 1) * P)
            for k in range(DK):
                last = exact_product(pe, out, (w_hi[:, n, k, cols], w_lo[:, n, k, cols]), (xT_hi[:, k, :], xT_lo[:, k, :]),
                                     start=k == 0, stop=k == DK - 1)
            last.then_inc(work_ready, 1)

        def project_tokens(w, kind, which, parts, n):
            out = bank_for(w, kind, which)
            for t in (2 * which, 2 * which + 1):
                for k in range(DK):
                    last = exact_product(pe, out[:, (t % 2) * D:(t % 2 + 1) * D], tuple(v[:, k, t * P:(t + 1) * P] for v in parts),
                                         (w_hi[:, n, k, :], w_lo[:, n, k, :]), start=k == 0, stop=k == DK - 1)
            last.then_inc(work_ready, 1)

        def max_job(w, it, u, g, n):
            qt, heads = MAX_JOBS[n]
            width = (qt + 1) * P
            out = bank_for(w, "max", (u, g, n))
            if g == 0 and n == 0:
                pe.wait_ge(stack_in[u], STACK_READS * 16 * (it + 1))
            for i, hh in enumerate(heads):
                h = g * GH + hh
                pe.matmul(out[:, i * width:(i + 1) * width], q_st[u][0:ROWS_QK, h, qt * P:(qt + 1) * P], k_st[u][0:ROWS_QK, h, 0:width],
                          start=True, stop=False)
                last = pe.matmul(out[:, (i + 1) * width - P:(i + 1) * width], ident16[:, :], mask16[:, :], start=False, stop=True)
            last.then_inc(work_ready, 1)

        def score_pair(it, q, u, g, p):
            n = PAIRS * (GROUPS * q + g) + p
            if g == 0 and p == 0:
                pe.wait_ge(max_row_in[u], 16 * (it + 1 - u))
            if not is_number(n, 0, 1):
                pe.wait_ge(exp_done, n - 1)
            for hh in range(GH):
                for kt in range(TB):
                    pair, col, width = block_of(hh, kt)
                    if pair == p:
                        h = g * GH + hh
                        last = pe.matmul(ps_s[:, (PAIRS * g + p) % 2, col:col + width], k_st[u][0:ROWS_ALL, h, kt * P:(kt + 1) * P],
                                         q_st[u][0:ROWS_ALL, h, kt * P:S], start=True, stop=True)
            last.then_inc(scores_ready, 1)

        def p_v(q, u, g):
            G = GROUPS * q + g
            pe.wait_ge(mask_done, PAIRS * (G + 1))
            if not is_number(G, 0):
                pe.wait_ge(o_copied, G)
            for kt in range(TB):
                for hh in range(GH):
                    pair, col, width = block_of(hh, kt)
                    last = pe.matmul(ps_o[hh * STRIP:(hh + 1) * STRIP, kt * P:S], v_aug[:, kt, u * HU + g * GH + hh, :],
                                     probs[:, g, pair * PAIR + col:pair * PAIR + col + width], start=kt == 0, stop=kt == TB - 1)
            last.then_inc(pv_done, 1)

        def max_rows(w, u):
            out = bank_for(w, "mT", u)
            pe.wait_ge(freed["dve"], w.freed("max", (u, GROUPS - 1, len(MAX_JOBS) - 1))[1])
            for t in range(TB):
                last = pe.transpose(out[0:HU, t * P:(t + 1) * P], neg_max[u][:, t, :], ident[:, :])
            last.then_inc(work_ready, 1)

        def step(w, it, kind, which):
            if kind == "xT":
                if which == 0:
                    pe.wait_ge(xn_done, 1 if w.kind == "start" else it + 2)
                transposed(w, kind, which, xn)
            elif kind in ("Q", "K"):
                if kind == "Q" and which == 0:
                    pe.wait_ge(freed["dve"], w.freed("xT", 1)[1])
                project_qk(w, kind, which)
            elif kind == "S":
                u, g, p = which
                if u == 0 and g == 0 and p == 0:
                    pe.wait_ge(freed["act"], w.freed("V", 1)[1])
                score_pair(it, 2 * it - u, u, g, p)
            elif kind == "max":
                max_job(w, it, *which)
            elif kind == "mT":
                max_rows(w, which)
            elif kind == "V":
                project_tokens(w, kind, which, (xT_hi, xT_lo), 2)
            elif kind == "PV":
                q, u, g = {0: (2 * it, 0, 0), 1: (2 * it - 2, 0, 1), 2: (2 * it - 1, 1, 0), 3: (2 * it - 1, 1, 1)}[which]
                p_v(q, u, g)
            elif kind == "oT":
                G = group_of(it, which)
                out = bank_for(w, kind, which)
                pe.wait_ge(o_copied, G + 1)
                for t in range(TB):
                    last = pe.transpose(out[:, t * P:(t + 1) * P], o_raw[:, which % 2, t * P:(t + 1) * P], ident[:, :])
                last.then_inc(work_ready, 1)
            elif kind == "oTT":
                if which == 0:
                    pe.wait_ge(freed["dve"], w.freed("oT", 3)[1])
                transposed(w, kind, which, o_tok)
            elif kind == "O":
                if which == 0:
                    pe.wait_ge(freed["dve"], w.freed("oTT", 1)[1])
                project_tokens(w, kind, which, (oT_hi, oT_lo), 3)
            elif kind == "x2T":
                if which == 0:
                    pe.wait_ge(xn2_done, it)
                transposed(w, kind, which, xn2)
            elif kind == "L":
                if which == 0:
                    pe.wait_ge(freed["act"], w.freed("x2T", 1)[1])
                out = bank_for(w, kind, which)
                for t in (2 * which, 2 * which + 1):
                    for k in range(DK):
                        last = pe.matmul(out[:, (t % 2) * LOGITS:(t % 2 + 1) * LOGITS], x2T[:, k, t * P:(t + 1) * P], gates_sb[:, k, :],
                                         start=k == 0, stop=k == DK - 1)
                last.then_inc(work_ready, 1)

        def body(it, kind):
            w = Work(it, kind)
            for name, which in w.steps:
                step(w, it, name, which)

        pe.wait_ge(pool_chain, POOL_CONSTS)
        pe.wait_ge(weights_split, 1)
        pe.wait_ge(gates_in, 16)
        body(0, "start")
        iterations(pe, body)


FF = 704
FT = (FF + P - 1) // P
FF_LAST = FF - (FT - 1) * P
F = 128
EW = DK * 2 * F + D
MOE_TILES = (2 * B * S + E * (P - 1)) // P
MOE_TILES += -MOE_TILES % 4
TILE_PAIRS = MOE_TILES // 2
X_BANK, UP_BANK, H_BANK, Y_BANK = 0, 2, 4, 6
SLOTS = MOE_TILES * P
HALF = B // 2


def build_routing(nc, ctx, logits_all, slots, tile_expert, weight, gate):
    f32, bf16, i32, u32 = mybir.dt.float32, mybir.dt.bfloat16, mybir.dt.int32, mybir.dt.uint32
    ALU, ACT, AX = mybir.AluOpType, mybir.ActivationFunctionType, mybir.AxisListType

    def sb(name, shape, dt=f32):
        return ctx.enter_context(nc.sbuf_tensor(name, shape, dt))

    def sem(name):
        return ctx.enter_context(nc.semaphore(name))

    iota_e, iota_t = sb("iota_e", [P, E]), sb("iota_t", [P, MOE_TILES])
    before, ones = sb("before", [P, P], bf16), sb("ones", [P, P], bf16)
    top, index = sb("top", [P, NT, 8]), sb("index", [P, NT, 8], u32)
    index_f = sb("index_f", [P, NT, 2])
    args, exps = sb("args", [P, 2, NT]), sb("exps", [P, 2, NT])
    hot = sb("hot", [P, 2, NT, E])
    both = sb("both", [P, NT, E], bf16)
    counts, incl, excl = sb("counts", [P, E, NT]), sb("incl", [P, E, NT]), sb("excl", [P, E, NT])
    one_col = sb("one_col", [P, E * NT])
    total, tiles_i, tiles = sb("total", [P, E]), sb("tiles_i", [P, E], i32), sb("tiles", [P, E])
    tiles_to, tiles_before, base = sb("tiles_to", [P, E]), sb("tiles_before", [P, E]), sb("base", [P, E])
    slot_of, slot_f = sb("slot_of", [P, NT, E]), sb("slot_f", [P, 2, NT])
    passed, expert_f = sb("passed", [P, MOE_TILES, E]), sb("expert_f", [P, MOE_TILES])
    ps_rank = ctx.enter_context(nc.psum_tensor("ps_rank", [P, NT, E], f32))
    ps_count = ctx.enter_context(nc.psum_tensor("ps_count", [P, NT, E], f32))

    consts_done, consts_raw = sem("consts_done"), sem("consts_raw")
    args_ready, exps_ready = sem("args_ready"), sem("exps_ready")
    choices_ready, counts_ready = sem("choices_ready"), sem("counts_ready")
    dve_steps = sem("dve_steps")

    block = ctx.enter_context(nc.Block())

    @block.gpsimd
    def _(pool):
        pool.iota(iota_e[:, :], pattern=[[1, E]], base=0, channel_multiplier=0, allow_small_or_imprecise_dtypes=True).then_inc(consts_done, 1)
        pool.iota(iota_t[:, :], pattern=[[1, MOE_TILES]], base=0, channel_multiplier=0, allow_small_or_imprecise_dtypes=True).then_inc(consts_done, 1)
        pool.memset(one_col[:, :], 1.0).then_inc(consts_done, 1)
        pool.memset(ones[:, :], 1.0).then_inc(consts_done, 1)
        pool.memset(before[:, :], 1.0).then_inc(consts_raw, 1)
        pool.wait_ge(consts_raw, 1)
        pool.affine_select(out=before[:, :], in_=before[:, :], compare_op=ALU.is_gt, fill=0.0, base=0,
                           pattern=[[1, P]], channel_multiplier=-1).then_inc(consts_done, 1)

    @block.scalar
    def _(act):
        act.wait_ge(args_ready, 2)
        act.activation(exps[:, :, :], args[:, :, :], ACT.Exp).then_inc(exps_ready, 1)

    @block.tensor
    def _(pe):
        pe.wait_ge(consts_done, 5)
        pe.wait_ge(choices_ready, 1)
        flat = both[:, :, :].rearrange("p t e -> p (t e)")
        pe.matmul(ps_rank[:, :, :].rearrange("p t e -> p (t e)"), before[:, :], flat, start=True, stop=True)
        pe.matmul(ps_count[:, :, :].rearrange("p t e -> p (t e)"), ones[:, :], flat, start=True, stop=True).then_inc(counts_ready, 1)

    @block.vector
    def _(dve):
        chain = Chain(dve, dve_steps)

        def do(instruction):
            chain.step(instruction)
            chain.wait()

        for t in range(NT):
            chain.step(dve.max(out=top[:, t, :], in_=logits_all[:, t, 0:E]))
        chain.wait()
        dve.tensor_tensor(out=args[:, 0, :], in0=top[:, :, 1], in1=top[:, :, 0], op=ALU.subtract).then_inc(args_ready, 1)
        dve.tensor_scalar(out=args[:, 1, :], in0=logits_all[:, :, E], scalar1=-1.0, scalar2=None, op0=ALU.mult).then_inc(args_ready, 1)
        for t in range(NT):
            chain.step(dve.max_index(out=index[:, t, :], in_max=top[:, t, :], in_values=logits_all[:, t, 0:E]))
        chain.wait()
        do(dve.tensor_copy(index_f[:, :, :], index[:, :, 0:2]))
        dve.wait_ge(consts_done, 5)
        for c in range(2):
            chain.step(dve.tensor_tensor(out=hot[:, c], in0=iota_e[:, :].unsqueeze(1).to_broadcast([P, NT, E]),
                                         in1=index_f[:, :, c].unsqueeze(2).to_broadcast([P, NT, E]), op=ALU.is_equal))
        chain.wait()
        dve.tensor_tensor(out=both[:, :, :], in0=hot[:, 0], in1=hot[:, 1], op=ALU.add).then_inc(choices_ready, 1)
        dve.wait_ge(exps_ready, 1)
        do(dve.tensor_scalar(out=args[:, :, :], in0=exps[:, :, :], scalar1=1.0, scalar2=None, op0=ALU.add))
        do(dve.reciprocal(args[:, :, :], args[:, :, :]))
        dve.tensor_copy(weight[:, 0, :], args[:, 0, :])
        dve.tensor_tensor(out=weight[:, 1, :], in0=exps[:, 0, :], in1=args[:, 0, :], op=ALU.mult)
        dve.tensor_copy(gate[:, :], args[:, 1, :])
        dve.wait_ge(counts_ready, 1)
        do(dve.tensor_copy(counts[:, :, :], ps_count[:, :, :].rearrange("p t e -> p e t")))
        flat = lambda v: v[:, :, :].rearrange("p e t -> p (e t)")
        do(dve.tensor_tensor_scan(flat(incl), one_col[:, :], flat(counts), 0.0, ALU.mult, ALU.add))
        do(dve.tensor_tensor(out=excl[:, :, :], in0=incl[:, :, :], in1=counts[:, :, :], op=ALU.subtract))
        do(dve.tensor_reduce(out=total[:, :], in_=counts[:, :, :], axis=AX.X, op=ALU.add))
        do(dve.tensor_scalar(out=tiles_i[:, :], in0=total[:, :], scalar1=float(P - 1), scalar2=None, op0=ALU.add))
        do(dve.tensor_scalar(out=tiles_i[:, :], in0=tiles_i[:, :], scalar1=P.bit_length() - 1, scalar2=None, op0=ALU.arith_shift_right))
        do(dve.tensor_copy(tiles[:, :], tiles_i[:, :]))
        do(dve.tensor_tensor_scan(tiles_to[:, :], one_col[:, 0:E], tiles[:, :], 0.0, ALU.mult, ALU.add))
        do(dve.tensor_tensor(out=tiles_before[:, :], in0=tiles_to[:, :], in1=tiles[:, :], op=ALU.subtract))
        do(dve.scalar_tensor_tensor(out=base[:, :], in0=tiles_before[:, :], scalar=float(P), in1=excl[:, :, 0], op0=ALU.mult, op1=ALU.subtract))
        do(dve.tensor_tensor(out=excl[:, :, :], in0=excl[:, :, :], in1=base[:, :].unsqueeze(2).to_broadcast([P, E, NT]), op=ALU.add))
        do(dve.tensor_tensor(out=slot_of[:, :, :], in0=ps_rank[:, :, :], in1=excl[:, :, :].rearrange("p e t -> p t e"), op=ALU.add))
        for c in range(2):
            do(dve.tensor_tensor(out=hot[:, c], in0=hot[:, c], in1=slot_of[:, :, :], op=ALU.mult))
            do(dve.tensor_reduce(out=slot_f[:, c, :], in_=hot[:, c], axis=AX.X, op=ALU.add))
        dve.tensor_copy(slots[:, :, :], slot_f[:, :, :])
        do(dve.tensor_tensor(out=passed[:, :, :], in0=iota_t[:, :].unsqueeze(2).to_broadcast([P, MOE_TILES, E]),
                             in1=tiles_to[:, :].unsqueeze(1).to_broadcast([P, MOE_TILES, E]), op=ALU.is_ge))
        do(dve.tensor_reduce(out=expert_f[:, :], in_=passed[:, :, :], axis=AX.X, op=ALU.add))
        dve.tensor_scalar(out=tile_expert[:, :], in0=expert_f[:, :], scalar1=float(E - 1), scalar2=None, op0=ALU.min)


def build_ffn(nc, ctx, slots, tile_expert, weight, gate, x1_dram, xn2_dram, xg_dram, yg_dram, y1_dram,
              shared_up, shared_down, experts, out):
    f32, f32r = mybir.dt.float32, mybir.dt.float32r
    ALU, ACT = mybir.AluOpType, mybir.ActivationFunctionType

    def sb(name, shape, dt=f32):
        return ctx.enter_context(nc.sbuf_tensor(name, shape, dt))

    def sem(name):
        return ctx.enter_context(nc.semaphore(name))

    up_hi, up_lo = sb("up_hi", [P, DK * 2 * FF], f32r), sb("up_lo", [P, DK * 2 * FF], f32r)
    down_hi, down_lo = sb("down_hi", [P, FT * D], f32r), sb("down_lo", [P, FT * D], f32r)
    ex = sb("ex", [P, E, 2, EW], f32r)
    stage = sb("stage", [P, 2, EW])
    ident = sb("ident_f", [P, P])
    xn = sb("xn_f", [P, TB, D])
    x1 = sb("x1_f", [P, TB, D])
    xT_hi, xT_lo = sb("xT_hi_f", [P, DK, S], f32r), sb("xT_lo_f", [P, DK, S], f32r)
    silu, h = sb("silu", [P, 2, S]), sb("h", [P, 2, S])
    h_hi, h_lo = sb("h_hi", [P, FT, S], f32r), sb("h_lo", [P, FT, S], f32r)
    xg, y_e = (v.rearrange("p (two t) d -> p two t d", two=2) for v in (xn[:, :, :], x1[:, :, :]))
    xgT_hi, xgT_lo = xT_hi, xT_lo
    hT_hi, hT_lo = (v[:, 0:2, 0:2 * P] for v in (h_hi, h_lo))
    silu_e, h_e = (v[:, :, 0:2 * F].rearrange("p two (t f) -> p two t f", t=2) for v in (silu, h))
    srow = sb("srow", [P, 2, TB, D])
    back = srow[:, :, :, :].rearrange("p a (t c) d -> p (a t) c d", c=2)
    y1 = sb("y1", [P, TB, D])
    ps = ctx.enter_context(nc.psum_tensor("ps_f", [P, 8, BANK], f32))

    ident_made = sem("ident_made")
    stage_in, w_hi_done, w_split = [sem("stage_in0"), sem("stage_in1")], sem("w_hi_done"), sem("w_split")
    xn_in, x1_in, y1_out = sem("xn_in"), sem("x1_in_f"), sem("y1_out")
    xT_ready, xT_hi_done, xT_split = sem("xT_ready"), sem("xT_hi_done"), sem("xT_split")
    up_ready, silu_done, h_done, h_hi_done, h_split = (sem(n) for n in ("up_ready", "silu_done", "h_done", "h_hi_done", "h_split"))
    down_ready, y_done = sem("down_ready"), sem("y_done")
    rows_in, scattered = [sem("rows_in0"), sem("rows_in1")], [sem("scattered0"), sem("scattered1")]
    moe_in, moe_out = [sem("moe_in0"), sem("moe_in1")], [sem("moe_out0"), sem("moe_out1")]
    m_xT, m_xT_hi, m_xT_split = sem("m_xT"), sem("m_xT_hi"), sem("m_xT_split")
    m_up, m_silu, m_h = sem("m_up"), sem("m_silu"), sem("m_h")
    m_hT, m_hT_hi, m_hT_split = sem("m_hT"), sem("m_hT_hi"), sem("m_hT_split")
    m_down, m_y = sem("m_down"), sem("m_y")
    gathered = [sem(f"gathered{n}") for n in range(4)]
    y1_in, first_added, both_added, result_out = sem("y1_in"), sem("first_added"), sem("both_added"), sem("result_out")

    rows = lambda d: d.rearrange("(b t p) d -> b p t d", p=P, t=TB)
    x1_v, xn2_v, y1_v = rows(x1_dram), rows(xn2_dram), rows(y1_dram)
    out_v = out.rearrange("b (t p) d -> b p t d", p=P)
    xg_pairs, yg_pairs = (v.rearrange("(q t) p d -> q p t d", t=2) for v in (xg_dram, yg_dram))
    SCATTERS = 2 * TB * 16

    def item(view, n):
        return view[n] if isinstance(n, int) else view[bass.ds(n, 1)].squeeze(0)

    halves = lambda n, width: slice(n * width, (n + 1) * width)
    chunks = [(shared_up[:, halves(n, FF)], up_hi[:, halves(n, FF)], up_lo[:, halves(n, FF)]) for n in range(4)]
    chunks += [(shared_down[:, halves(n, EW)], down_hi[:, halves(n, EW)], down_lo[:, halves(n, EW)]) for n in range(FT * D // EW)]
    NC = len(chunks)
    PER = E // HALF
    assert NC % 2 == 0 and PER % 2 == 0

    def two_halves(engine, first_half, between, second_half):
        first_half(0)
        with engine.Fori(1, HALF) as b:
            first_half(b)
        between()
        with engine.Fori(HALF, B) as b:
            second_half(b)

    def pairs_loop(engine, two_pairs):
        two_pairs(0, True)
        with engine.Fori(2, TILE_PAIRS - 3, 2) as q:
            two_pairs(q, True)
        two_pairs(TILE_PAIRS - 2, False)

    def expert(e, part, lo, hi):
        return ex[:, e, part, lo:hi] if isinstance(e, int) else ex[:, bass.ds(e, 1), part, lo:hi].rearrange("p o n -> p (o n)")

    def width(j):
        return P if j < FT - 1 else FF_LAST

    block = ctx.enter_context(nc.Block())

    @block.sync
    def _(sp):
        for n, (src, _, _) in enumerate(chunks):
            if n >= 2:
                sp.wait_ge(w_split, n - 1)
            sp.dma_start(stage[:, n % 2, 0:src.shape[1]], src).then_inc(stage_in[n % 2], 16)

        def load_xn(b):
            sp.dma_start(xn[:, :, :], item(xn2_v, b)).then_inc(xn_in, 16)

        def load_x1(b):
            sp.wait_ge(y1_out, 16 * b)
            sp.dma_start(x1[:, :, :], item(x1_v, b)).then_inc(x1_in, 16)

        def store_y1(b):
            sp.wait_ge(y_done, TB * (b + 1))
            sp.dma_start(item(y1_v, b), x1[:, :, :]).then_inc(y1_out, 16)

        def first_half(b):
            load_x1(b)
            sp.wait_ge(xT_ready, DK * (b + 1))
            load_xn(b + 1)
            for par in range(2):
                sp.wait_ge(scattered[par], SCATTERS * b)
                sp.dma_start(srow[:, par], item(xn2_v, b * 2 + par)).then_inc(rows_in[par], 16)
            for i in range(PER):
                e = b * PER + i
                sp.wait_ge(w_split, e + (NC - 1))
                sp.dma_start(stage[:, i % 2, :], item(experts, e)).then_inc(stage_in[i % 2], 16)
            store_y1(b)

        def load_pair(q, par):
            if not is_number(q, 0, 1):
                sp.wait_ge(m_xT, q - 1)
            sp.dma_start(xg[:, par], item(xg_pairs, q)).then_inc(moe_in[par], 16)

        def two_pairs(q, more):
            if more:
                load_pair(q + 2, 0)
                load_pair(q + 3, 1)

        def tiles():
            for par in range(2):
                sp.wait_ge(scattered[par], SCATTERS * HALF)
                load_pair(par, par)
            pairs_loop(sp, two_pairs)
            sp.wait_ge(m_xT, TILE_PAIRS)
            load_xn(HALF)
            for par in range(2):
                sp.wait_ge(moe_out[par], 8 * TILE_PAIRS)

        def load_y1(b):
            sp.wait_ge(result_out, 16 * b)
            sp.dma_start(y1[:, :, :], item(y1_v, b)).then_inc(y1_in, 16)

        def store_result(b):
            sp.wait_ge(both_added, TB * (b + 1))
            sp.dma_start(item(out_v, b), y1[:, :, :]).then_inc(result_out, 16)

        def second_half(b, last):
            load_x1(b)
            load_y1(b - HALF)
            if not last:
                sp.wait_ge(xT_ready, DK * (b + 1))
                load_xn(b + 1)
            store_y1(b)
            store_result(b - HALF)

        load_xn(0)
        first_half(0)
        with sp.Fori(1, HALF - 1) as b:
            first_half(b)
        load_x1(HALF - 1)
        b = HALF - 1
        for par in range(2):
            sp.wait_ge(scattered[par], SCATTERS * b)
            sp.dma_start(srow[:, par], item(xn2_v, b * 2 + par)).then_inc(rows_in[par], 16)
        for i in range(PER):
            e = b * PER + i
            sp.wait_ge(w_split, e + (NC - 1))
            sp.dma_start(stage[:, i % 2, :], item(experts, e)).then_inc(stage_in[i % 2], 16)
        store_y1(b)
        tiles()
        second_half(HALF, False)
        with sp.Fori(HALF + 1, B - 1) as b:
            second_half(b, False)
        second_half(B - 1, True)
        sp.wait_ge(y1_out, 16 * B)
        with sp.Fori(HALF, B) as b:
            load_y1(b)
            store_result(b)
        sp.wait_ge(result_out, 16 * B)

    @block.gpsimd
    def _(pool):
        pool.memset(ident[:, :], 0.0).then_inc(ident_made, 1)
        pool.wait_ge(ident_made, 1)
        pool.affine_select(out=ident[:, :], in_=ident[:, :], compare_op=ALU.not_equal, fill=1.0, base=0,
                           pattern=[[-1, P]], channel_multiplier=1).then_inc(ident_made, 1)
        xg_rows, yg_rows = (v.rearrange("n p d -> (n p) d") for v in (xg_dram, yg_dram))
        for n in range(NT):
            b, t = divmod(n, TB)
            if t == 0:
                pool.wait_ge(rows_in[b % 2], 16 * (b // 2 + 1))
            for c in range(2):
                pool.indirect_dma_start(out=xg_rows, out_offset=bass.IndirectOffsetOnAxis(ap=slots[:, c, n:n + 1], axis=0),
                                        in_=srow[:, b % 2, t, :], in_offset=None).then_inc(scattered[b % 2], 16)
        for par in range(2):
            pool.wait_ge(scattered[par], SCATTERS * HALF)
            pool.wait_ge(moe_out[par], 8 * TILE_PAIRS)
        for n in range(NT):
            if n >= 4:
                pool.wait_ge(both_added, n - 3)
            for c in range(2):
                pool.indirect_dma_start(out=back[:, n % 4, c, :], out_offset=None, in_=yg_rows,
                                        in_offset=bass.IndirectOffsetOnAxis(ap=slots[:, c, n:n + 1], axis=0)).then_inc(gathered[n % 4], 16)

    @block.scalar
    def _(act):
        for n, (_, hi, _) in enumerate(chunks):
            act.wait_ge(stage_in[n % 2], 16 * (n // 2 + 1))
            act.activation(hi, stage[:, n % 2, 0:hi.shape[1]], ACT.Copy).then_inc(w_hi_done, 1)

        def shared(b):
            for k in range(DK):
                act.wait_ge(xT_ready, b * DK + (k + 1))
                act.activation(xT_hi[:, k, :], ps[:, k, :], ACT.Copy).then_inc(xT_hi_done, 1)
            for j in range(FT + 1):
                n = b * FT + j
                if j < FT:
                    act.wait_ge(up_ready, n + 1)
                    act.wait_ge(h_done, n - 1 if j else n)
                    act.activation(silu[0:width(j), j % 2, :], ps[0:width(j), 2 + 2 * (j % 2), :], ACT.Silu).then_inc(silu_done, 1)
                if j > 0:
                    act.wait_ge(h_done, n)
                    if j == 1:
                        act.wait_ge(down_ready, b * 2)
                    act.activation(h_hi[0:width(j - 1), j - 1, :], h[0:width(j - 1), (j - 1) % 2, :], ACT.Copy).then_inc(h_hi_done, 1)

        def first_half(b):
            shared(b)
            for i in range(PER):
                e = b * PER + i
                act.wait_ge(stage_in[i % 2], 8 * (e - i % 2) + 16 * (NC // 2 + 1))
                act.activation(expert(e, 0, 0, EW), stage[:, i % 2, :], ACT.Copy).then_inc(w_hi_done, 1)

        def split_x(q, par):
            act.wait_ge(m_xT, q + 1)
            act.activation(xgT_hi[:, par, :], ps[:, X_BANK + par, :], ACT.Copy).then_inc(m_xT_hi, 1)

        def two_pairs(q, more):
            for par in range(2):
                act.wait_ge(m_up, q + par + 1)
                if not is_number(q, 0):
                    act.wait_ge(m_h, q + par - 1)
                act.activation(silu_e[:, par], ps[:, UP_BANK + par, :].rearrange("p (t f) -> p t f", t=2)[:, :, 0:F], ACT.Silu)\
                   .then_inc(m_silu, 1)
            for par in range(2):
                if more:
                    split_x(q + 2 + par, par)
                act.wait_ge(m_hT, q + par + 1)
                act.activation(hT_hi[:, par, :], ps[:, H_BANK + par, 0:2 * P], ACT.Copy).then_inc(m_hT_hi, 1)
            for par in range(2):
                act.wait_ge(m_down, q + par + 1)
                if not is_number(q, 0):
                    act.wait_ge(moe_out[par], 8 * q)
                act.activation(y_e[:, par], ps[:, Y_BANK + par, :].rearrange("p (t d) -> p t d", t=2), ACT.Copy).then_inc(m_y, 1)
                act.wait_ge(m_y, q + par + 1)
                act.dma_start(item(yg_pairs, q + par), y_e[:, par]).then_inc(moe_out[par], 16)

        def tiles():
            act.wait_ge(y1_out, 16 * HALF)
            for par in range(2):
                split_x(par, par)
            pairs_loop(act, two_pairs)

        two_halves(act, first_half, tiles, shared)

    @block.vector
    def _(dve):
        for n, (_, hi, lo) in enumerate(chunks):
            dve.wait_ge(w_hi_done, n + 1)
            dve.tensor_tensor(out=lo, in0=stage[:, n % 2, 0:hi.shape[1]], in1=hi.bitcast(f32), op=ALU.subtract).then_inc(w_split, 1)

        def shared(b):
            for k in range(DK):
                dve.wait_ge(xT_hi_done, b * DK + (k + 1))
                dve.tensor_tensor(out=xT_lo[:, k, :], in0=ps[:, k, :], in1=xT_hi[:, k, :].bitcast(f32), op=ALU.subtract).then_inc(xT_split, 1)
            for j in range(FT + 1):
                n = b * FT + j
                if j < FT:
                    dve.wait_ge(silu_done, n + 1)
                    for done in (h_hi_done, h_split):
                        dve.wait_ge(done, n - 1 if j else n)
                    up = ps[:, 3 + 2 * (j % 2), :] if j < FT - 1 else ps[FF_LAST:P, 2 + 2 * (j % 2), :]
                    dve.tensor_tensor(out=h[0:width(j), j % 2, :], in0=up, in1=silu[0:width(j), j % 2, :], op=ALU.mult).then_inc(h_done, 1)
                if j > 0:
                    dve.wait_ge(h_hi_done, n)
                    dve.tensor_tensor(out=h_lo[0:width(j - 1), j - 1, :], in0=h[0:width(j - 1), (j - 1) % 2, :],
                                      in1=h_hi[0:width(j - 1), j - 1, :].bitcast(f32), op=ALU.subtract).then_inc(h_split, 1)
            dve.wait_ge(x1_in, 16 * (b + 1))
            for t in range(TB):
                dve.wait_ge(down_ready, b * 2 + (t // 2 + 1))
                dve.scalar_tensor_tensor(out=x1[:, t, :], in0=ps[:, 6 + t // 2, (t % 2) * D:(t % 2 + 1) * D],
                                         scalar=gate[:, bass.ds(b * TB + t, 1)], in1=x1[:, t, :], op0=ALU.mult, op1=ALU.add).then_inc(y_done, 1)

        def first_half(b):
            shared(b)
            for i in range(PER):
                e = b * PER + i
                dve.wait_ge(w_hi_done, e + (NC + 1))
                dve.tensor_tensor(out=expert(e, 1, 0, EW), in0=stage[:, i % 2, :], in1=expert(e, 0, 0, EW).bitcast(f32),
                                  op=ALU.subtract).then_inc(w_split, 1)

        def split_x(q, par):
            dve.wait_ge(m_xT_hi, q + 1)
            dve.tensor_tensor(out=xgT_lo[:, par, :], in0=ps[:, X_BANK + par, :], in1=xgT_hi[:, par, :].bitcast(f32), op=ALU.subtract)\
               .then_inc(m_xT_split, 1)

        def two_pairs(q, more):
            for par in range(2):
                dve.wait_ge(m_silu, q + par + 1)
                if not is_number(q, 0):
                    dve.wait_ge(m_hT, q + par - 1)
                dve.tensor_tensor(out=h_e[:, par], in0=ps[:, UP_BANK + par, :].rearrange("p (t f) -> p t f", t=2)[:, :, F:2 * F],
                                  in1=silu_e[:, par], op=ALU.mult).then_inc(m_h, 1)
            for par in range(2):
                if more:
                    split_x(q + 2 + par, par)
                dve.wait_ge(m_hT_hi, q + par + 1)
                dve.tensor_tensor(out=hT_lo[:, par, :], in0=ps[:, H_BANK + par, 0:2 * P], in1=hT_hi[:, par, :].bitcast(f32),
                                  op=ALU.subtract).then_inc(m_hT_split, 1)

        def tiles():
            for par in range(2):
                split_x(par, par)
            pairs_loop(dve, two_pairs)

        def combine(b):
            dve.wait_ge(y1_in, 16 * (b + 1))
            for c, done in enumerate((first_added, both_added)):
                for t in range(TB):
                    if c == 0:
                        dve.wait_ge(gathered[t], 32 * (b + 1))
                    elif t == 0:
                        dve.wait_ge(first_added, TB * (b + 1))
                    dve.scalar_tensor_tensor(out=y1[:, t, :], in0=back[:, t, c, :], scalar=weight[:, c, bass.ds(b * TB + t, 1)],
                                             in1=y1[:, t, :], op0=ALU.mult, op1=ALU.add).then_inc(done, 1)

        def second_half(b):
            shared(b)
            combine(b - HALF)

        two_halves(dve, first_half, tiles, second_half)
        with dve.Fori(HALF, B) as b:
            combine(b)

    @block.tensor
    def _(pe):
        def shared(b):
            pe.wait_ge(xn_in, 16 * (b + 1))
            pe.wait_ge(xT_split, b * DK)
            for k in range(DK):
                for t in range(TB):
                    last = pe.transpose(ps[:, k, t * P:(t + 1) * P], xn[:, t, k * P:(k + 1) * P], ident[:, :])
                last.then_inc(xT_ready, 1)
            pe.wait_ge(xT_split, (b + 1) * DK)
            for j in range(FT):
                pe.wait_ge(h_done, b * FT + max(j - 1, 0))
                tiles_ = 2 if j < FT - 1 else 1
                for i in range(tiles_):
                    col = (2 * j + i) * P
                    for k in range(DK):
                        at = slice(k * 2 * FF + col, k * 2 * FF + col + P)
                        last = exact_product(pe, ps[:, 2 + 2 * (j % 2) + i, :], (up_hi[:, at], up_lo[:, at]), (xT_hi[:, k, :], xT_lo[:, k, :]),
                                             start=k == 0, stop=k == DK - 1)
                last.then_inc(up_ready, 1)
            pe.wait_ge(h_split, (b + 1) * FT)
            pe.wait_ge(y_done, b * TB)
            for t in range(TB):
                for j in range(FT):
                    height = P if j < FT - 1 else FF_LAST
                    last = exact_product(pe, ps[:, 6 + t // 2, (t % 2) * D:(t % 2 + 1) * D],
                                         tuple(v[0:height, j, t * P:(t + 1) * P] for v in (h_hi, h_lo)),
                                         tuple(v[0:height, j * D:(j + 1) * D] for v in (down_hi, down_lo)), start=j == 0, stop=j == FT - 1)
                if t % 2:
                    last.then_inc(down_ready, 1)

        def experts_of(q):
            return [pe.value_load(tile_expert[0:1, bass.ds(q * 2 + t, 1)], min_val=0, max_val=E - 1) for t in range(2)]

        def transpose_x(q, par):
            pe.wait_ge(moe_in[par], 8 * (q - par) + 16)
            if not is_number(q, 0, 1):
                pe.wait_ge(m_xT_split, q - 1)
            for n in range(2 * DK):
                t, k = divmod(n, DK)
                last = pe.transpose(ps[:, X_BANK + par, n * P:(n + 1) * P], xg[:, par, t, k * P:(k + 1) * P], ident[:, :])
            last.then_inc(m_xT, 1)

        def gate_and_up(q, par, chosen):
            pe.wait_ge(m_xT_split, q + 1)
            if not is_number(q, 0, 1):
                pe.wait_ge(m_h, q - 1)
            for n in range(2 * DK):
                t, k = divmod(n, DK)
                last = exact_product(pe, ps[:, UP_BANK + par, t * 2 * F:(t + 1) * 2 * F],
                                     tuple(v[:, par, n * P:(n + 1) * P] for v in (xgT_hi, xgT_lo)),
                                     tuple(expert(chosen[t], part, k * 2 * F, (k + 1) * 2 * F) for part in range(2)),
                                     start=k == 0, stop=k == DK - 1)
            last.then_inc(m_up, 1)

        def transpose_h(q, par):
            pe.wait_ge(m_h, q + 1)
            if not is_number(q, 0, 1):
                pe.wait_ge(m_hT_split, q - 1)
            for t in range(2):
                last = pe.transpose(ps[:, H_BANK + par, t * P:(t + 1) * P], h_e[:, par, t, :], ident[:, :])
            last.then_inc(m_hT, 1)

        def project_down(q, par, chosen):
            pe.wait_ge(m_hT_split, q + 1)
            if not is_number(q, 0, 1):
                pe.wait_ge(m_y, q - 1)
            for t in range(2):
                last = exact_product(pe, ps[:, Y_BANK + par, t * D:(t + 1) * D], tuple(v[:, par, t * P:(t + 1) * P] for v in (hT_hi, hT_lo)),
                                     tuple(expert(chosen[t], part, DK * 2 * F, EW) for part in range(2)), start=True, stop=True)
            last.then_inc(m_down, 1)

        def two_pairs(q, more):
            chosen = []
            for par in range(2):
                chosen.append(experts_of(q + par))
                gate_and_up(q + par, par, chosen[par])
            for par in range(2):
                if more:
                    transpose_x(q + 2 + par, par)
                transpose_h(q + par, par)
            for par in range(2):
                project_down(q + par, par, chosen[par])

        def tiles():
            pe.wait_ge(w_split, NC + E)
            pe.wait_ge(xT_split, HALF * DK)
            pe.wait_ge(h_done, HALF * FT)
            pe.wait_ge(y_done, HALF * TB)
            for par in range(2):
                transpose_x(par, par)
            pairs_loop(pe, two_pairs)
            pe.wait_ge(m_xT_split, TILE_PAIRS)
            pe.wait_ge(m_h, TILE_PAIRS)
            pe.wait_ge(m_hT_split, TILE_PAIRS)
            pe.wait_ge(m_y, TILE_PAIRS)

        pe.wait_ge(ident_made, 2)
        pe.wait_ge(w_split, NC)
        two_halves(pe, shared, tiles, shared)


def block_program(nc, x, wq, wk, wv, wo, gates, shared_up, shared_down, experts, out):
    f32, i32 = mybir.dt.float32, mybir.dt.int32
    dram = lambda name, shape: nc.dram_tensor(name, shape, f32).ap()
    x1_dram, xn2_dram, y1_dram = (dram(n, [B * S, D]) for n in ("x1_dram", "xn2_dram", "y1_dram"))
    qk_dram = dram("qk_dram", [UNITS, 2, P, 2, S])
    xg_dram, yg_dram = (dram(n, [MOE_TILES, P, D]) for n in ("xg_dram", "yg_dram"))
    with ExitStack() as whole:
        sb = lambda name, shape, dt: whole.enter_context(nc.sbuf_tensor(name, shape, dt))
        logits_all = sb("logits_all", [P, NT, LOGITS], f32)
        slots, tile_expert = sb("slots", [P, 2, NT], i32), sb("tile_expert", [P, MOE_TILES], i32)
        weight, gate = sb("weight", [P, 2, NT], f32), sb("gate", [P, NT], f32)
        with ExitStack() as ctx:
            build_attention(nc, ctx, x, wq, wk, wv, wo, gates, logits_all, qk_dram, x1_dram, xn2_dram, xg_dram)
        with ExitStack() as ctx:
            build_routing(nc, ctx, logits_all, slots, tile_expert, weight, gate)
        with ExitStack() as ctx:
            build_ffn(nc, ctx, slots, tile_expert, weight, gate, x1_dram, xn2_dram, xg_dram, yg_dram, y1_dram,
                      shared_up, shared_down, experts, out)


def kernel(L0_attn_x, L0_attn_W_Q, L0_attn_W_K, L0_attn_W_V, L0_attn_W_O, L0_ffn_gate_w, L0_ffn_w_gate_up, L0_ffn_w_down,
           L0_ffn_shared_w_gate, L0_ffn_shared_w_up, L0_ffn_shared_w_down, L0_ffn_shared_gate_w):
    import numpy as np
    import concourse.bacc as bacc
    from concourse.bass_utils import run_bass_kernel_spmd

    def by_input(w):
        w = np.asarray(w)
        return np.ascontiguousarray(w.T.reshape(-1, P, w.shape[0]).transpose(1, 0, 2))

    gates = by_input(np.concatenate([np.asarray(L0_ffn_gate_w), np.asarray(L0_ffn_shared_gate_w)]))
    tiles = []
    for lo in range(0, FF, P):
        tiles += [np.asarray(L0_ffn_shared_w_gate)[lo:lo + P], np.asarray(L0_ffn_shared_w_up)[lo:lo + P]]
    shared_up = by_input(np.concatenate(tiles)).reshape(P, -1)
    down = np.zeros((FT * P, D), np.float32)
    down[:FF] = np.asarray(L0_ffn_shared_w_down).T
    shared_down = np.ascontiguousarray(down.reshape(FT, P, D).transpose(1, 0, 2)).reshape(P, -1)
    gate_up = np.asarray(L0_ffn_w_gate_up).reshape(E, DK, P, 2 * F).transpose(0, 2, 1, 3).reshape(E, P, -1)
    experts = np.ascontiguousarray(np.concatenate([gate_up, np.asarray(L0_ffn_w_down)], axis=2))

    arrays = {"x": np.asarray(L0_attn_x), "wq": by_input(L0_attn_W_Q), "wk": by_input(L0_attn_W_K), "wv": by_input(L0_attn_W_V),
              "wo": by_input(L0_attn_W_O), "gates": gates, "shared_up": shared_up, "shared_down": shared_down, "experts": experts}
    nc = bacc.Bacc("TRN2", target_bir_lowering=False, num_devices=1)
    args = [nc.dram_tensor(n, a.shape, mybir.dt.from_np(a.dtype), kind="ExternalInput").ap() for n, a in arrays.items()]
    out = nc.dram_tensor("out", (B, S, D), mybir.dt.float32, kind="ExternalOutput").ap()
    block_program(nc, *args, out)
    result = run_bass_kernel_spmd(nc, [arrays], core_ids=[0])
    return result.results[0]["out"]
```

```python
import concourse.bass as bass
from concourse import mybir
from contextlib import ExitStack

P = 128
B, S, D = 8, 512, 256
H, DH = 16, 16
DK = D // P
TB = S // P
NT = B * TB
HU = 8
GH = 4
UNITS = H // HU
GROUPS = HU // GH
STRIP = P // GH
E = 16
LOGITS = E + 1
EPS = 1e-5
NEG = -1.0e30
SCALE = float(DH) ** -0.5

ROW_HH, ROW_HL, ROW_LH = 0, DH, 2 * DH
ROWS_QK = 96
ROW_M = 96
ROWS_ALL = ROW_M + 1

BANK = 512
PAIRS = 5
PAIR = 2 * BANK


def block_of(head, kt):
    width = (TB - kt) * P
    if kt == 0:
        return head // 2, (head % 2) * BANK, width
    if kt == 1:
        return 2 + head // 2, (head % 2) * BANK, width
    if kt == 3:
        return 2 + head // 2, (head % 2) * BANK + 3 * P, width
    return 4, head * 2 * P, width


def max_jobs_of_group():
    return [(3, (h,)) for h in range(GH)] + [(2, (h,)) for h in range(GH)] + [(1, (0, 1)), (1, (2, 3)), (0, (0, 1, 2, 3))]


MAX_JOBS = max_jobs_of_group()
EVEN = [0, 3, 5, 7, 9, 11]
LATE = [0, 0, 0, 0, 5, 11]

WORK_BANKS = 3


def phase_steps(u, with_max, with_scores, split, between):
    steps = []
    for g in range(GROUPS):
        for p in range(PAIRS):
            if with_scores:
                steps.append(("S", (1 - u, g, p)))
            steps += between.get((g, p), [])
            if with_max:
                steps += [("max", (u, g, n)) for n in range(split[g][p], split[g][p + 1])]
    return steps


def steps_of(kind):
    before = kind in ("full", "eighth", "last")
    this = kind in ("first", "full", "eighth")
    after = kind in ("first", "full")
    project = [("xT", 0), ("xT", 1), ("Q", 0), ("K", 0)]
    if kind == "start":
        return [("moments_x", 0)] + project

    def only(condition, *steps):
        return list(steps) if condition else []

    steps = only(before, ("PV", 1))
    steps += phase_steps(0, this, before, (EVEN, EVEN), {(0, 1): only(before, ("oT", 1)), (0, 3): only(this, ("Q", 1), ("K", 1)),
                                                         (1, 3): only(before, ("PV", 2))})
    steps += only(before, ("oT", 2)) + only(this, ("mT", 0)) + only(before, ("PV", 3))
    steps += only(this, ("V", 0)) + only(before, ("oT", 3)) + only(after, ("moments_x", 0))
    steps += phase_steps(1, this, this, (LATE, EVEN), {(0, 1): only(before, ("oTT", 0), ("oTT", 1)) + only(this, ("V", 1)),
                                                       (0, 2): only(before, ("O", 0), ("O", 1), ("moments_x1", 0)),
                                                       (1, 0): only(after, *project[:2]), (1, 2): only(after, *project[2:]),
                                                       (1, 3): only(this, ("PV", 0))})
    steps += only(this, ("oT", 0), ("mT", 1))
    steps += only(before, ("x2T", 0), ("x2T", 1), ("L", 0), ("L", 1))
    return steps


EMPTIED_BY = {"xT": "dve", "Q": "dve", "K": "dve", "max": "dve", "mT": "act", "V": "act", "oT": "dve", "oTT": "dve",
              "O": "dve", "x2T": "act", "L": "dve"}
SPLIT_STEPS = ("xT", "Q", "K", "oTT")


class Work:

    def __init__(self, it, kind):
        self.steps, self.kind = steps_of(kind), kind
        self.banked = [x for x in self.steps if x[0] in EMPTIED_BY]
        self.it = it

    @staticmethod
    def amount(steps, what):
        if what == "ready":
            return sum(k in EMPTIED_BY for k, _ in steps)
        if what == "hi":
            return sum(k in SPLIT_STEPS for k, _ in steps)
        if what == "chain":
            return sum({"moments_x": TB, "moments_x1": TB, "oT": 1}.get(k, 0) for k, _ in steps)
        if what == "ticks":
            return sum(k in ("moments_x", "moments_x1") for k, _ in steps)
        return sum(EMPTIED_BY.get(k) == what for k, _ in steps)

    def base(self, what):
        if self.kind == "start":
            return 0
        base = self.amount(steps_of("start"), what)
        if self.kind == "first":
            return base
        full, eighth = (self.amount(steps_of(k), what) for k in ("full", "eighth"))
        base += self.amount(steps_of("first"), what)
        if self.kind == "last":
            return base + (B - 2) * full + eighth
        return (self.it - 1) * full + base

    def before(self, what, kind, which):
        return self.base(what) + self.amount(self.steps[:self.steps.index((kind, which))], what)

    def upto(self, what, kind, which):
        return self.base(what) + self.amount(self.steps[:self.steps.index((kind, which)) + 1], what)

    def bank(self, kind, which):
        first = {"start": (), "first": ("start",)}.get(self.kind, ("start", "first"))
        return (sum(self.amount(steps_of(k), "ready") for k in first) + self.banked.index((kind, which))) % WORK_BANKS

    def freed(self, kind, which):
        return EMPTIED_BY[kind], self.upto(EMPTIED_BY[kind], kind, which)

    def needed(self, kind, which):
        n = self.banked.index((kind, which)) - WORK_BANKS
        if n >= 0:
            return [self.freed(*self.banked[n])]
        return [] if self.kind == "start" else [(e, self.base(e)) for e in ("act", "dve")]


assert Work.amount(steps_of("full"), "ready") % WORK_BANKS == 0


def is_number(value, *which):
    return isinstance(value, int) and value in which


class Chain:

    def __init__(self, engine, sem, base=0):
        self.engine, self.sem, self.base, self.n = engine, sem, base, 0

    def step(self, instruction):
        instruction.then_inc(self.sem, 1)
        self.n += 1

    def wait(self):
        self.engine.wait_ge(self.sem, self.base + self.n)


class Ticks(Chain):

    def __init__(self, engine, sem, tiny):
        super().__init__(engine, sem)
        self.tiny = tiny

    def start(self, base):
        self.base, self.n = base, 0

    def tick(self):
        self.wait()
        self.step(self.tiny())


def exact_product(pe, out, stationary, moving, start, stop):
    (s_hi, s_lo), (m_hi, m_lo) = stationary, moving
    pe.matmul(out, s_hi, m_hi, start=start, stop=False)
    pe.matmul(out, s_hi, m_lo, start=False, stop=False)
    return pe.matmul(out, s_lo, m_hi, start=False, stop=stop)


def build_attention(nc, ctx, ident, x, wq, wk, wv, wo, gates, logits_all, qk_dram, x1_dram, xn2_dram, xg_dram):
    f32, f32r, bf16 = mybir.dt.float32, mybir.dt.float32r, mybir.dt.bfloat16
    ALU, ACT, AX = mybir.AluOpType, mybir.ActivationFunctionType, mybir.AxisListType

    def sb(name, shape, dt):
        return ctx.enter_context(nc.sbuf_tensor(name, shape, dt))

    def ps(name, shape):
        return ctx.enter_context(nc.psum_tensor(name, shape, f32))

    def sem(name):
        return ctx.enter_context(nc.semaphore(name))

    wstage = sb("wstage", [P, 4, DK, D], f32)
    w_hi = sb("w_hi", [P, 4, DK, D], f32r)
    w_lo = sb("w_lo", [P, 4, DK, D], f32r)
    gates_sb = sb("gates_sb", [P, DK, LOGITS], f32)
    ident16 = sb("ident16", [P, P], bf16)
    mask16 = sb("mask16", [P, P], bf16)
    minus_half = sb("minus_half", [P, TB], f32)
    zeros = sb("zeros", [P, 4, D], f32)
    xb = sb("xb", [P, TB, D], f32)
    xn = sb("xn", [P, TB, D], f32)
    xT_hi = sb("xT_hi", [P, DK, S], f32r)
    xT_lo = sb("xT_lo", [P, DK, S], f32r)
    qk_sb = sb("qk_sb", [P, 2, 2, S], f32r)
    q_st = [sb(f"q_st{u}", [P, HU, S], f32r) for u in range(UNITS)]
    k_st = [sb(f"k_st{u}", [P, HU, S], f32r) for u in range(UNITS)]
    v_aug = sb("v_aug", [P, TB, H, STRIP], f32)
    probs = sb("probs", [P, GROUPS, PAIRS * PAIR], f32)
    neg_max = [sb(f"neg_max{u}", [P, TB, HU], f32) for u in range(UNITS)]
    max_row = [sb(f"max_row{u}", [HU, S], f32r) for u in range(UNITS)]
    o_raw = sb("o_raw", [P, 2, S], f32)
    inverse = sb("inverse", [P, TB, GH], f32)
    o_tok = sb("o_tok", [P, TB, D], f32)
    oT_hi, oT_lo = sb("oT_hi", [P, DK, S], f32r), sb("oT_lo", [P, DK, S], f32r)
    xres = sb("xres", [P, TB, D], f32)
    x1 = sb("x1", [P, TB, D], f32)
    xn2 = sb("xn2", [P, TB, D], f32)
    x2T = sb("x2T", [P, DK, S], f32)
    stats = [sb(f"stats{n}", [P, TB, 6], f32) for n in range(2)]
    mean_var = [sb(f"mean_var{n}", [P, TB, 2], f32) for n in range(2)]
    rstd = [sb(f"rstd{n}", [P, TB], f32) for n in range(2)]
    pool_scratch, dve_scratch = sb("pool_scratch", [1, 3], f32), sb("dve_scratch", [1, 1], f32)

    ps_s = ps("ps_s", [P, 2, PAIR])
    ps_o = ps("ps_o", [P, S])
    ps_w = ps("ps_w", [P, WORK_BANKS, BANK])

    weights_in, gates_in = sem("weights_in"), sem("gates_in")
    stack_made = [sem(f"stack_made{u}") for u in range(UNITS)]
    zeros_made, weights_split = sem("zeros_made"), sem("weights_split")
    zero_rows_out = sem("zero_rows_out")
    x_in, xres_in = sem("x_in"), sem("xres_in")
    moments_done = [sem(f"moments_done{n}") for n in range(2)]
    xn_done, xn2_done = sem("xn_done"), sem("xn2_done")
    work_ready = sem("work_ready")
    freed = {"act": sem("freed_by_act"), "dve": sem("freed_by_dve")}
    hi_done = sem("hi_done")
    stack_out = sem("stack_out")
    stack_in = [sem(f"stack_in{u}") for u in range(UNITS)]
    max_row_in = [sem(f"max_row_in{u}") for u in range(UNITS)]
    scores_ready, exp_done, mask_done = sem("scores_ready"), sem("exp_done"), sem("mask_done")
    pv_done, o_copied = sem("pv_done"), sem("o_copied")
    x1_out, xn2_out = sem("x1_out"), sem("xn2_out")
    dve_chain, pool_chain, dve_ticks, pool_ticks = (sem(n) for n in ("dve_chain", "pool_chain", "dve_ticks", "pool_ticks"))

    x_v = x.rearrange("b (t p) d -> b p t d", p=P)
    x1_v = x1_dram.rearrange("(b t p) d -> b p t d", b=B, p=P)
    xn2_v = xn2_dram.rearrange("(b t p) d -> b p t d", b=B, p=P)
    STACK_READS = 6

    def batch(view, b):
        if isinstance(b, int):
            return view[b]
        return view[bass.ds(b, 1)].rearrange("o p t d -> (o p) t d")

    def iterations(engine, body):
        body(0, "first")
        with engine.Fori(1, B - 1) as it:
            body(it, "full")
        body(B - 1, "eighth")
        body(B, "last")

    def has(kind):
        return kind in ("full", "eighth", "last"), kind != "last", kind in ("first", "full")

    def group_of(it, slot):
        return 4 * it + (slot - 4 if slot else 0)

    LN_STEPS = 2
    POOL_CONSTS = 8

    block = ctx.enter_context(nc.Block())

    @block.sync
    def _(sp):
        sp.dma_start(xb[:, :, :], batch(x_v, 0)).then_inc(x_in, 16)
        for n, w in enumerate((wq, wk, wv, wo)):
            sp.dma_start(wstage[:, n], w).then_inc(weights_in, 16)
        sp.dma_start(gates_sb[:, :, :], gates).then_inc(gates_in, 16)

        def stack_out_of_sbuf(w, u):
            sp.wait_ge(freed["dve"], w.freed("K", u)[1])
            for op in range(2):
                sp.dma_start(qk_dram[u, op], qk_sb[:, op].bitcast(f32)).then_inc(stack_out, 16)

        def stack_back(it, u):
            q = it * UNITS + u
            if not is_number(it, 0):
                sp.wait_ge(scores_ready, GROUPS * PAIRS * (q - 1))
            else:
                sp.wait_ge(stack_made[u], 3)
            sp.wait_ge(stack_out, 32 * (q + 1))
            for op, (dst, parts) in enumerate(((q_st[u], (0, 0, 1)), (k_st[u], (0, 1, 0)))):
                for n, part in enumerate(parts):
                    src = qk_dram[u, op].rearrange("(j d) r t -> r d j t", d=DH)[part]
                    sp.dma_start(dst[n * DH:(n + 1) * DH].bitcast(f32), src).then_inc(stack_in[u], 16)

        def max_rows(w, it, u):
            sp.wait_ge(freed["act"], w.freed("mT", u)[1])
            sp.dma_start(q_st[u][ROW_M:ROW_M + 1].bitcast(f32).rearrange("o j t -> o (j t)"), max_row[u][:, :].bitcast(f32)).then_inc(max_row_in[u], 16)

        def body(it, kind):
            w = Work(it, kind)
            before, this, after = has(kind)
            if after:
                sp.wait_ge(xn_done, it + 1)
                sp.dma_start(xb[:, :, :], batch(x_v, it + 1)).then_inc(x_in, 16)
            if before:
                sp.wait_ge(x1_out, 16 * it)
                sp.dma_start(xres[:, :, :], batch(x_v, it - 1)).then_inc(xres_in, 16)
            if this:
                stack_out_of_sbuf(w, 1)
                max_rows(w, it, 0)
                stack_back(it, 1)
            if kind == "first":
                sp.wait_ge(zeros_made, 1)
                for n in range(MOE_TILES // 4):
                    sp.dma_start(xg_dram[n * 4:(n + 1) * 4].rearrange("t p d -> p t d"), zeros[:, :, :]).then_inc(zero_rows_out, 16)
            if before:
                sp.wait_ge(freed["dve"], w.freed("O", 1)[1])
                sp.dma_start(batch(x1_v, it - 1), x1[:, :, :]).then_inc(x1_out, 16)
                sp.wait_ge(xn2_done, it)
                sp.dma_start(batch(xn2_v, it - 1), xn2[:, :, :]).then_inc(xn2_out, 16)
            if after:
                stack_out_of_sbuf(w, 0)
            if this:
                max_rows(w, it, 1)
            if after:
                stack_back(it + 1, 0)

        stack_out_of_sbuf(Work(0, "start"), 0)
        stack_back(0, 0)
        iterations(sp, body)
        sp.wait_ge(x1_out, 16 * (B + 1))
        sp.wait_ge(xn2_out, 16 * (B + 1))
        sp.wait_ge(zero_rows_out, 16 * (MOE_TILES // 4))

    @block.gpsimd
    def _(pool):
        first = Chain(pool, pool_chain)
        first.step(pool.memset(ident[:, :], 0.0))
        first.step(pool.memset(ident16[:, :], 0.0))
        first.step(pool.memset(mask16[:, :], 0.0))
        first.step(pool.memset(minus_half[:, :], -0.5))
        first.step(pool.memset(v_aug[:, :, :, DH:STRIP], 1.0))
        pool.memset(zeros[:, :, :], 0.0).then_inc(zeros_made, 1)
        pool.memset(pool_scratch[:, 0:1], 0.0).then_inc(x1_out, 16)
        pool.memset(pool_scratch[:, 1:2], 0.0).then_inc(xn2_out, 16)
        first.wait()
        for m in (ident, ident16):
            first.step(pool.affine_select(out=m[:, :], in_=m[:, :], compare_op=ALU.not_equal, fill=1.0, base=0,
                                          pattern=[[-1, P]], channel_multiplier=1))
        first.step(pool.affine_select(out=mask16[:, :], in_=mask16[:, :], compare_op=ALU.is_ge, fill=NEG, base=0,
                                      pattern=[[-1, P]], channel_multiplier=1))
        tiny = first.n
        assert tiny == POOL_CONSTS

        ticks = Ticks(pool, pool_ticks, lambda: pool.tensor_tensor(out=pool_scratch[:, 2:3], in0=minus_half[0:1, 0:1],
                                                                   in1=minus_half[0:1, 0:1], op=ALU.add))

        def layer_norm(n, source, target, base, apply=True):
            chain = Chain(pool, pool_chain, base)
            mv = mean_var[n]
            chain.step(pool.tensor_scalar(out=rstd[n][:, :], in0=mv[:, :, 1], scalar1=EPS, scalar2=None, op0=ALU.add))
            chain.wait()
            chain.step(pool.tensor_tensor(out=rstd[n][:, :], in0=rstd[n][:, :], in1=minus_half[:, :], op=ALU.pow))
            chain.wait()
            ticks.tick()
            if not apply:
                return
            for t in range(TB):
                last = pool.tensor_scalar(out=target[:, t, :], in0=source[:, t, :], scalar1=mv[:, t, 0:1],
                                          scalar2=rstd[n][:, t:t + 1], op0=ALU.subtract, op1=ALU.mult)
            return last

        def masks(q, g):
            for p in range(PAIRS):
                pool.wait_ge(exp_done, PAIRS * (GROUPS * q + g) + p + 1)
                ticks.tick()
                v = probs[:, g, p * PAIR:(p + 1) * PAIR]
                for first_col, step, number in [[(0, BANK, 2)], [(0, BANK, 2), (3 * P, BANK, 2)], [(0, 2 * P, 4)]][(p >= 2) + (p >= 4)]:
                    diagonal = v.rearrange("p (k n) -> p k n", n=step)[:, :, first_col:first_col + P]
                    last = pool.affine_select(out=diagonal, in_=diagonal, compare_op=ALU.is_ge, fill=0.0, base=0,
                                              pattern=[[0, number], [1, P]], channel_multiplier=-1)
                last.then_inc(mask_done, 1)

        def norm_x(it, steps, apply=True):
            pool.wait_ge(moments_done[0], it + 1)
            ticks.tick()
            last = layer_norm(0, xb, xn, steps, apply)
            if apply:
                last.then_inc(xn_done, 1)

        norm_x(0, tiny, apply=False)
        pool.memset(q_st[0][:, :, :].bitcast(f32), 0.0).then_inc(stack_made[0], 1)
        pool.memset(k_st[0][0:ROW_M].bitcast(f32), 0.0).then_inc(stack_made[0], 1)
        pool.memset(q_st[1][:, :, :].bitcast(f32), 0.0).then_inc(stack_made[1], 1)
        pool.memset(k_st[1][0:ROW_M].bitcast(f32), 0.0).then_inc(stack_made[1], 1)

        def body(it, kind):
            w = Work(it, kind)
            base = tiny + LN_STEPS if kind == "first" else tiny + 2 * LN_STEPS + (it - 1) * 2 * LN_STEPS
            LN_TICKS, MASK_TICKS = 2, GROUPS * PAIRS
            in_full = 2 * LN_TICKS + UNITS * MASK_TICKS
            ticks.start(LN_TICKS if kind == "first" else (it - 1) * in_full + (2 * LN_TICKS + MASK_TICKS))
            if kind == "last":
                base = base - LN_STEPS
                ticks.base -= LN_TICKS
            before, this, after = has(kind)
            if before:
                for g in range(GROUPS):
                    masks(2 * it - 1, g)
            if after:
                pool.wait_ge(work_ready, w.base("ready"))
                norm_x(it + 1, base)
                base = base + LN_STEPS
            if this:
                masks(2 * it, 0)
            if before:
                pool.wait_ge(moments_done[1], it)
                pool.wait_ge(xn2_out, 16 * it)
                pool.wait_ge(work_ready, w.base("ready"))
                ticks.tick()
                last = layer_norm(1, x1, xn2, base, apply=kind != "last")
                if kind != "last":
                    last.then_inc(xn2_done, 1)
            if this:
                masks(2 * it, 1)

        iterations(pool, body)

    @block.scalar
    def _(act):
        def step(w, it, kind, which):
            if kind in EMPTIED_BY and kind not in ("max", "oT", "O", "L"):
                act.wait_ge(work_ready, w.upto("ready", kind, which))
                bank = ps_w[:, w.bank(kind, which), :]
            if kind == "xT":
                act.activation(xT_hi[:, which, :], bank, ACT.Copy).then_inc(hi_done, 1)
            elif kind == "Q":
                q = (it + 1) * UNITS if which == 0 and w.kind != "start" else it * UNITS + which
                if not is_number(q, 0):
                    act.wait_ge(stack_out, 32 * q)
                act.activation(qk_sb[:, 0, 0, :], bank, ACT.Copy, scale=SCALE).then_inc(hi_done, 1)
            elif kind == "K":
                act.activation(qk_sb[:, 1, 0, :], bank, ACT.Copy).then_inc(hi_done, 1)
            elif kind == "oTT":
                act.activation(oT_hi[:, which, :], bank, ACT.Copy).then_inc(hi_done, 1)
            elif kind == "mT":
                if w.kind != "first":
                    act.wait_ge(max_row_in[which], 16 * it)
                act.activation(max_row[which][:, :], bank[0:HU, :], ACT.Copy).then_inc(freed["act"], 1)
            elif kind == "V":
                act.activation(v_aug[:, 2 * which:2 * which + 2, :, 0:DH], bank.rearrange("p (t h d) -> p t h d", t=2, h=H), ACT.Copy)\
                   .then_inc(freed["act"], 1)
            elif kind == "x2T":
                act.activation(x2T[:, which, :], bank, ACT.Copy).then_inc(freed["act"], 1)
            elif kind == "S":
                u, g, p = which
                G = GROUPS * (2 * it - u) + g
                if p == 0 and not is_number(G, 0, 1):
                    act.wait_ge(pv_done, G - 1)
                act.wait_ge(scores_ready, PAIRS * G + p + 1)
                act.activation(probs[:, g, p * PAIR:(p + 1) * PAIR], ps_s[:, (PAIRS * g + p) % 2, :], ACT.Exp).then_inc(exp_done, 1)
            elif kind == "PV":
                G = group_of(it, which)
                act.wait_ge(pv_done, G + 1)
                if w.kind != "first":
                    act.wait_ge(work_ready, w.base("ready") if which in (1, 2) else w.upto("ready", "oT", {3: 1, 0: 2}[which]))
                act.activation(o_raw[:, which % 2, :], ps_o[:, :], ACT.Copy).then_inc(o_copied, 1)

        def body(it, kind):
            w = Work(it, kind)
            for name, which in w.steps:
                step(w, it, name, which)

        body(0, "start")
        iterations(act, body)

    @block.vector
    def _(dve):
        PARTS_STEPS = 1

        def normalised(n, source, target, rstd_count, done):
            dve.wait_ge(pool_chain, rstd_count)
            for t in range(TB):
                last = dve.tensor_scalar(out=target[:, t, :], in0=source[:, t, :], scalar1=mean_var[n][:, t, 0:1],
                                         scalar2=rstd[n][:, t:t + 1], op0=ALU.subtract, op1=ALU.mult)
            last.then_inc(done, 1)

        ticks = Ticks(dve, dve_ticks, lambda: dve.memset(dve_scratch[:, :], 0.0))

        def moments(n, source, base):
            chain = Chain(dve, dve_chain, base)
            for t in range(TB):
                chain.step(dve.bn_stats(out=stats[n][:, t, :], in_=source[:, t, :]))
            chain.wait()
            ticks.tick()
            for t in range(TB):
                last = dve.bn_aggr(out=mean_var[n][:, t, :], in_=stats[n][:, t, :])
            last.then_inc(moments_done[n], 1)
            return chain.n

        def lower(w, kind, which, hi_part, lo_part, scale=1.0):
            dve.wait_ge(hi_done, w.upto("hi", kind, which))
            dve.scalar_tensor_tensor(out=lo_part, in0=ps_w[:, w.bank(kind, which), :], scalar=scale,
                                     in1=hi_part.bitcast(f32), op0=ALU.mult, op1=ALU.subtract).then_inc(freed["dve"], 1)

        def step(w, it, kind, which):
            if kind in ("max", "oT", "O", "L"):
                dve.wait_ge(work_ready, w.upto("ready", kind, which))
                bank = ps_w[:, w.bank(kind, which), :]
            if kind == "xT":
                lower(w, kind, which, xT_hi[:, which, :], xT_lo[:, which, :])
            elif kind == "Q":
                lower(w, kind, which, qk_sb[:, 0, 0, :], qk_sb[:, 0, 1, :], SCALE)
            elif kind == "K":
                lower(w, kind, which, qk_sb[:, 1, 0, :], qk_sb[:, 1, 1, :])
            elif kind == "oTT":
                lower(w, kind, which, oT_hi[:, which, :], oT_lo[:, which, :])
            elif kind == "max":
                u, g, n = which
                qt, heads = MAX_JOBS[n]
                width, h = (qt + 1) * P, g * GH + heads[0]
                dve.tensor_reduce(out=neg_max[u][:, qt, h:h + len(heads)],
                                  in_=bank[:, 0:len(heads) * width].rearrange("p (h n) -> p h n", h=len(heads)),
                                  axis=AX.X, op=ALU.max, negate=True).then_inc(freed["dve"], 1)
            elif kind == "oT":
                dve.wait_ge(freed["dve"], w.before("dve", kind, which))
                v = bank.rearrange("p (t h c) -> p t h c", t=TB, h=GH)
                chain = Chain(dve, dve_chain, w.before("chain", kind, which) + PARTS_STEPS)
                chain.step(dve.reciprocal(inverse[:, :, :], v[:, :, :, DH]))
                chain.wait()
                head = {0: 0, 1: GH, 2: HU, 3: HU + GH}[which]
                dve.tensor_tensor(out=o_tok[:, :, head * DH:(head + GH) * DH].rearrange("p t (h d) -> p t h d", h=GH), in0=v[:, :, :, 0:DH],
                                  in1=inverse[:, :, :].unsqueeze(3).to_broadcast([P, TB, GH, DH]), op=ALU.mult).then_inc(freed["dve"], 1)
            elif kind == "O":
                if which == 0:
                    dve.wait_ge(xres_in, 16 * it)
                    dve.wait_ge(x1_out, 16 * it)
                    dve.wait_ge(xn2_out, 16 * it)
                dve.tensor_tensor(out=x1[:, 2 * which:2 * which + 2, :], in0=bank.rearrange("p (t d) -> p t d", t=2),
                                  in1=xres[:, 2 * which:2 * which + 2, :], op=ALU.add).then_inc(freed["dve"], 1)
            elif kind in ("moments_x", "moments_x1"):
                ticks.start(w.before("ticks", kind, which))
                base = w.before("chain", kind, which) + (0 if w.kind == "start" else PARTS_STEPS)
                if kind == "moments_x1":
                    dve.wait_ge(freed["dve"], w.freed("O", 1)[1])
                    moments(1, x1, base)
                    if w.kind == "last":
                        normalised(1, x1, xn2, POOL_CONSTS + LN_STEPS * 2 * B, xn2_done)
                else:
                    dve.wait_ge(x_in, 16 if w.kind == "start" else 16 * (it + 2))
                    moments(0, xb, base)
            elif kind == "L":
                dve.tensor_copy(logits_all[:, bass.ds((it - 1) * TB + 2 * which, 2), :],
                                bank[:, 0:2 * LOGITS].rearrange("p (t e) -> p t e", t=2)).then_inc(freed["dve"], 1)

        def body(it, kind):
            w = Work(it, kind)
            for name, which in w.steps:
                step(w, it, name, which)

        start = Work(0, "start")
        step(start, 0, "moments_x", 0)
        dve.wait_ge(weights_in, 64)
        parts = Chain(dve, dve_chain, TB)
        parts.step(dve.tensor_copy(w_hi[:, :, :, :], wstage[:, :, :, :]))
        parts.wait()
        dve.tensor_tensor(out=w_lo[:, :, :, :], in0=wstage[:, :, :, :], in1=w_hi[:, :, :, :].bitcast(f32), op=ALU.subtract)\
           .then_inc(weights_split, 1)
        normalised(0, xb, xn, POOL_CONSTS + LN_STEPS, xn_done)
        for name, which in start.steps[1:]:
            step(start, 0, name, which)
            if (name, which) == ("xT", 1):
                dve.memset(k_st[0][ROW_M:P].bitcast(f32), 1.0).then_inc(stack_made[0], 1)
        dve.memset(k_st[1][ROW_M:P].bitcast(f32), 1.0).then_inc(stack_made[1], 1)
        iterations(dve, body)

    @block.tensor
    def _(pe):
        def bank_for(w, kind, which):
            for e, count in w.needed(kind, which):
                pe.wait_ge(freed[e], count)
            return ps_w[:, w.bank(kind, which), :]

        def transposed(w, kind, k, source):
            out = bank_for(w, kind, k)
            for t in range(TB):
                last = pe.transpose(out[:, t * P:(t + 1) * P], source[:, t, k * P:(k + 1) * P], ident[:, :])
            last.then_inc(work_ready, 1)

        def project_qk(w, kind, u):
            out, n, cols = bank_for(w, kind, u), ("Q", "K").index(kind), slice(u * P, (u + 1) * P)
            for k in range(DK):
                last = exact_product(pe, out, (w_hi[:, n, k, cols], w_lo[:, n, k, cols]), (xT_hi[:, k, :], xT_lo[:, k, :]),
                                     start=k == 0, stop=k == DK - 1)
            last.then_inc(work_ready, 1)

        def project_tokens(w, kind, which, parts, n):
            out = bank_for(w, kind, which)
            for t in (2 * which, 2 * which + 1):
                for k in range(DK):
                    last = exact_product(pe, out[:, (t % 2) * D:(t % 2 + 1) * D], tuple(v[:, k, t * P:(t + 1) * P] for v in parts),
                                         (w_hi[:, n, k, :], w_lo[:, n, k, :]), start=k == 0, stop=k == DK - 1)
            last.then_inc(work_ready, 1)

        def max_job(w, it, u, g, n):
            qt, heads = MAX_JOBS[n]
            width = (qt + 1) * P
            out = bank_for(w, "max", (u, g, n))
            if g == 0 and n == 0:
                pe.wait_ge(stack_in[u], STACK_READS * 16 * (it + 1))
            for i, hh in enumerate(heads):
                h = g * GH + hh
                pe.matmul(out[:, i * width:(i + 1) * width], q_st[u][0:ROWS_QK, h, qt * P:(qt + 1) * P], k_st[u][0:ROWS_QK, h, 0:width],
                          start=i == 0, stop=False)
            blocks = out[:, 0:len(heads) * width].rearrange("p (h n) -> p h n", h=len(heads))[:, :, width - P:width]
            last = pe.matmul(blocks, ident16[:, :], mask16[:, :].unsqueeze(1).to_broadcast([P, len(heads), P]), start=False, stop=True)
            last.then_inc(work_ready, 1)

        def score_pair(it, q, u, g, p):
            n = PAIRS * (GROUPS * q + g) + p
            if g == 0 and p == 0:
                pe.wait_ge(max_row_in[u], 16 * (it + 1 - u))
            if not is_number(n, 0, 1):
                pe.wait_ge(exp_done, n - 1)
            for hh in range(GH):
                for kt in range(TB):
                    pair, col, width = block_of(hh, kt)
                    if pair == p:
                        h = g * GH + hh
                        last = pe.matmul(ps_s[:, (PAIRS * g + p) % 2, col:col + width], k_st[u][0:ROWS_ALL, h, kt * P:(kt + 1) * P],
                                         q_st[u][0:ROWS_ALL, h, kt * P:S], start=True, stop=True)
            last.then_inc(scores_ready, 1)

        def p_v(q, u, g):
            G = GROUPS * q + g
            pe.wait_ge(mask_done, PAIRS * (G + 1))
            if not is_number(G, 0):
                pe.wait_ge(o_copied, G)
            for kt in range(TB):
                for hh in range(GH):
                    pair, col, width = block_of(hh, kt)
                    last = pe.matmul(ps_o[hh * STRIP:(hh + 1) * STRIP, kt * P:S], v_aug[:, kt, u * HU + g * GH + hh, :],
                                     probs[:, g, pair * PAIR + col:pair * PAIR + col + width], start=kt == 0, stop=kt == TB - 1)
            last.then_inc(pv_done, 1)

        def max_rows(w, u):
            out = bank_for(w, "mT", u)
            pe.wait_ge(freed["dve"], w.freed("max", (u, GROUPS - 1, len(MAX_JOBS) - 1))[1])
            for t in range(TB):
                last = pe.transpose(out[0:HU, t * P:(t + 1) * P], neg_max[u][:, t, :], ident[:, :])
            last.then_inc(work_ready, 1)

        def step(w, it, kind, which):
            if kind == "xT":
                if which == 0:
                    pe.wait_ge(xn_done, 1 if w.kind == "start" else it + 2)
                transposed(w, kind, which, xn)
            elif kind in ("Q", "K"):
                if kind == "Q" and which == 0:
                    pe.wait_ge(freed["dve"], w.freed("xT", 1)[1])
                project_qk(w, kind, which)
            elif kind == "S":
                u, g, p = which
                score_pair(it, 2 * it - u, u, g, p)
            elif kind == "max":
                max_job(w, it, *which)
            elif kind == "mT":
                max_rows(w, which)
            elif kind == "V":
                project_tokens(w, kind, which, (xT_hi, xT_lo), 2)
            elif kind == "PV":
                q, u, g = {0: (2 * it, 0, 0), 1: (2 * it - 2, 0, 1), 2: (2 * it - 1, 1, 0), 3: (2 * it - 1, 1, 1)}[which]
                if which == 0:
                    pe.wait_ge(freed["act"], w.freed("V", 1)[1])
                p_v(q, u, g)
            elif kind == "oT":
                G = group_of(it, which)
                out = bank_for(w, kind, which)
                pe.wait_ge(o_copied, G + 1)
                for t in range(TB):
                    last = pe.transpose(out[:, t * P:(t + 1) * P], o_raw[:, which % 2, t * P:(t + 1) * P], ident[:, :])
                last.then_inc(work_ready, 1)
            elif kind == "oTT":
                if which == 0:
                    pe.wait_ge(freed["dve"], w.freed("oT", 3)[1])
                transposed(w, kind, which, o_tok)
            elif kind == "O":
                if which == 0:
                    pe.wait_ge(freed["dve"], w.freed("oTT", 1)[1])
                project_tokens(w, kind, which, (oT_hi, oT_lo), 3)
            elif kind == "x2T":
                if which == 0:
                    pe.wait_ge(xn2_done, it)
                transposed(w, kind, which, xn2)
            elif kind == "L":
                if which == 0:
                    pe.wait_ge(freed["act"], w.freed("x2T", 1)[1])
                out = bank_for(w, kind, which)
                for t in (2 * which, 2 * which + 1):
                    for k in range(DK):
                        last = pe.matmul(out[:, (t % 2) * LOGITS:(t % 2 + 1) * LOGITS], x2T[:, k, t * P:(t + 1) * P], gates_sb[:, k, :],
                                         start=k == 0, stop=k == DK - 1)
                last.then_inc(work_ready, 1)

        def body(it, kind):
            w = Work(it, kind)
            for name, which in w.steps:
                step(w, it, name, which)

        pe.wait_ge(pool_chain, POOL_CONSTS)
        pe.wait_ge(weights_split, 1)
        pe.wait_ge(gates_in, 16)
        body(0, "start")
        iterations(pe, body)


FF = 704
FT = (FF + P - 1) // P
FF_LAST = FF - (FT - 1) * P
F = 128
EW = DK * 2 * F + D
MOE_TILES = (2 * B * S + E * (P - 1)) // P
MOE_TILES += -MOE_TILES % 4
TILE_PAIRS = MOE_TILES // 2
X_BANK, UP_BANK, H_BANK, Y_BANK = 0, 2, 4, 6
SLOTS = MOE_TILES * P
HALF = B // 2


def build_routing(nc, ctx, logits_all, slots, experts_of_four, weight, gate, xn2_dram, xn, shared_up, shared_down, stage, up_parts, down_parts):
    f32, bf16, i32, u32 = mybir.dt.float32, mybir.dt.bfloat16, mybir.dt.int32, mybir.dt.uint32
    ALU, ACT, AX = mybir.AluOpType, mybir.ActivationFunctionType, mybir.AxisListType

    def sb(name, shape, dt=f32):
        return ctx.enter_context(nc.sbuf_tensor(name, shape, dt))

    def sem(name):
        return ctx.enter_context(nc.semaphore(name))

    iota_e, iota_t = sb("iota_e", [P, E]), sb("iota_t", [P, MOE_TILES])
    before, ones = sb("before", [P, P], bf16), sb("ones", [P, P], bf16)
    top, index = sb("top", [P, NT, 8]), sb("index", [P, NT, 8], u32)
    index_f = sb("index_f", [P, NT, 2])
    args, exps = sb("args", [P, 2, NT]), sb("exps", [P, 2, NT])
    hot = sb("hot", [P, 2, NT, E])
    both = sb("both", [P, NT, E], bf16)
    counts, incl, excl = sb("counts", [P, E, NT]), sb("incl", [P, E, NT]), sb("excl", [P, E, NT])
    one_col = sb("one_col", [P, E * NT])
    total, tiles_i, tiles = sb("total", [P, E]), sb("tiles_i", [P, E], i32), sb("tiles", [P, E])
    tiles_to, tiles_before, base = sb("tiles_to", [P, E]), sb("tiles_before", [P, E]), sb("base", [P, E])
    slot_of, slot_f = sb("slot_of", [P, NT, E]), sb("slot_f", [P, 2, NT])
    passed, expert_f = sb("passed", [P, MOE_TILES, E]), sb("expert_f", [P, MOE_TILES])
    ps_rank = ctx.enter_context(nc.psum_tensor("ps_rank", [P, NT, E], f32))
    ps_count = ctx.enter_context(nc.psum_tensor("ps_count", [P, NT, E], f32))

    consts_done, consts_raw = sem("consts_done"), sem("consts_raw")
    args_ready, exps_ready = sem("args_ready"), sem("exps_ready")
    choices_ready, counts_ready = sem("choices_ready"), sem("counts_ready")
    dve_steps, first_in = sem("dve_steps"), sem("first_in")
    stage_in, hi_done, lo_done = [sem("w_stage_in0"), sem("w_stage_in1")], sem("w_hi_made"), sem("w_lo_made")

    chunks = []
    for src, (hi, lo) in ((shared_up, up_parts), (shared_down, down_parts)):
        width = FF if src is shared_up else EW
        for first in range(0, src.shape[1], width):
            cols = slice(first, first + width)
            chunks.append((src[:, cols], hi[:, cols], lo[:, cols]))

    block = ctx.enter_context(nc.Block())

    @block.sync
    def _(sp):
        sp.dma_start(xn[:, :, :], xn2_dram[0:S].rearrange("(t p) d -> p t d", p=P)).then_inc(first_in, 16)
        for n, (src, _, _) in enumerate(chunks):
            if n >= 2:
                sp.wait_ge(lo_done, n - 1)
            sp.dma_start(stage[:, n % 2, 0:src.shape[1]], src).then_inc(stage_in[n % 2], 16)
        sp.wait_ge(first_in, 16)

    @block.gpsimd
    def _(pool):
        pool.iota(iota_e[:, :], pattern=[[1, E]], base=0, channel_multiplier=0, allow_small_or_imprecise_dtypes=True).then_inc(consts_done, 1)
        pool.iota(iota_t[:, :], pattern=[[1, MOE_TILES]], base=0, channel_multiplier=0, allow_small_or_imprecise_dtypes=True).then_inc(consts_done, 1)
        pool.memset(one_col[:, :], 1.0).then_inc(consts_done, 1)
        pool.memset(ones[:, :], 1.0).then_inc(consts_done, 1)
        pool.memset(before[:, :], 1.0).then_inc(consts_raw, 1)
        pool.wait_ge(consts_raw, 1)
        pool.affine_select(out=before[:, :], in_=before[:, :], compare_op=ALU.is_gt, fill=0.0, base=0,
                           pattern=[[1, P]], channel_multiplier=-1).then_inc(consts_done, 1)
        for n, (_, hi, lo) in enumerate(chunks):
            pool.wait_ge(hi_done, n + 1)
            pool.tensor_tensor(out=lo, in0=stage[:, n % 2, 0:hi.shape[1]], in1=hi.bitcast(f32), op=ALU.subtract).then_inc(lo_done, 1)

    @block.scalar
    def _(act):
        for n, (_, hi, _) in enumerate(chunks):
            if n == 2:
                act.wait_ge(args_ready, 2)
                act.activation(exps[:, :, :], args[:, :, :], ACT.Exp).then_inc(exps_ready, 1)
            act.wait_ge(stage_in[n % 2], 16 * (n // 2 + 1))
            act.activation(hi, stage[:, n % 2, 0:hi.shape[1]], ACT.Copy).then_inc(hi_done, 1)

    @block.tensor
    def _(pe):
        pe.wait_ge(consts_done, 5)
        pe.wait_ge(choices_ready, 1)
        flat = both[:, :, :].rearrange("p t e -> p (t e)")
        pe.matmul(ps_rank[:, :, :].rearrange("p t e -> p (t e)"), before[:, :], flat, start=True, stop=True)
        pe.matmul(ps_count[:, :, :].rearrange("p t e -> p (t e)"), ones[:, :], flat, start=True, stop=True).then_inc(counts_ready, 1)

    @block.vector
    def _(dve):
        chain = Chain(dve, dve_steps)

        def do(instruction):
            chain.step(instruction)
            chain.wait()

        for t in range(NT):
            chain.step(dve.max(out=top[:, t, :], in_=logits_all[:, t, 0:E]))
        chain.wait()
        dve.tensor_tensor(out=args[:, 0, :], in0=top[:, :, 1], in1=top[:, :, 0], op=ALU.subtract).then_inc(args_ready, 1)
        dve.tensor_scalar(out=args[:, 1, :], in0=logits_all[:, :, E], scalar1=-1.0, scalar2=None, op0=ALU.mult).then_inc(args_ready, 1)
        for t in range(NT):
            chain.step(dve.max_index(out=index[:, t, :], in_max=top[:, t, :], in_values=logits_all[:, t, 0:E]))
        chain.wait()
        do(dve.tensor_copy(index_f[:, :, :], index[:, :, 0:2]))
        dve.wait_ge(consts_done, 5)
        for c in range(2):
            chain.step(dve.tensor_tensor(out=hot[:, c], in0=iota_e[:, :].unsqueeze(1).to_broadcast([P, NT, E]),
                                         in1=index_f[:, :, c].unsqueeze(2).to_broadcast([P, NT, E]), op=ALU.is_equal))
        chain.wait()
        dve.tensor_tensor(out=both[:, :, :], in0=hot[:, 0], in1=hot[:, 1], op=ALU.add).then_inc(choices_ready, 1)
        dve.wait_ge(exps_ready, 1)
        do(dve.tensor_scalar(out=args[:, :, :], in0=exps[:, :, :], scalar1=1.0, scalar2=None, op0=ALU.add))
        do(dve.reciprocal(args[:, :, :], args[:, :, :]))
        dve.tensor_copy(weight[:, 0, :], args[:, 0, :])
        dve.tensor_tensor(out=weight[:, 1, :], in0=exps[:, 0, :], in1=args[:, 0, :], op=ALU.mult)
        dve.tensor_copy(gate[:, :], args[:, 1, :])
        dve.wait_ge(counts_ready, 1)
        do(dve.tensor_copy(counts[:, :, :], ps_count[:, :, :].rearrange("p t e -> p e t")))
        flat = lambda v: v[:, :, :].rearrange("p e t -> p (e t)")
        do(dve.tensor_tensor_scan(flat(incl), one_col[:, :], flat(counts), 0.0, ALU.mult, ALU.add))
        do(dve.tensor_tensor(out=excl[:, :, :], in0=incl[:, :, :], in1=counts[:, :, :], op=ALU.subtract))
        do(dve.tensor_reduce(out=total[:, :], in_=counts[:, :, :], axis=AX.X, op=ALU.add))
        do(dve.tensor_scalar(out=tiles_i[:, :], in0=total[:, :], scalar1=float(P - 1), scalar2=None, op0=ALU.add))
        do(dve.tensor_scalar(out=tiles_i[:, :], in0=tiles_i[:, :], scalar1=P.bit_length() - 1, scalar2=None, op0=ALU.arith_shift_right))
        do(dve.tensor_copy(tiles[:, :], tiles_i[:, :]))
        do(dve.tensor_tensor_scan(tiles_to[:, :], one_col[:, 0:E], tiles[:, :], 0.0, ALU.mult, ALU.add))
        do(dve.tensor_tensor(out=tiles_before[:, :], in0=tiles_to[:, :], in1=tiles[:, :], op=ALU.subtract))
        do(dve.scalar_tensor_tensor(out=base[:, :], in0=tiles_before[:, :], scalar=float(P), in1=excl[:, :, 0], op0=ALU.mult, op1=ALU.subtract))
        do(dve.tensor_tensor(out=excl[:, :, :], in0=excl[:, :, :], in1=base[:, :].unsqueeze(2).to_broadcast([P, E, NT]), op=ALU.add))
        do(dve.tensor_tensor(out=slot_of[:, :, :], in0=ps_rank[:, :, :], in1=excl[:, :, :].rearrange("p e t -> p t e"), op=ALU.add))
        for c in range(2):
            do(dve.tensor_tensor(out=hot[:, c], in0=hot[:, c], in1=slot_of[:, :, :], op=ALU.mult))
            do(dve.tensor_reduce(out=slot_f[:, c, :], in_=hot[:, c], axis=AX.X, op=ALU.add))
        dve.tensor_copy(slots[:, :, :], slot_f[:, :, :])
        do(dve.tensor_tensor(out=passed[:, :, :], in0=iota_t[:, :].unsqueeze(2).to_broadcast([P, MOE_TILES, E]),
                             in1=tiles_to[:, :].unsqueeze(1).to_broadcast([P, MOE_TILES, E]), op=ALU.is_ge))
        do(dve.tensor_reduce(out=expert_f[:, :], in_=passed[:, :, :], axis=AX.X, op=ALU.add))
        do(dve.tensor_scalar(out=expert_f[:, :], in0=expert_f[:, :], scalar1=float(E - 1), scalar2=None, op0=ALU.min))
        four = expert_f[:, :].rearrange("p (n four) -> p n four", four=4)
        for n in range(1, 4):
            do(dve.scalar_tensor_tensor(out=four[:, :, 0], in0=four[:, :, n], scalar=float(E ** n), in1=four[:, :, 0], op0=ALU.mult, op1=ALU.add))
        dve.tensor_copy(experts_of_four[:, 0:TILE_PAIRS:2], four[:, :, 0])


def build_ffn(nc, ctx, slots, experts_of_four, weight, gate, x1_dram, xn2_dram, xg_dram, yg_dram, y1_dram,
              ident, xn, stage, up_parts, down_parts, experts, out):
    f32, f32r = mybir.dt.float32, mybir.dt.float32r
    ALU, ACT = mybir.AluOpType, mybir.ActivationFunctionType

    def sb(name, shape, dt=f32):
        return ctx.enter_context(nc.sbuf_tensor(name, shape, dt))

    def sem(name):
        return ctx.enter_context(nc.semaphore(name))

    (up_hi, up_lo), (down_hi, down_lo) = up_parts, down_parts
    ex = sb("ex", [P, E, 2, EW], f32r)
    x1 = sb("x1_f", [P, TB, D])
    xT_hi, xT_lo = sb("xT_hi_f", [P, DK, S], f32r), sb("xT_lo_f", [P, DK, S], f32r)
    silu, h = sb("silu", [P, 2, S]), sb("h", [P, 2, S])
    h_hi, h_lo = sb("h_hi", [P, FT, S], f32r), sb("h_lo", [P, FT, S], f32r)
    xg, y_e = (v.rearrange("p (two t) d -> p two t d", two=2) for v in (xn[:, :, :], x1[:, :, :]))
    xgT_hi, xgT_lo = xT_hi, xT_lo
    hT_hi, hT_lo = (v[:, 0:2, 0:2 * P] for v in (h_hi, h_lo))
    silu_e, h_e = (v[:, :, 0:2 * F].rearrange("p two (t f) -> p two t f", t=2) for v in (silu, h))
    srow = sb("srow", [P, 2, TB, D])
    back = srow[:, :, :, :].rearrange("p a (t c) d -> p (a t) c d", c=2)
    y1 = sb("y1", [P, TB, D])
    ps = ctx.enter_context(nc.psum_tensor("ps_f", [P, 8, BANK], f32))

    stage_in, w_hi_done, w_split = [sem("stage_in0"), sem("stage_in1")], sem("w_hi_done"), sem("w_split")
    xn_in, x1_in, x1_left = sem("xn_in"), sem("x1_in_f"), sem("x1_left")
    xT_ready, xT_hi_done, xT_split = sem("xT_ready"), sem("xT_hi_done"), sem("xT_split")
    up_ready, silu_done, h_done, h_hi_done, h_split = (sem(n) for n in ("up_ready", "silu_done", "h_done", "h_hi_done", "h_split"))
    down_ready, y_done = sem("down_ready"), sem("y_done")
    rows_in, scattered = [sem("rows_in0"), sem("rows_in1")], [sem("scattered0"), sem("scattered1")]
    moe_in, moe_out = [sem("moe_in0"), sem("moe_in1")], [sem("moe_out0"), sem("moe_out1")]
    m_xT, m_xT_hi, m_xT_split = sem("m_xT"), sem("m_xT_hi"), sem("m_xT_split")
    m_up, m_silu, m_h = sem("m_up"), sem("m_silu"), sem("m_h")
    m_hT, m_hT_hi, m_hT_split = sem("m_hT"), sem("m_hT_hi"), sem("m_hT_split")
    m_down, m_y = sem("m_down"), sem("m_y")
    gathered = [sem(f"gathered{n}") for n in range(4)]
    y1_in, first_added, both_added, result_out = sem("y1_in"), sem("first_added"), sem("both_added"), sem("result_out")

    rows = lambda d: d.rearrange("(b t p) d -> b p t d", p=P, t=TB)
    x1_v, xn2_v, y1_v = rows(x1_dram), rows(xn2_dram), rows(y1_dram)
    out_v = out.rearrange("b (t p) d -> b p t d", p=P)
    xg_pairs, yg_pairs = (v.rearrange("(q t) p d -> q p t d", t=2) for v in (xg_dram, yg_dram))
    SCATTERS = 2 * TB * 16

    def item(view, n):
        return view[n] if isinstance(n, int) else view[bass.ds(n, 1)].squeeze(0)

    PER = E // HALF
    assert PER % 2 == 0 and PER == TB

    def two_halves(engine, ahead, first_half, between, second_half):
        for start, half in ((0, first_half), (HALF, second_half)):
            if start:
                between()
            ahead(start)
            half(start, True)
            with engine.Fori(start + 1, start + HALF - 1) as b:
                half(b, True)
            half(start + HALF - 1, False)

    def pairs_loop(engine, two_pairs):
        two_pairs(0, True)
        with engine.Fori(2, TILE_PAIRS - 3, 2) as q:
            two_pairs(q, True)
        two_pairs(TILE_PAIRS - 2, False)

    def expert(e, part, lo, hi):
        return ex[:, e, part, lo:hi] if isinstance(e, int) else ex[:, bass.ds(e, 1), part, lo:hi].rearrange("p o n -> p (o n)")

    def width(j):
        return P if j < FT - 1 else FF_LAST

    block = ctx.enter_context(nc.Block())

    @block.sync
    def _(sp):
        def load_xn(b):
            sp.dma_start(xn[:, :, :], item(xn2_v, b)).then_inc(xn_in, 16)

        def load_x1(b):
            sp.wait_ge(x1_left, 16 * b)
            sp.dma_start(x1[:, :, :], item(x1_v, b)).then_inc(x1_in, 16)

        def load_next_xn(b, more):
            if more:
                sp.wait_ge(xT_ready, DK * (b + 1))
                load_xn(b + 1)

        def first_half(b, more):
            for i in range(PER):
                e = b * PER + i
                if i == 2:
                    load_next_xn(b, more)
                    load_x1(b)
                if not is_number(e, 0, 1):
                    sp.wait_ge(w_split, e - 1)
                sp.dma_start(stage[:, i % 2, :], item(experts, e)).then_inc(stage_in[i % 2], 16)
            sp.wait_ge(y_done, TB * (b + 1))
            sp.dma_start(item(y1_v, b), x1[:, :, :]).then_inc(x1_left, 16)

        def load_pair(q, par):
            if not is_number(q, 0, 1):
                sp.wait_ge(m_xT, q - 1)
            sp.dma_start(xg[:, par], item(xg_pairs, q)).then_inc(moe_in[par], 16)

        def two_pairs(q, more):
            if more:
                load_pair(q + 2, 0)
                load_pair(q + 3, 1)

        def tiles():
            for par in range(2):
                sp.wait_ge(scattered[par], SCATTERS * HALF)
                load_pair(par, par)
            pairs_loop(sp, two_pairs)
            sp.wait_ge(m_xT, TILE_PAIRS)
            load_xn(HALF)
            for par in range(2):
                sp.wait_ge(moe_out[par], 8 * TILE_PAIRS)
            load_y1(0)

        def load_y1(b):
            sp.dma_start(y1[:, :, :], item(y1_v, b)).then_inc(y1_in, 16)

        def second_half(b, more):
            load_x1(b)
            load_next_xn(b, more)
            sp.wait_ge(both_added, 2 * TB * (b - HALF) + TB)
            sp.dma_start(item(out_v, b - HALF), y1[:, :, :]).then_inc(result_out, 16)
            if more:
                sp.wait_ge(result_out, 16 * (b - HALF + 1))
                load_y1(b - HALF + 1)
            sp.wait_ge(both_added, 2 * TB * (b - HALF + 1))
            sp.dma_start(item(out_v, b), x1[:, :, :]).then_inc(x1_left, 16)

        two_halves(sp, lambda b: None, first_half, tiles, second_half)
        sp.wait_ge(result_out, 16 * HALF)
        sp.wait_ge(x1_left, 16 * B)

    @block.gpsimd
    def _(pool):
        xg_rows, yg_rows = (v.rearrange("n p d -> (n p) d") for v in (xg_dram, yg_dram))
        for b in range(2):
            pool.dma_start(srow[:, b], xn2_v[b]).then_inc(rows_in[b], 16)
        for n in range(NT):
            b, t = divmod(n, TB)
            if t == 0:
                pool.wait_ge(rows_in[b % 2], 16 * (b // 2 + 1))
            if t == 3 and 1 <= b < B - 1:
                pool.wait_ge(scattered[(b - 1) % 2], SCATTERS * ((b - 1) // 2 + 1))
                pool.dma_start(srow[:, (b - 1) % 2], xn2_v[b + 1]).then_inc(rows_in[(b - 1) % 2], 16)
            for c in range(2):
                pool.indirect_dma_start(out=xg_rows, out_offset=bass.IndirectOffsetOnAxis(ap=slots[:, c, n:n + 1], axis=0),
                                        in_=srow[:, b % 2, t, :], in_offset=None).then_inc(scattered[b % 2], 16)
        for par in range(2):
            pool.wait_ge(scattered[par], SCATTERS * HALF)
            pool.wait_ge(moe_out[par], 8 * TILE_PAIRS)
        for m in range(NT):
            pair, r = divmod(m, 2 * TB)
            n = pair * TB + r if r < TB else (pair + HALF) * TB + r - TB
            if m >= TB:
                pool.wait_ge(both_added, m - TB + 1)
            for c in range(2):
                pool.indirect_dma_start(out=back[:, m % TB, c, :], out_offset=None, in_=yg_rows,
                                        in_offset=bass.IndirectOffsetOnAxis(ap=slots[:, c, n:n + 1], axis=0)).then_inc(gathered[m % TB], 16)

    @block.scalar
    def _(act):
        def split_xT(b):
            for k in range(DK):
                act.wait_ge(xT_ready, b * DK + (k + 1))
                act.activation(xT_hi[:, k, :], ps[:, k, :], ACT.Copy).then_inc(xT_hi_done, 1)

        def shared(b, more, beside=None):
            for j in range(FT + 1):
                n = b * FT + j
                if j < FT:
                    act.wait_ge(up_ready, n + 1)
                    act.wait_ge(h_done, n - 1 if j else n)
                    act.activation(silu[0:width(j), j % 2, :], ps[0:width(j), 2 + 2 * (j % 2), :], ACT.Silu).then_inc(silu_done, 1)
                if j > 0:
                    act.wait_ge(h_done, n)
                    if j == 1:
                        act.wait_ge(down_ready, b * 2)
                    act.activation(h_hi[0:width(j - 1), j - 1, :], h[0:width(j - 1), (j - 1) % 2, :], ACT.Copy).then_inc(h_hi_done, 1)
                if beside and 1 <= j <= PER:
                    beside(j - 1)
            if more:
                split_xT(b + 1)

        def first_half(b, more):
            def split_expert(i):
                e = b * PER + i
                act.wait_ge(stage_in[i % 2], 8 * (e - i % 2) + 16)
                act.activation(expert(e, 0, 0, EW), stage[:, i % 2, :], ACT.Copy).then_inc(w_hi_done, 1)

            shared(b, more, split_expert)

        def split_x(q, par):
            act.wait_ge(m_xT, q + 1)
            act.activation(xgT_hi[:, par, :], ps[:, X_BANK + par, :], ACT.Copy).then_inc(m_xT_hi, 1)

        def two_pairs(q, more):
            for par in range(2):
                act.wait_ge(m_up, q + par + 1)
                if not is_number(q, 0):
                    act.wait_ge(m_h, q + par - 1)
                act.activation(silu_e[:, par], ps[:, UP_BANK + par, :].rearrange("p (t f) -> p t f", t=2)[:, :, 0:F], ACT.Silu)\
                   .then_inc(m_silu, 1)
                if more and par == 0:
                    split_x(q + 2, 0)
            for par in range(2):
                act.wait_ge(m_hT, q + par + 1)
                act.activation(hT_hi[:, par, :], ps[:, H_BANK + par, 0:2 * P], ACT.Copy).then_inc(m_hT_hi, 1)
            if more:
                split_x(q + 3, 1)
            for par in range(2):
                act.wait_ge(m_down, q + par + 1)
                if not is_number(q, 0):
                    act.wait_ge(moe_out[par], 8 * q)
                act.activation(y_e[:, par], ps[:, Y_BANK + par, :].rearrange("p (t d) -> p t d", t=2), ACT.Copy).then_inc(m_y, 1)
                act.wait_ge(m_y, q + par + 1)
                act.dma_start(item(yg_pairs, q + par), y_e[:, par]).then_inc(moe_out[par], 16)

        def tiles():
            act.wait_ge(x1_left, 16 * HALF)
            for par in range(2):
                split_x(par, par)
            pairs_loop(act, two_pairs)

        two_halves(act, split_xT, first_half, tiles, shared)

    @block.vector
    def _(dve):
        def split_xT(b):
            for k in range(DK):
                dve.wait_ge(xT_hi_done, b * DK + (k + 1))
                dve.tensor_tensor(out=xT_lo[:, k, :], in0=ps[:, k, :], in1=xT_hi[:, k, :].bitcast(f32), op=ALU.subtract).then_inc(xT_split, 1)

        def shared(b, more, beside):
            for j in range(FT + 1):
                n = b * FT + j
                if j < FT:
                    dve.wait_ge(silu_done, n + 1)
                    for done in (h_hi_done, h_split):
                        dve.wait_ge(done, n - 1 if j else n)
                    up = ps[:, 3 + 2 * (j % 2), :] if j < FT - 1 else ps[FF_LAST:P, 2 + 2 * (j % 2), :]
                    dve.tensor_tensor(out=h[0:width(j), j % 2, :], in0=up, in1=silu[0:width(j), j % 2, :], op=ALU.mult).then_inc(h_done, 1)
                if j > 0:
                    dve.wait_ge(h_hi_done, n)
                    dve.tensor_tensor(out=h_lo[0:width(j - 1), j - 1, :], in0=h[0:width(j - 1), (j - 1) % 2, :],
                                      in1=h_hi[0:width(j - 1), j - 1, :].bitcast(f32), op=ALU.subtract).then_inc(h_split, 1)
                if 1 <= j <= PER:
                    beside(j - 1)
            if more:
                split_xT(b + 1)
            dve.wait_ge(x1_in, 16 * (b + 1))
            for t in range(TB):
                dve.wait_ge(down_ready, b * 2 + (t // 2 + 1))
                dve.scalar_tensor_tensor(out=x1[:, t, :], in0=ps[:, 6 + t // 2, (t % 2) * D:(t % 2 + 1) * D],
                                         scalar=gate[:, bass.ds(b * TB + t, 1)], in1=x1[:, t, :], op0=ALU.mult, op1=ALU.add).then_inc(y_done, 1)

        def add_rows(c, t, n, buffer, done):
            dve.scalar_tensor_tensor(out=buffer[:, t, :], in0=back[:, t, c, :], scalar=weight[:, c, bass.ds(n, 1)],
                                     in1=buffer[:, t, :], op0=ALU.mult, op1=ALU.add).then_inc(done, 1)

        def add_first(m, t, n, buffer):
            dve.wait_ge(gathered[t], (m - t) * 8 + 32)
            add_rows(0, t, n, buffer, first_added)

        def add_second(m, t, n, buffer):
            dve.wait_ge(first_added, m + 1)
            add_rows(1, t, n, buffer, both_added)

        def first_half(b, more):
            def split_expert(i):
                e = b * PER + i
                dve.wait_ge(w_hi_done, e + 1)
                dve.tensor_tensor(out=expert(e, 1, 0, EW), in0=stage[:, i % 2, :], in1=expert(e, 0, 0, EW).bitcast(f32),
                                  op=ALU.subtract).then_inc(w_split, 1)

            shared(b, more, split_expert)

        def split_x(q, par):
            dve.wait_ge(m_xT_hi, q + 1)
            dve.tensor_tensor(out=xgT_lo[:, par, :], in0=ps[:, X_BANK + par, :], in1=xgT_hi[:, par, :].bitcast(f32), op=ALU.subtract)\
               .then_inc(m_xT_split, 1)

        def two_pairs(q, more):
            for par in range(2):
                dve.wait_ge(m_silu, q + par + 1)
                if not is_number(q, 0):
                    dve.wait_ge(m_hT, q + par - 1)
                dve.tensor_tensor(out=h_e[:, par], in0=ps[:, UP_BANK + par, :].rearrange("p (t f) -> p t f", t=2)[:, :, F:2 * F],
                                  in1=silu_e[:, par], op=ALU.mult).then_inc(m_h, 1)
                if more and par == 0:
                    split_x(q + 2, 0)
            for par in range(2):
                dve.wait_ge(m_hT_hi, q + par + 1)
                dve.tensor_tensor(out=hT_lo[:, par, :], in0=ps[:, H_BANK + par, 0:2 * P], in1=hT_hi[:, par, :].bitcast(f32),
                                  op=ALU.subtract).then_inc(m_hT_split, 1)
            if more:
                split_x(q + 3, 1)

        def tiles():
            for par in range(2):
                split_x(par, par)
            pairs_loop(dve, two_pairs)

        def second_half(b, more):
            old = b - HALF

            def add_old(t):
                if t == 0:
                    dve.wait_ge(y1_in, 16 * (old + 1))
                add_first(old * 2 * TB + t, t, old * TB + t, y1)
                add_second(old * 2 * TB + t, t, old * TB + t, y1)

            shared(b, more, add_old)
            dve.wait_ge(y_done, TB * (b + 1))
            m = (b - HALF) * 2 * TB + TB
            for t in range(TB):
                add_first(m + t, t, b * TB + t, x1)
            for t in range(TB):
                add_second(m + t, t, b * TB + t, x1)

        two_halves(dve, split_xT, first_half, tiles, second_half)

    @block.tensor
    def _(pe):
        def transpose_xn(b):
            if not is_number(b, 0):
                pe.wait_ge(xn_in, 16 * b)
            pe.wait_ge(xT_split, b * DK)
            for k in range(DK):
                for t in range(TB):
                    last = pe.transpose(ps[:, k, t * P:(t + 1) * P], xn[:, t, k * P:(k + 1) * P], ident[:, :])
                last.then_inc(xT_ready, 1)

        def shared(b, more):
            pe.wait_ge(xT_split, (b + 1) * DK)
            for j in range(FT):
                pe.wait_ge(h_done, b * FT + max(j - 1, 0))
                for i in range(2 if j < FT - 1 else 1):
                    col = (2 * j + i) * P
                    for k in range(DK):
                        at = slice(k * 2 * FF + col, k * 2 * FF + col + P)
                        last = exact_product(pe, ps[:, 2 + 2 * (j % 2) + i, :], (up_hi[:, at], up_lo[:, at]), (xT_hi[:, k, :], xT_lo[:, k, :]),
                                             start=k == 0, stop=k == DK - 1)
                last.then_inc(up_ready, 1)
            if more:
                transpose_xn(b + 1)
            pe.wait_ge(y_done, b * TB)
            for j in range(FT):
                pe.wait_ge(h_split, b * FT + j + 1)
                for t in range(TB):
                    last = exact_product(pe, ps[:, 6 + t // 2, (t % 2) * D:(t % 2 + 1) * D],
                                         tuple(v[0:width(j), j, t * P:(t + 1) * P] for v in (h_hi, h_lo)),
                                         tuple(v[0:width(j), j * D:(j + 1) * D] for v in (down_hi, down_lo)),
                                         start=j == 0 and t % 2 == 0, stop=j == FT - 1 and t % 2 == 1)
                    if j == FT - 1 and t % 2:
                        last.then_inc(down_ready, 1)

        def experts_of(q):
            four = pe.value_load(experts_of_four[0:1, bass.ds(q, 1)], min_val=0, max_val=E ** 4 - 1)
            return [[four % E, (four // E) % E], [(four // E ** 2) % E, four // E ** 3]]

        def transpose_x(q, par):
            pe.wait_ge(moe_in[par], 8 * (q - par) + 16)
            if not is_number(q, 0, 1):
                pe.wait_ge(m_xT_split, q - 1)
            for n in range(2 * DK):
                t, k = divmod(n, DK)
                last = pe.transpose(ps[:, X_BANK + par, n * P:(n + 1) * P], xg[:, par, t, k * P:(k + 1) * P], ident[:, :])
            last.then_inc(m_xT, 1)

        def gate_and_up(q, par, chosen):
            pe.wait_ge(m_xT_split, q + 1)
            for n in range(2 * DK):
                t, k = divmod(n, DK)
                last = exact_product(pe, ps[:, UP_BANK + par, t * 2 * F:(t + 1) * 2 * F],
                                     tuple(v[:, par, n * P:(n + 1) * P] for v in (xgT_hi, xgT_lo)),
                                     tuple(expert(chosen[t], part, k * 2 * F, (k + 1) * 2 * F) for part in range(2)),
                                     start=k == 0, stop=k == DK - 1)
            last.then_inc(m_up, 1)

        def transpose_h(q, par):
            pe.wait_ge(m_h, q + 1)
            for t in range(2):
                last = pe.transpose(ps[:, H_BANK + par, t * P:(t + 1) * P], h_e[:, par, t, :], ident[:, :])
            last.then_inc(m_hT, 1)

        def project_down(q, par, chosen):
            pe.wait_ge(m_hT_split, q + 1)
            if not is_number(q, 0, 1):
                pe.wait_ge(m_y, q - 1)
            for t in range(2):
                last = exact_product(pe, ps[:, Y_BANK + par, t * D:(t + 1) * D], tuple(v[:, par, t * P:(t + 1) * P] for v in (hT_hi, hT_lo)),
                                     tuple(expert(chosen[t], part, DK * 2 * F, EW) for part in range(2)), start=True, stop=True)
            last.then_inc(m_down, 1)

        def two_pairs(q, more):
            if more:
                transpose_x(q + 2, 0)
            chosen = experts_of(q)
            for par in range(2):
                gate_and_up(q + par, par, chosen[par])
            transpose_h(q, 0)
            if more:
                transpose_x(q + 3, 1)
            transpose_h(q + 1, 1)
            for par in range(2):
                project_down(q + par, par, chosen[par])

        def tiles():
            pe.wait_ge(xT_split, HALF * DK)
            for par in range(2):
                transpose_x(par, par)
            pe.wait_ge(h_done, HALF * FT)
            pe.wait_ge(y_done, HALF * TB)
            pe.wait_ge(w_split, E)
            pairs_loop(pe, two_pairs)
            pe.wait_ge(m_xT_split, TILE_PAIRS)
            pe.wait_ge(m_h, TILE_PAIRS)
            pe.wait_ge(m_hT_split, TILE_PAIRS)
            pe.wait_ge(m_y, TILE_PAIRS)

        two_halves(pe, transpose_xn, shared, tiles, shared)


def block_program(nc, x, wq, wk, wv, wo, gates, shared_up, shared_down, experts, out):
    f32, i32 = mybir.dt.float32, mybir.dt.int32
    dram = lambda name, shape: nc.dram_tensor(name, shape, f32).ap()
    x1_dram, xn2_dram, y1_dram = (dram(n, [B * S, D]) for n in ("x1_dram", "xn2_dram", "y1_dram"))
    qk_dram = dram("qk_dram", [UNITS, 2, P, 2, S])
    xg_dram, yg_dram = (dram(n, [MOE_TILES, P, D]) for n in ("xg_dram", "yg_dram"))
    with ExitStack() as whole:
        sb = lambda name, shape, dt: whole.enter_context(nc.sbuf_tensor(name, shape, dt))
        logits_all = sb("logits_all", [P, NT, LOGITS], f32)
        slots, experts_of_four = sb("slots", [P, 2, NT], i32), sb("experts_of_four", [P, TILE_PAIRS], i32)
        weight, gate = sb("weight", [P, 2, NT], f32), sb("gate", [P, NT], f32)
        ident = sb("ident", [P, P], f32)
        with ExitStack() as ctx:
            build_attention(nc, ctx, ident, x, wq, wk, wv, wo, gates, logits_all, qk_dram, x1_dram, xn2_dram, xg_dram)
        xn = sb("xn_f", [P, TB, D], f32)
        stage = sb("stage", [P, 2, EW], f32)
        up_parts, down_parts = ([sb(f"{n}_{part}", [P, width], mybir.dt.float32r) for part in ("hi", "lo")]
                                for n, width in (("up", DK * 2 * FF), ("down", FT * D)))
        with ExitStack() as ctx:
            build_routing(nc, ctx, logits_all, slots, experts_of_four, weight, gate, xn2_dram, xn, shared_up, shared_down, stage, up_parts, down_parts)
        with ExitStack() as ctx:
            build_ffn(nc, ctx, slots, experts_of_four, weight, gate, x1_dram, xn2_dram, xg_dram, yg_dram, y1_dram,
                      ident, xn, stage, up_parts, down_parts, experts, out)


def kernel(L0_attn_x, L0_attn_W_Q, L0_attn_W_K, L0_attn_W_V, L0_attn_W_O, L0_ffn_gate_w, L0_ffn_w_gate_up, L0_ffn_w_down,
           L0_ffn_shared_w_gate, L0_ffn_shared_w_up, L0_ffn_shared_w_down, L0_ffn_shared_gate_w):
    import numpy as np
    import concourse.bacc as bacc
    from concourse.bass_utils import run_bass_kernel_spmd

    def by_input(w):
        w = np.asarray(w)
        return np.ascontiguousarray(w.T.reshape(-1, P, w.shape[0]).transpose(1, 0, 2))

    gates = by_input(np.concatenate([np.asarray(L0_ffn_gate_w), np.asarray(L0_ffn_shared_gate_w)]))
    tiles = []
    for lo in range(0, FF, P):
        tiles += [np.asarray(L0_ffn_shared_w_gate)[lo:lo + P], np.asarray(L0_ffn_shared_w_up)[lo:lo + P]]
    shared_up = by_input(np.concatenate(tiles)).reshape(P, -1)
    down = np.zeros((FT * P, D), np.float32)
    down[:FF] = np.asarray(L0_ffn_shared_w_down).T
    shared_down = np.ascontiguousarray(down.reshape(FT, P, D).transpose(1, 0, 2)).reshape(P, -1)
    gate_up = np.asarray(L0_ffn_w_gate_up).reshape(E, DK, P, 2 * F).transpose(0, 2, 1, 3).reshape(E, P, -1)
    experts = np.ascontiguousarray(np.concatenate([gate_up, np.asarray(L0_ffn_w_down)], axis=2))

    arrays = {"x": np.asarray(L0_attn_x), "wq": by_input(L0_attn_W_Q), "wk": by_input(L0_attn_W_K), "wv": by_input(L0_attn_W_V),
              "wo": by_input(L0_attn_W_O), "gates": gates, "shared_up": shared_up, "shared_down": shared_down, "experts": experts}
    nc = bacc.Bacc("TRN2", target_bir_lowering=False, num_devices=1)
    args = [nc.dram_tensor(n, a.shape, mybir.dt.from_np(a.dtype), kind="ExternalInput").ap() for n, a in arrays.items()]
    out = nc.dram_tensor("out", (B, S, D), mybir.dt.float32, kind="ExternalOutput").ap()
    block_program(nc, *args, out)
    result = run_bass_kernel_spmd(nc, [arrays], core_ids=[0])
    return result.results[0]["out"]
```
